# Optimizing a Trainium2 kernel written in Bass

```python
import numpy as np
import jax
import jax.numpy as jnp

def _softmax(x, axis=-1):
    return jax.nn.softmax(x, axis=axis)

def _gelu(x):
    return jax.nn.gelu(x, approximate=True)

def _silu(x):
    return jax.nn.silu(x)

def _sigmoid(x):
    return jax.nn.sigmoid(x)

def _layernorm(x, axis=-1, eps=1e-05):
    m = jnp.mean(x, axis=axis, keepdims=True)
    v = jnp.var(x, axis=axis, keepdims=True)
    return (x - m) / jnp.sqrt(v + eps)

def _scatter_add(tgt, idx, src, axis=0):
    return tgt.at[idx].add(src)

def _segment_sum(src, seg, n):
    return jax.ops.segment_sum(src, seg, n)
kernel_name = 'mk_gnn_preln_d4_gnn_r8_c6f7a5'

def setup_inputs(seed: int=0):
    np.random.seed(seed)
    _w = jnp.asarray

    def _rec_inputs():
        import jax
        import jax.numpy as jnp
        _gk = jax.random.key(seed)
        x = -0.0001006 + 1 * jax.random.normal(jax.random.fold_in(_gk, 1), (6250, 96), jnp.float32)
        src = jax.random.randint(jax.random.fold_in(_gk, 2), (200000,), 0, 6250, jnp.int32)
        dst = jax.random.randint(jax.random.fold_in(_gk, 3), (200000,), 0, 6250, jnp.int32)
        _o = jnp.argsort(dst, stable=True)
        src = src[_o]
        dst = dst[_o]
        edge_attr_32 = 0.000196303 + 1.00016 * jax.random.normal(jax.random.fold_in(_gk, 12), (200000, 32), jnp.float32)
        return (x, src, dst, edge_attr_32)
    x, src, dst, edge_attr_32 = _rec_inputs()

    def _L0_gnn_setup():
        import jax, jax.numpy as jnp
        import numpy as np
        N_NODES = 6250
        N_EDGES = 100000
        D = 96
        N_LAYERS = 3
        key = jax.random.key(seed)
        ks = jax.random.split(key, 8)
        s = 1.0 / np.sqrt(D)
        x = jax.random.normal(ks[0], (N_NODES, D), dtype=jnp.float32)
        edge_index = jax.random.randint(ks[1], (2, N_EDGES), 0, N_NODES, dtype=jnp.int32)
        W_in = jax.random.normal(ks[2], (D, D), dtype=jnp.float32) * s
        b_in = jnp.zeros((D,), dtype=jnp.float32)
        gcn_W = jax.random.normal(ks[3], (N_LAYERS, D, D), dtype=jnp.float32) * s
        gcn_b = jnp.zeros((N_LAYERS, D), dtype=jnp.float32)
        W_out = jax.random.normal(ks[4], (D, D), dtype=jnp.float32) * s
        b_out = jnp.zeros((D,), dtype=jnp.float32)
        return {'x': x, 'edge_index': edge_index, 'W_in': W_in, 'b_in': b_in, 'gcn_W': gcn_W, 'gcn_b': gcn_b, 'W_out': W_out, 'b_out': b_out}
    _L0_gnn_all = _L0_gnn_setup()
    _L0_gnn_in = {k: v for k, v in _L0_gnn_all.items() if k in ('W_in', 'b_in', 'gcn_W', 'gcn_b', 'W_out', 'b_out')}
    del _L0_gnn_all

    def _L1_gnn_setup():
        import jax, jax.numpy as jnp
        import numpy as np
        N = 6250
        E = 100000
        D = 96

        def _gcn_conv(x, W, b, src, dst, norm, n):
            h = x @ W
            msg = h[src] * norm[:, None]
            out = jax.ops.segment_sum(msg, dst, num_segments=n)
            return out + b
        key = jax.random.key(seed)
        ks = jax.random.split(key, 6)
        scale = 1.0 / np.sqrt(D)
        return {'x': jax.random.normal(ks[0], (N, D), jnp.float32), 'edge_index': jax.random.randint(ks[1], (2, E), 0, N, dtype=jnp.int64), 'W1': jax.random.normal(ks[2], (D, D), jnp.float32) * scale, 'b1': jnp.zeros((D,), jnp.float32), 'a1': jnp.full((1,), 0.25, jnp.float32), 'W2': jax.random.normal(ks[3], (D, D), jnp.float32) * scale, 'b2': jnp.zeros((D,), jnp.float32)}
    _L1_gnn_all = _L1_gnn_setup()
    _L1_gnn_in = {k: v for k, v in _L1_gnn_all.items() if k in ('W1', 'b1', 'a1', 'W2', 'b2')}
    del _L1_gnn_all

    def _L2_gnn_setup():
        import jax, jax.numpy as jnp
        import numpy as np
        N, E = (6250, 100000)
        ND, ED = (96, 32)

        def _gelu(x):
            return jax.nn.gelu(x, approximate=False)
        key = jax.random.key(seed)
        ks = jax.random.split(key, 16)
        s = lambda fan_in: 1.0 / np.sqrt(fan_in)
        inp = {'x': jax.random.normal(ks[0], (N, ND), jnp.float32), 'edge_index': jax.random.randint(ks[1], (2, E), 0, N, jnp.int32), 'edge_attr': jax.random.normal(ks[2], (E, ED), jnp.float32), 'mW1': jax.random.uniform(ks[3], (ND + ED, ND), jnp.float32, -s(ND + ED), s(ND + ED)), 'mb1': jnp.zeros((ND,), jnp.float32), 'mW2': jax.random.uniform(ks[4], (ND, ND), jnp.float32, -s(ND), s(ND)), 'mb2': jnp.zeros((ND,), jnp.float32), 'gW1': jax.random.uniform(ks[5], (ND + ED, ND), jnp.float32, -s(ND + ED), s(ND + ED)), 'gb1': jnp.zeros((ND,), jnp.float32), 'gW2': jax.random.uniform(ks[6], (ND, 1), jnp.float32, -s(ND), s(ND)), 'gb2': jnp.zeros((1,), jnp.float32), 'uW1': jax.random.uniform(ks[7], (2 * ND, ND), jnp.float32, -s(2 * ND), s(2 * ND)), 'ub1': jnp.zeros((ND,), jnp.float32), 'uW2': jax.random.uniform(ks[8], (ND, ND), jnp.float32, -s(ND), s(ND)), 'ub2': jnp.zeros((ND,), jnp.float32), 'ln_g': jnp.ones((ND,), jnp.float32), 'ln_b': jnp.zeros((ND,), jnp.float32)}
        return inp
    _L2_gnn_all = _L2_gnn_setup()
    _L2_gnn_in = {k: v for k, v in _L2_gnn_all.items() if k in ('mW1', 'mb1', 'mW2', 'mb2', 'gW1', 'gb1', 'gW2', 'gb2', 'uW1', 'ub1', 'uW2', 'ub2', 'ln_g', 'ln_b')}
    del _L2_gnn_all

    def _L3_gnn_setup():
        import jax, jax.numpy as jnp
        import numpy as np
        N_NODES = 6250
        N_EDGES = 100000
        D_MODEL = 96
        HEADS = 4
        key = jax.random.key(seed)
        ks = jax.random.split(key, 6)
        scale = 1.0 / np.sqrt(D_MODEL)
        return {'embeds': jax.random.normal(ks[0], (N_NODES, D_MODEL), dtype=jnp.float32), 'qW': jax.random.normal(ks[1], (D_MODEL, D_MODEL), dtype=jnp.float32) * scale, 'kW': jax.random.normal(ks[2], (D_MODEL, D_MODEL), dtype=jnp.float32) * scale, 'vW': jax.random.normal(ks[3], (D_MODEL, D_MODEL), dtype=jnp.float32) * scale, 'rows': jax.random.randint(ks[4], (N_EDGES,), 0, N_NODES, dtype=jnp.int32), 'cols': jax.random.randint(ks[5], (N_EDGES,), 0, N_NODES, dtype=jnp.int32)}
    _L3_gnn_all = _L3_gnn_setup()
    _L3_gnn_in = {k: v for k, v in _L3_gnn_all.items() if k in ('qW', 'kW', 'vW')}
    del _L3_gnn_all
    return {'x': x, 'src': src, 'dst': dst, 'edge_attr_32': edge_attr_32, 'L0_gnn_W_in': _L0_gnn_in['W_in'], 'L0_gnn_b_in': _L0_gnn_in['b_in'], 'L0_gnn_gcn_W': _L0_gnn_in['gcn_W'], 'L0_gnn_gcn_b': _L0_gnn_in['gcn_b'], 'L0_gnn_W_out': _L0_gnn_in['W_out'], 'L0_gnn_b_out': _L0_gnn_in['b_out'], 'L1_gnn_W1': _L1_gnn_in['W1'], 'L1_gnn_b1': _L1_gnn_in['b1'], 'L1_gnn_a1': _L1_gnn_in['a1'], 'L1_gnn_W2': _L1_gnn_in['W2'], 'L1_gnn_b2': _L1_gnn_in['b2'], 'L2_gnn_mW1': _L2_gnn_in['mW1'], 'L2_gnn_mb1': _L2_gnn_in['mb1'], 'L2_gnn_mW2': _L2_gnn_in['mW2'], 'L2_gnn_mb2': _L2_gnn_in['mb2'], 'L2_gnn_gW1': _L2_gnn_in['gW1'], 'L2_gnn_gb1': _L2_gnn_in['gb1'], 'L2_gnn_gW2': _L2_gnn_in['gW2'], 'L2_gnn_gb2': _L2_gnn_in['gb2'], 'L2_gnn_uW1': _L2_gnn_in['uW1'], 'L2_gnn_ub1': _L2_gnn_in['ub1'], 'L2_gnn_uW2': _L2_gnn_in['uW2'], 'L2_gnn_ub2': _L2_gnn_in['ub2'], 'L2_gnn_ln_g': _L2_gnn_in['ln_g'], 'L2_gnn_ln_b': _L2_gnn_in['ln_b'], 'L3_gnn_qW': _L3_gnn_in['qW'], 'L3_gnn_kW': _L3_gnn_in['kW'], 'L3_gnn_vW': _L3_gnn_in['vW']}

def reference(x, src, dst, edge_attr_32, L0_gnn_W_in, L0_gnn_b_in, L0_gnn_gcn_W, L0_gnn_gcn_b, L0_gnn_W_out, L0_gnn_b_out, L1_gnn_W1, L1_gnn_b1, L1_gnn_a1, L1_gnn_W2, L1_gnn_b2, L2_gnn_mW1, L2_gnn_mb1, L2_gnn_mW2, L2_gnn_mb2, L2_gnn_gW1, L2_gnn_gb1, L2_gnn_gW2, L2_gnn_gb2, L2_gnn_uW1, L2_gnn_ub1, L2_gnn_uW2, L2_gnn_ub2, L2_gnn_ln_g, L2_gnn_ln_b, L3_gnn_qW, L3_gnn_kW, L3_gnn_vW):
    import jax
    import jax.numpy as jnp

    def _L0_gnn_ref(x, edge_index, W_in, b_in, gcn_W, gcn_b, W_out, b_out):
        import jax, jax.numpy as jnp
        import numpy as np
        N_NODES = 6250
        N_EDGES = 100000
        D = 96
        N_LAYERS = 3
        N = x.shape[0]
        loop = jnp.arange(N, dtype=edge_index.dtype)
        row = jnp.concatenate([edge_index[0], loop])
        col = jnp.concatenate([edge_index[1], loop])
        deg = jax.ops.segment_sum(jnp.ones_like(col, dtype=x.dtype), col, num_segments=N)
        dinv = jnp.where(deg > 0, jax.lax.rsqrt(deg), 0.0)
        norm = (dinv[row] * dinv[col])[:, None]

        def gcn_conv(h, W, b):
            hw = h @ W.T
            msg = norm * hw[row]
            out = jax.ops.segment_sum(msg, col, num_segments=N)
            return out + b
        h = jax.nn.relu(x @ W_in.T + b_in)
        for l in range(N_LAYERS):
            h = h + jax.nn.relu(gcn_conv(h, gcn_W[l], gcn_b[l]))
        return h @ W_out.T + b_out

    def _L1_gnn_ref(x, edge_index, W1, b1, a1, W2, b2):
        import jax, jax.numpy as jnp
        import numpy as np
        N = 6250
        E = 100000
        D = 96

        def _gcn_conv(x, W, b, src, dst, norm, n):
            h = x @ W
            msg = h[src] * norm[:, None]
            out = jax.ops.segment_sum(msg, dst, num_segments=n)
            return out + b
        n = x.shape[0]
        loop = jnp.arange(n, dtype=edge_index.dtype)
        src = jnp.concatenate([edge_index[0], loop])
        dst = jnp.concatenate([edge_index[1], loop])
        ones = jnp.ones(src.shape[0], dtype=x.dtype)
        deg = jax.ops.segment_sum(ones, dst, num_segments=n)
        dinv = jnp.where(deg > 0, jax.lax.rsqrt(deg), 0.0)
        norm = dinv[src] * dinv[dst]
        h = _gcn_conv(x, W1, b1, src, dst, norm, n)
        h = jnp.where(h > 0, h, a1 * h)
        h = _gcn_conv(h, W2, b2, src, dst, norm, n)
        return h

    def _L2_gnn_ref(x, edge_index, edge_attr, mW1, mb1, mW2, mb2, gW1, gb1, gW2, gb2, uW1, ub1, uW2, ub2, ln_g, ln_b):
        import jax, jax.numpy as jnp
        import numpy as np
        N, E = (6250, 100000)
        ND, ED = (96, 32)

        def _gelu(x):
            return jax.nn.gelu(x, approximate=False)
        src, dst = (edge_index[0], edge_index[1])
        edge_input = jnp.concatenate([x[src], edge_attr], axis=-1)
        messages = _gelu(edge_input @ mW1 + mb1) @ mW2 + mb2
        gates = jax.nn.sigmoid(_gelu(edge_input @ gW1 + gb1) @ gW2 + gb2)
        aggregated = jax.ops.segment_sum(messages * gates, dst, num_segments=x.shape[0])
        combined = jnp.concatenate([x, aggregated], axis=-1)
        update = _gelu(combined @ uW1 + ub1) @ uW2 + ub2
        h = x + update
        mu = jnp.mean(h, axis=-1, keepdims=True)
        var = jnp.mean(jnp.square(h - mu), axis=-1, keepdims=True)
        return (h - mu) * jax.lax.rsqrt(var + 1e-05) * ln_g + ln_b

    def _L3_gnn_ref(embeds, qW, kW, vW, rows, cols):
        import jax, jax.numpy as jnp
        import numpy as np
        N_NODES = 6250
        N_EDGES = 100000
        D_MODEL = 96
        HEADS = 4
        nvar, d = embeds.shape
        dh = d // HEADS
        e = rows.shape[0]
        q = (embeds[rows] @ qW).reshape(e, HEADS, dh)
        k = (embeds[cols] @ kW).reshape(e, HEADS, dh)
        v = (embeds[cols] @ vW).reshape(e, HEADS, dh)
        scores = jnp.clip(jnp.einsum('ehd,ehd->eh', q, k), -10.0, 10.0)
        exp_s = jnp.exp(scores)
        norms = jax.ops.segment_sum(exp_s, rows, num_segments=nvar)[rows]
        w = exp_s / (norms + 1e-08)
        res = jax.ops.segment_sum(w[:, :, None] * v, rows, num_segments=nvar).reshape(nvar, d)
        return embeds + res
    edge_index = jnp.stack([src, dst])
    h = jnp.maximum(_layernorm(x, axis=-1), 0.0)
    x = x + _L0_gnn_ref(h, edge_index, L0_gnn_W_in, L0_gnn_b_in, L0_gnn_gcn_W, L0_gnn_gcn_b, L0_gnn_W_out, L0_gnn_b_out)
    h = jnp.maximum(_layernorm(x, axis=-1), 0.0)
    x = x + _L1_gnn_ref(h, edge_index, L1_gnn_W1, L1_gnn_b1, L1_gnn_a1, L1_gnn_W2, L1_gnn_b2)
    h = jnp.maximum(_layernorm(x, axis=-1), 0.0)
    x = x + _L2_gnn_ref(h, edge_index, edge_attr_32, L2_gnn_mW1, L2_gnn_mb1, L2_gnn_mW2, L2_gnn_mb2, L2_gnn_gW1, L2_gnn_gb1, L2_gnn_gW2, L2_gnn_gb2, L2_gnn_uW1, L2_gnn_ub1, L2_gnn_uW2, L2_gnn_ub2, L2_gnn_ln_g, L2_gnn_ln_b)
    h = jnp.maximum(_layernorm(x, axis=-1), 0.0)
    x = x + _L3_gnn_ref(h, L3_gnn_qW, L3_gnn_kW, L3_gnn_vW, src, dst)
    return x

_drawn_inputs = setup_inputs


def setup_inputs(seed=0):
    import zlib

    import numpy as np

    out = dict(_drawn_inputs(seed))
    spreads = {'L0_gnn_b_in': (0.0, 0.1),
     'L0_gnn_gcn_b': (0.0, 0.1),
     'L0_gnn_b_out': (0.0, 0.1),
     'L1_gnn_b1': (0.0, 0.1),
     'L1_gnn_b2': (0.0, 0.1),
     'L2_gnn_mb1': (0.0, 0.1),
     'L2_gnn_mb2': (0.0, 0.1),
     'L2_gnn_gb1': (0.0, 2.0),
     'L2_gnn_ub1': (0.0, 0.429),
     'L2_gnn_ub2': (0.0, 0.1),
     'L2_gnn_ln_g': (1.0, 0.2),
     'L2_gnn_ln_b': (0.0, 0.1)}
    factors = {'L2_gnn_gW1': 8.0, 'L2_gnn_gW2': 8.0}
    for name, (base, spread) in spreads.items():
        noise = np.random.default_rng([zlib.crc32(name.encode()), seed]).standard_normal(out[name].shape)
        drawn = base * np.exp(spread * noise) if base else spread * noise
        out[name] = jnp.asarray(drawn.astype(out[name].dtype))
    for name, factor in factors.items():
        out[name] = (out[name] * factor).astype(out[name].dtype)
    return out
```

```python
from contextlib import ExitStack

import numpy as np

import concourse.bass as bass
from concourse import mybir

F32 = mybir.dt.float32
BF16 = mybir.dt.bfloat16
I32 = mybir.dt.int32
ALU = mybir.AluOpType
ACT = mybir.ActivationFunctionType
AX_X = mybir.AxisListType.X

N = 6250
E = 200000
D = 96
ED = 32
HEADS = 4
DH = D // HEADS
P = 128
TILES = -(-N // P)
NPAD = TILES * P
FULL = N // P
REST = N - FULL * P
GRP = 4
GROUPS = -(-TILES // GRP)

CH = 125
STEPS = E // CH
U = 16
ITER = STEPS // (2 * U)
assert CH * STEPS == E and ITER * 2 * U == STEPS

EG = 4
MW = D + 1
AW = D + HEADS
ACCS = 3
TRASH = P
AROWS = 50 * P
assert AROWS >= N + TRASH
GW = 3 * D

BIASES = ["L0_gnn_b_in", "L0_gnn_b_out", "L1_gnn_b1", "L1_gnn_b2", "L2_gnn_mb1", "L2_gnn_gb1", "L2_gnn_mb2",
          "L2_gnn_ub1", "L2_gnn_ub2", "L2_gnn_ln_g", "L2_gnn_ln_b"]
WEIGHTS = ["W_in_T", "gcn_T0", "gcn_T1", "gcn_T2", "W_out_T", "L1_gnn_W1", "L1_gnn_W2", "mW1_x", "gW1_x",
           "L2_gnn_mW2", "uW1_x", "uW1_a", "L2_gnn_uW2", "L3_gnn_qW", "L3_gnn_kW", "L3_gnn_vW"]

C_ID, C_TRI, C_IOTA = 0, P, 2 * P
C_BEFORE = C_IOTA + GRP * P
C_TRASH = C_BEFORE + P
C_GRP = C_TRASH + 1
C_W = C_GRP + GROUPS

PASS_L2, PASS_L3 = 5, 6


def shape_constants():
    c = np.zeros((P, C_W), np.float32)
    c[:, C_ID:C_ID + P] = np.eye(P)
    c[:, C_TRI:C_TRI + P] = np.triu(np.ones((P, P)))
    c[:, C_IOTA:C_IOTA + GRP * P] = np.arange(GRP * P)
    c[:, C_BEFORE:C_BEFORE + P] = np.tril(np.ones((P, P)), -1)
    c[:, C_TRASH] = N + np.arange(P)
    c[:, C_GRP:C_GRP + GROUPS] = np.arange(GROUPS) * GRP * P
    return c


def build(nc, x, src, dst, src_rows, edge_t, consts, weights, bias, gcn_b, scalars, gate_w, mg_edge, out):
    def dram(name, shape, dt=F32):
        return nc.dram_tensor(name, shape, dt, kind="Internal").ap()

    table = dram("table", (NPAD, D))
    table_mg = dram("table_mg", (NPAD, 2 * D))
    table_q = dram("table_q", (NPAD, D))
    table_kv = dram("table_kv", (NPAD, 2 * D))
    run_d = dram("run_d", (E, D))
    run_m = dram("run_m", (E, MW))
    acc_d = [dram(f"acc{a}", (AROWS, AW)) for a in range(ACCS)]

    def by_chunk(ap):
        return ap.rearrange("(p s) f -> p s f", p=CH)

    def by_tile(ap):
        return ap.rearrange("(t p) f -> p t f", p=P)

    with ExitStack() as ctx:
        def sb(name, shape, dt=F32):
            return ctx.enter_context(nc.sbuf_tensor(name, shape, dt))

        def ps(name, shape, dt=F32):
            return ctx.enter_context(nc.psum_tensor(name, shape, dt))

        def sem(name):
            return ctx.enter_context(nc.semaphore(name))

        X = sb("X", [P, TILES, D])
        H = sb("H", [P, TILES, D])
        T = sb("T", [P, TILES, D])
        V = sb("V", [P, TILES, D])
        AGG = sb("AGG", [P, TILES, AW])
        G = sb("G", [P, 2, U, GW])
        A = sb("A", [P, 2, U, 2 * D])
        R = sb("R", [CH, 2, U, AW])
        M = sb("M", [CH, U, AW])
        EA = sb("EA", [P, 2, EG, CH])
        keep = sb("keep", [CH, STEPS])
        kp = sb("kp", [CH, 2, U])
        si = [sb(f"si{h}", [CH, U], I32) for h in (0, 1)]
        di = [sb(f"di{h}", [CH, U], I32) for h in (0, 1)]
        ai = [sb(f"ai{h}", [CH, U], I32) for h in (0, 1)]
        small = sb("small", [CH, 4, U * HEADS])
        C = sb("C", [P, C_W])
        W = sb("W", [D, len(WEIGHTS), D])
        B = sb("B", [P, len(BIASES) + 3, D])
        gw2 = sb("gw2", [P, D])
        sc = sb("sc", [P, 2])
        BD = sb("BD", [P, EG, 2, D])
        hT = sb("hT", [D, 2, GRP * P])
        deg = sb("deg", [P, TILES])
        dinv = sb("dinv", [P, TILES])
        has_in = sb("has_in", [P, TILES])
        ends = sb("ends", [P, TILES], I32)
        st = sb("st", [P, 6, TILES])
        lastg = sb("lastg", [CH, GROUPS])
        open_c = sb("open_c", [CH, 1])
        nxt = sb("nxt", [CH, 1], I32)

        scratch = AGG[:, :, :].rearrange("p t f -> p (t f)")
        dst_i = scratch[0:CH, 0:STEPS].bitcast(I32)
        dst_hi = scratch[0:CH, STEPS:2 * STEPS]
        dst_lo = scratch[0:CH, 2 * STEPS:3 * STEPS]
        OH = M[:, :, :].rearrange("p u f -> p (u f)")[:, 0:2 * GRP * P].rearrange("p (k n) -> p k n", k=2)
        g_flat = G[:, :, :, :].rearrange("p h u f -> p (h u f)")
        a_flat = A[:, :, :, :].rearrange("p h u f -> p (h u f)")
        lo_bits = [a_flat[0:CH, h * U * P // 2:(h + 1) * U * P // 2].bitcast(BF16).rearrange("p (u f) -> p u f", u=U)
                   for h in (0, 1)]
        hi_bits = [g_flat[0:CH, h * 1024:h * 1024 + U * 64 // 2].bitcast(BF16).rearrange("p (u f) -> p u f", u=U)
                   for h in (0, 1)]
        same = [a_flat[0:CH, h * U * P:h * U * P + U * CH].rearrange("p (u j) -> p u j", u=U) for h in (0, 1)]
        srow = V[:, :, :].rearrange("p t f -> p (t f)")[0:CH, 0:2 * U * CH].bitcast(I32).rearrange(
            "p (h u j) -> p h u j", h=2, u=U)
        stmp = T[:, :, :].rearrange("p t f -> p (t f)")[0:CH, 0:U * CH].rearrange("p (u j) -> p u j", u=U)
        gmg = [G[0:CH, h, :, 0:2 * D] for h in (0, 1)]

        p_tr = [ps(f"p_tr{k}", [P, 512]) for k in (0, 1)]
        p_mm = [ps(f"p_mm{k}", [P, 512]) for k in (0, 1)]
        p_e = [ps(f"p_e{k}", [P, 512]) for k in range(4)]

        inputs_landed = sem("inputs_landed")
        zeros_landed = sem("zeros_landed")
        cleared = sem("cleared")
        bd_cleared = sem("bd_cleared")
        onehot_ready = sem("onehot_ready")
        onehot_used = sem("onehot_used")
        deg_counted = sem("deg_counted")
        deg_ready = sem("deg_ready")
        cum_ready = sem("cum_ready")
        root_wanted = sem("root_wanted")
        root_ready = sem("root_ready")
        nodes_ready = sem("nodes_ready")
        turned = sem("turned")
        hT_ready = sem("hT_ready")
        product = sem("product")
        product_used = sem("product_used")
        table_ready = sem("table_ready")
        table_stored = sem("table_stored")
        idx_landed = [sem(f"idx_landed{h}") for h in (0, 1)]
        rows_landed = [[sem(f"rows_landed{n}_{h}") for h in (0, 1)] for n in range(7)]
        rows_used = [sem(f"rows_used{h}") for h in (0, 1)]
        sums_ready = [sem(f"sums_ready{h}") for h in (0, 1)]
        sums_stored = [sem(f"sums_stored{h}") for h in (0, 1)]
        ends_landed = sem("ends_landed")
        open_ready = sem("open_ready")
        edge_landed = [sem(f"edge_landed{h}") for h in (0, 1)]
        edge_product = sem("edge_product")
        edge_added = sem("edge_added")
        gelu_done = sem("gelu_done")
        logit_ready = sem("logit_ready")
        gate_ready = sem("gate_ready")
        gelu_wanted = sem("gelu_wanted")
        gelu_nodes = sem("gelu_nodes")
        srow_landed = [sem(f"srow_landed{h}") for h in (0, 1)]
        targets_ready = sem("targets_ready")
        score_ready = sem("score_ready")
        exp_ready = sem("exp_ready")
        msg_ready = sem("msg_ready")
        combined = sem("combined")
        comb_ready = sem("comb_ready")
        scattered = [sem(f"scattered{a}") for a in range(ACCS)]
        acc_landed = sem("acc_landed")
        out_ready = sem("out_ready")
        pool_passed = sem("pool_passed")
        sp_passed = sem("sp_passed")
        out_stored = sem("out_stored")

        block = ctx.enter_context(nc.Block())

        def wait(eng, s, v):
            if not isinstance(v, int) or v > 0:
                eng.wait_ge(s, v)

        def turns(eng, body, n):
            if n in (0, PASS_L2, PASS_L3):
                body(0)
                with eng.Fori(1, ITER) as i:
                    body(i)
            else:
                with eng.Fori(0, ITER) as i:
                    body(i)

        def passed(eng, s):
            eng.sem_inc(s, 1)

        n_inputs = 15

        @block.sync
        def _(sp):
            def load(to, of, slow=False):
                sp.dma_start(to, of, allow_slow_non_contiguous=slow).then_inc(inputs_landed, 16)

            load(C[:, :], consts)
            load(dst_i, dst.rearrange("(p s) -> p s", p=CH))
            load(nxt[0:CH - 1, :], dst.rearrange("(p s) -> p s", p=CH)[1:CH, 0:1], slow=True)
            load(nxt[CH - 1:CH, :], dst.rearrange("(p s) -> p s", p=CH)[0:1, 0:1], slow=True)
            load(W[:, :, :], weights.rearrange("n i o -> i n o"))
            load(B[:, 0:len(BIASES), :], bias.unsqueeze(0).to_broadcast((P, len(BIASES), D)))
            load(B[:, len(BIASES):, :], gcn_b.unsqueeze(0).to_broadcast((P, 3, D)))
            load(gw2[:, :], gate_w.unsqueeze(0).to_broadcast((P, D)))
            load(sc[:, :], scalars.unsqueeze(0).to_broadcast((P, 2)))
            sp.wait_ge(bd_cleared, 2)
            for a in range(EG):
                load(BD[a * ED:(a + 1) * ED, a, :, :], mg_edge)
            load(X[:, 0:FULL, :], by_tile(x[0:FULL * P, :]))
            load(X[0:REST, FULL, :], x[FULL * P:N, :])
            sp.wait_ge(cleared, 1)
            for a in range(ACCS):
                sp.dma_start(acc_d[a].rearrange("(p t) f -> p (t f)", p=P),
                             g_flat[:, 0:AROWS // P * AW]).then_inc(zeros_landed, 16)

            def put_table(k, to, of):
                sp.wait_ge(table_ready, k)
                sp.dma_start(by_tile(to), of).then_inc(table_stored, 16)

            def load_src(h, i):
                sp.dma_start(si[h][:, :], src.rearrange("(p s) -> p s", p=CH)[:, bass.ds(i * (2 * U) + U * h, U)]
                             ).then_inc(idx_landed[h], 16)

            def sum_pass(n, run):
                def body(i, last=False):
                    for h in (0, 1):
                        sp.wait_ge(rows_landed[n][h], (i + 1) * (16 * U))
                        passed(sp, sp_passed)
                        if not last:
                            load_src(h, i + 1)
                        if n == PASS_L2 and not last:
                            load_edges(h, i + 1)
                        sp.wait_ge(sums_ready[h], i + (n * ITER + 1))
                        passed(sp, sp_passed)
                        sp.dma_start(by_chunk(run)[:, bass.ds(i * (2 * U) + U * h, U), :],
                                     R[:, h, :, 0:run.shape[1]]).then_inc(sums_stored[h], 16)
                load_src(0, 0)
                load_src(1, 0)
                if n == PASS_L2:
                    load_edges(0, 0)
                    load_edges(1, 0)
                with sp.Fori(0, ITER - 1) as i:
                    body(i)
                body(ITER - 1, last=True)

            def load_edges(h, i):
                wait(sp, edge_added, i * 8 + (4 * h - 4) if not isinstance(i, int) or i > 0 else 0)
                passed(sp, sp_passed)
                sp.dma_start(EA[:, h, :, :], edge_t[:, bass.ds(i * (2 * U // EG) + (U // EG) * h, U // EG), :]
                             ).then_inc(edge_landed[h], 16)

            for n in range(5):
                put_table(n + 1, table, T[:, :, :])
                sum_pass(n, run_d)
            put_table(6, table_mg[:, 0:D], T[:, :, :])
            put_table(6, table_mg[:, D:2 * D], V[:, :, :])
            sum_pass(PASS_L2, run_m)

            put_table(7, table_q, T[:, :, :])
            put_table(7, table_kv[:, 0:D], V[:, :, :])
            put_table(7, table_kv[:, D:2 * D], AGG[:, :, 0:D])

            def load_l3(h, i):
                load_src(h, i)
                sp.dma_start(di[h][:, :], dst.rearrange("(p s) -> p s", p=CH)[:, bass.ds(i * (2 * U) + U * h, U)]
                             ).then_inc(idx_landed[h], 16)
                sp.dma_start(srow[:, h, :, :],
                             src_rows[bass.ds(i * (2 * U) + U * h, U), :].unsqueeze(0).to_broadcast((CH, U, CH))
                             ).then_inc(srow_landed[h], 16)

            sp.wait_ge(table_stored, 16 * 10)
            load_l3(0, 0)
            load_l3(1, 0)
            with sp.Fori(0, ITER - 1) as i:
                for h in (0, 1):
                    sp.wait_ge(rows_landed[PASS_L3][h], (i + 1) * (32 * U))
                    passed(sp, sp_passed)
                    sp.wait_ge(targets_ready, i * 2 + (1 + h))
                    passed(sp, sp_passed)
                    load_l3(h, i + 1)
            for a in range(ACCS):
                steps = len(range(a, U, ACCS))
                sp.wait_ge(scattered[a], 16 * steps * 2 * ITER)
            sp.wait_ge(comb_ready, 2 * ITER)
            by = [AGG[:, :, :].rearrange("p t f -> p (t f)"), g_flat, a_flat]
            for a in range(ACCS):
                sp.dma_start(by[a][:, 0:TILES * AW].rearrange("p (t f) -> p t f", t=TILES),
                             by_tile(acc_d[a][0:NPAD, :])).then_inc(acc_landed, 16)
            sp.wait_ge(out_ready, 1)
            sp.dma_start(by_tile(out[0:FULL * P, :]), X[:, 0:FULL, :]).then_inc(out_stored, 16)
            sp.dma_start(out[FULL * P:N, :], X[0:REST, FULL, :]).then_inc(out_stored, 16)
            sp.wait_ge(out_stored, 32)

        @block.gpsimd
        def _(pool):
            pool.memset(g_flat[:, 0:AROWS // P * AW], 0.0).then_inc(cleared, 1)

            def gather(to, of, at, s):
                pool.indirect_dma_start(out=to, out_offset=None, in_=of,
                                        in_offset=bass.IndirectOffsetOnAxis(ap=at, axis=0)).then_inc(s, 16)

            def sum_pass(n, of, run, stored):
                width, w = of.shape[1], run.shape[1]

                def body(i):
                    for h in (0, 1):
                        wait(pool, rows_used[h], i + n * ITER)
                        pool.wait_ge(idx_landed[h], i * 16 + (n * ITER + 1) * 16)
                        passed(pool, pool_passed)
                        for j in range(U):
                            gather(G[0:CH, h, j, 0:width], of, si[h][:, j:j + 1], rows_landed[n][h])
                pool.wait_ge(table_stored, stored)
                turns(pool, body, n)
                for h in (0, 1):
                    pool.wait_ge(sums_stored[h], 16 * (n + 1) * ITER)
                for t in range(TILES):
                    gather(AGG[:, t, 0:w], run, ends[:, t:t + 1], ends_landed)

            pool.wait_ge(zeros_landed, 16 * ACCS)
            for n in range(5):
                sum_pass(n, table, run_d, 16 * (n + 1))
            sum_pass(PASS_L2, table_mg, run_m, 16 * 7)

            def gathers(h, i, n=PASS_L3):
                wait(pool, rows_used[h], i + PASS_L3 * ITER)
                pool.wait_ge(idx_landed[h], i * 32 + (PASS_L3 * ITER * 16 + 32))
                passed(pool, pool_passed)
                for j in range(U):
                    gather(G[0:CH, h, j, 0:D], table_q, si[h][:, j:j + 1], rows_landed[n][h])
                    gather(G[0:CH, h, j, D:3 * D], table_kv, di[h][:, j:j + 1], rows_landed[n][h])

            def scatters(h, i):
                pool.wait_ge(comb_ready, i * 2 + (1 + h))
                for j in range(U):
                    a = j % ACCS
                    steps = len(range(a, U, ACCS))
                    wait(pool, scattered[a], i * (32 * steps) + 16 * (h * steps + j // ACCS))
                    passed(pool, pool_passed)
                    pool.indirect_dma_start(out=acc_d[a],
                                            out_offset=bass.IndirectOffsetOnAxis(ap=ai[h][:, j:j + 1], axis=0),
                                            in_=R[:, h, j, :], in_offset=None,
                                            compute_op=ALU.add).then_inc(scattered[a], 16)

            pool.wait_ge(table_stored, 16 * 10)
            gathers(0, 0)
            gathers(1, 0)
            scatters(0, 0)
            with pool.Fori(1, ITER) as i:
                gathers(0, i)
                scatters(1, i + (-1))
                gathers(1, i)
                scatters(0, i)
            scatters(1, ITER - 1)

        @block.tensor
        def _(pe):
            pe.wait_ge(inputs_landed, 16 * n_inputs)
            ident = C[:, C_ID:C_ID + P]
            counts = p_e[0][:, 0:TILES]

            def count(i, h, first=False, last=False):
                pe.wait_ge(onehot_ready, i * 2 + (1 + h))
                for j in range(U):
                    mm = pe.matmul(counts, lo_bits[h][:, j, :], hi_bits[h][:, j, 0:TILES],
                                   start=first and j == 0, stop=last and j == U - 1)
                mm.then_inc(onehot_used, 1)
            count(0, 0, first=True)
            count(0, 1)
            with pe.Fori(1, ITER - 1) as i:
                count(i, 0)
                count(i, 1)
            count(ITER - 1, 0)
            count(ITER - 1, 1, last=True)
            pe.wait_ge(deg_ready, 1)
            pe.matmul(p_mm[0][:, 0:TILES], C[:, C_TRI:C_TRI + P], deg[:, :], start=True, stop=True)
            pe.matmul(p_mm[1][:, 0:TILES], C[:, C_TRI + P - 1:C_TRI + P].to_broadcast((P, P)), deg[:, :], start=True, stop=True).then_inc(cum_ready, 1)

            at = {"turn": 0, "mm": 0, "stage": 0}

            def dense(h_in, ws):
                at["stage"] += 1
                pe.wait_ge(nodes_ready, at["stage"])

                def turn(g):
                    k = at["turn"] + g
                    wait(pe, hT_ready, k - 1)
                    for t in range(GRP * g, min(GRP * g + GRP, TILES)):
                        o = (t - GRP * g) * P
                        mm = pe.transpose(p_tr[k % 2][0:D, o:o + P], h_in[:, t, 0:D], ident)
                    mm.then_inc(turned, 1)
                turn(0)
                for g in range(GROUPS):
                    if g + 1 < GROUPS:
                        turn(g + 1)
                    k = at["turn"] + g
                    pe.wait_ge(hT_ready, k + 1)
                    for w in ws:
                        wait(pe, product_used, at["mm"] - 1)
                        for t in range(GRP * g, min(GRP * g + GRP, TILES)):
                            o = t - GRP * g
                            mm = pe.matmul(p_mm[at["mm"] % 2][:, o * D:(o + 1) * D],
                                           hT[:, k % 2, o * P:(o + 1) * P], W[:, WEIGHTS.index(w), :],
                                           start=True, stop=True)
                        mm.then_inc(product, 1)
                        at["mm"] += 1
                at["turn"] += GROUPS

            def close(n, w):
                for g in range(GROUPS):
                    pe.wait_ge(open_ready, n * GROUPS + g + 1)
                    wait(pe, product_used, at["mm"] - 1)
                    for t in range(GRP * g, min(GRP * g + GRP, TILES)):
                        o = t - GRP * g
                        mm = pe.matmul(p_mm[at["mm"] % 2][:, o * w:(o + 1) * w], OH[:, g % 2, o * P:(o + 1) * P],
                                       R[:, 1, U - 1, 0:w], start=True, stop=True)
                    mm.then_inc(product, 1)
                    at["mm"] += 1

            dense(H, ["W_in_T"])
            for n in range(3):
                dense(H, [f"gcn_T{n}"])
                close(n, D)
            dense(H, ["W_out_T"])
            dense(H, ["L1_gnn_W1"])
            close(3, D)
            dense(H, ["L1_gnn_W2"])
            close(4, D)
            dense(H, ["mW1_x", "gW1_x"])

            def edge_products(i):
                for h in (0, 1):
                    pe.wait_ge(edge_landed[h], i * 16 + 16)
                    for g in range(U // EG):
                        k = i * (2 * U // EG) + (h * U // EG + g - 1)
                        wait(pe, edge_added, k)
                        for c in (0, 1):
                            mm = pe.matmul(p_e[2 * (g % 2) + c][0:CH, 0:4 * D], EA[:, h, g, :],
                                           BD[:, 2 * c:2 * c + 2, :, :].rearrange("p a b f -> p (a b f)"),
                                           start=True, stop=True)
                        mm.then_inc(edge_product, 1)
            turns(pe, edge_products, PASS_L2)
            close(PASS_L2, MW)
            dense(AGG, ["L2_gnn_mW2"])
            dense(H, ["uW1_x"])
            dense(V, ["uW1_a"])
            dense(T, ["L2_gnn_uW2"])
            dense(H, ["L3_gnn_qW", "L3_gnn_kW", "L3_gnn_vW"])

            def combine(i):
                for h in (0, 1):
                    pe.wait_ge(msg_ready, i * 2 + (1 + h))
                    wait(pe, comb_ready, i * 2 + h)
                    for j in range(U):
                        mm = pe.matmul(p_e[j // 4][0:CH, (j % 4) * P:(j % 4) * P + AW], same[h][:, j, :], M[:, j, :],
                                       start=True, stop=True)
                    mm.then_inc(combined, 1)
            turns(pe, combine, PASS_L3)

        @block.scalar
        def _(act):
            act.wait_ge(inputs_landed, 16 * n_inputs)
            at = {"turn": 0, "mm": 0}

            def root(k):
                act.wait_ge(root_wanted, k)
                act.activation(st[:, 1, :], st[:, 0, :], ACT.Sqrt).then_inc(root_ready, 1)

            def dense(n_w):
                for g in range(GROUPS):
                    k = at["turn"]
                    act.wait_ge(turned, k + 1)
                    if g >= 2:
                        act.wait_ge(product, at["mm"] + (g - 1) * n_w)
                    cols = min(GRP, TILES - GRP * g) * P
                    act.activation(hT[:, k % 2, 0:cols], p_tr[k % 2][0:D, 0:cols], ACT.Copy).then_inc(hT_ready, 1)
                    at["turn"] += 1
                at["mm"] += n_w * GROUPS

            def close():
                at["mm"] += GROUPS

            root(1)
            root(2)
            dense(1)
            for n in range(3):
                dense(1)
                close()
            dense(1)
            root(3)
            dense(1)
            close()
            dense(1)
            close()
            root(4)
            dense(2)

            def gelus(i):
                for h in (0, 1):
                    act.wait_ge(edge_added, i * (2 * U // EG) + (h + 1) * (U // EG))
                    wait(act, sums_ready[h], i + PASS_L2 * ITER)
                    act.activation(A[0:CH, h, :, :], gmg[h], ACT.Gelu).then_inc(gelu_done, 1)
                    act.wait_ge(gelu_done, i * 2 + (1 + h))
                    act.sem_inc(rows_used[h], 1)
                    act.wait_ge(logit_ready, i * 2 + (1 + h))
                    act.activation(small[:, 1, 0:U], small[:, 0, 0:U], ACT.Sigmoid,
                                   bias=sc[0:CH, 1:2]).then_inc(gate_ready, 1)
            turns(act, gelus, PASS_L2)
            close()
            dense(1)
            dense(1)
            dense(1)
            act.wait_ge(gelu_wanted, 1)
            act.activation(T[:, :, :], T[:, :, :], ACT.Gelu).then_inc(gelu_nodes, 1)
            dense(1)
            root(5)
            root(6)
            dense(3)

            def exps(i):
                for h in (0, 1):
                    act.wait_ge(score_ready, i * 2 + (1 + h))
                    act.activation(M[:, :, D:AW], small[:, 1, :].rearrange("p (u e) -> p u e", u=U),
                                   ACT.Exp).then_inc(exp_ready, 1)
                    act.wait_ge(combined, i * 2 + (1 + h))
                    for a in range(ACCS):
                        steps = len(range(a, U, ACCS))
                        wait(act, scattered[a], i * (32 * steps) + 16 * steps * (h - 1)
                             if not isinstance(i, int) or i > 0 else 0)
                    for k in range(U // 4):
                        cp = act.activation(R[:, h, 4 * k:4 * k + 4, :],
                                            p_e[k][0:CH, :].rearrange("p (u f) -> p u f", u=4)[:, :, 0:AW], ACT.Copy)
                    cp.then_inc(comb_ready, 1)
            turns(act, exps, PASS_L3)

        @block.vector
        def _(dve):
            at = {"mm": 0, "root": 0, "table": 0}
            nodes = [P, TILES, D]

            def per_node(ap):
                return ap.unsqueeze(2).to_broadcast(nodes)

            def per_feature(name):
                k = BIASES.index(name) if name in BIASES else len(BIASES) + int(name)
                return B[:, k, :].unsqueeze(1).to_broadcast(nodes)

            dve.memset(BD[:, :, :, :], 0.0).then_inc(bd_cleared, 1)
            dve.memset(X[:, FULL, :], 0.0).then_inc(bd_cleared, 1)
            dve.wait_ge(inputs_landed, 16 * n_inputs)

            dve.memset(keep[:, 0:1], 0.0)
            dve.tensor_tensor(keep[:, 1:STEPS], dst_i[:, 1:STEPS], dst_i[:, 0:STEPS - 1], ALU.is_equal)
            dve.tensor_single_scalar(dst_hi.bitcast(I32), dst_i, 7, ALU.arith_shift_right)
            dve.tensor_single_scalar(dst_lo.bitcast(I32), dst_i, P - 1, ALU.bitwise_and)
            dve.tensor_tensor(open_c[:, :], nxt[:, :], dst_i[:, STEPS - 1:STEPS], ALU.is_equal)
            dve.tensor_copy(lastg[:, 0:1], dst_i[:, STEPS - 1:STEPS])
            dve.drain()
            dve.tensor_copy(dst_hi, dst_hi.bitcast(I32))
            dve.tensor_copy(dst_lo, dst_lo.bitcast(I32))
            dve.tensor_tensor(open_c[:, :], open_c[:, :], C[0:CH, C_ID + CH - 1:C_ID + CH], ALU.is_gt)
            dve.tensor_scalar(lastg[:, 1:GROUPS], C[0:CH, C_GRP + 1:C_GRP + GROUPS], lastg[:, 0:1], -1.0,
                              ALU.subtract, ALU.mult)
            dve.drain()

            dve.wait_ge(zeros_landed, 16 * ACCS)

            def onehots(i):
                for h in (0, 1):
                    wait(dve, onehot_used, i * 2 + (h - 1) if not isinstance(i, int) or i > 0 else 0)
                    at_step = bass.ds(i * (2 * U) + U * h, U)
                    dve.tensor_tensor(lo_bits[h][:, :, :], dst_lo[:, at_step].unsqueeze(2).to_broadcast([CH, U, P]),
                                      C[0:CH, C_IOTA:C_IOTA + P].unsqueeze(1).to_broadcast([CH, U, P]), ALU.is_equal)
                    dve.tensor_tensor(hi_bits[h][:, :, 0:TILES],
                                      dst_hi[:, at_step].unsqueeze(2).to_broadcast([CH, U, TILES]),
                                      C[0:CH, C_IOTA:C_IOTA + TILES].unsqueeze(1).to_broadcast([CH, U, TILES]),
                                      ALU.is_equal).then_inc(onehot_ready, 1)
            turns(dve, onehots, 0)
            dve.wait_ge(onehot_used, 2 * ITER)
            dve.tensor_copy(deg[:, :], p_e[0][:, 0:TILES]).then_inc(deg_ready, 1)

            def rsqrt(v_plus):
                at["root"] += 1
                dve.tensor_scalar(st[:, 0, :], st[:, 0, :], v_plus, None, ALU.add).then_inc(root_wanted, 1)
                dve.wait_ge(root_ready, at["root"])
                dve.reciprocal(st[:, 2, :], st[:, 1, :])
                dve.drain()
                dve.tensor_tensor(st[:, 1, :], st[:, 2, :], st[:, 2, :], ALU.mult)
                dve.drain()
                dve.tensor_tensor(st[:, 1, :], st[:, 1, :], st[:, 0, :], ALU.mult)
                dve.drain()
                dve.tensor_scalar(st[:, 1, :], st[:, 1, :], -0.5, 1.5, ALU.mult, ALU.add)
                dve.drain()
                dve.tensor_tensor(st[:, 2, :], st[:, 2, :], st[:, 1, :], ALU.mult)
                dve.drain()

            dve.drain()
            dve.tensor_copy(st[:, 0, :], deg[:, :])
            dve.tensor_scalar(has_in[:, :], deg[:, :], 0.0, None, ALU.is_gt)
            dve.drain()
            rsqrt(1.0)
            dve.tensor_copy(dinv[:, :], st[:, 2, :])
            dve.wait_ge(cum_ready, 1)
            dve.tensor_copy(st[:, 4, :], p_mm[1][:, 0:TILES])
            dve.memset(st[:, 5, :], 1.0)
            dve.drain()
            dve.tensor_tensor_scan(st[:, 3, :], st[:, 5, :], st[:, 4, :], 0.0, ALU.mult, ALU.add)
            dve.drain()
            dve.tensor_tensor(st[:, 3, :], st[:, 3, :], st[:, 4, :], ALU.subtract)
            dve.drain()
            dve.tensor_tensor(st[:, 3, :], st[:, 3, :], p_mm[0][:, 0:TILES], ALU.add)
            dve.drain()
            dve.tensor_scalar(ends[:, :], st[:, 3, :], -1.0, 0.0, ALU.add, ALU.max)
            dve.drain()

            def norm(to, of, tmp, finish):
                dve.tensor_reduce(st[:, 3, :], of[:, :, :], AX_X, ALU.add)
                dve.drain()
                dve.tensor_scalar(st[:, 3, :], st[:, 3, :], 1.0 / D, None, ALU.mult)
                dve.drain()
                dve.tensor_tensor(to[:, :, :], of[:, :, :], per_node(st[:, 3, :]), ALU.subtract)
                dve.drain()
                dve.tensor_tensor(tmp[:, :, :], to[:, :, :], to[:, :, :], ALU.mult)
                dve.drain()
                dve.tensor_reduce(st[:, 0, :], tmp[:, :, :], AX_X, ALU.add)
                dve.drain()
                dve.tensor_scalar(st[:, 0, :], st[:, 0, :], 1.0 / D, None, ALU.mult)
                dve.drain()
                rsqrt(1e-5)
                dve.tensor_tensor(to[:, :, :], to[:, :, :], per_node(st[:, 2, :]), ALU.mult)
                dve.drain()
                finish()

            def relu_nodes(ap):
                dve.tensor_scalar(ap[:, :, :], ap[:, :, :], 0.0, None, ALU.max).then_inc(nodes_ready, 1)
                dve.drain()

            def dense(tos, ready=False):
                if ready:
                    dve.sem_inc(nodes_ready, 1)
                for g in range(GROUPS):
                    for to in tos:
                        dve.wait_ge(product, at["mm"] + 1)
                        n_t = min(GRP, TILES - GRP * g)
                        dve.tensor_copy(to[:, GRP * g:GRP * g + n_t, 0:D],
                                        p_mm[at["mm"] % 2][:, 0:n_t * D].rearrange("p (t f) -> p t f", t=n_t)
                                        ).then_inc(product_used, 1)
                        at["mm"] += 1
                dve.drain()

            def running_sums(n, h, i, msg, w):
                for j in range(U):
                    before = R[:, h, j - 1, 0:w] if j else R[:, 1 - h, U - 1, 0:w]
                    dve.drain()
                    if j == 0:
                        wait(dve, sums_stored[h], i * 16 + n * ITER * 16)
                    op = dve.scalar_tensor_tensor(out=R[:, h, j, 0:w], in0=before, scalar=kp[:, h, j:j + 1],
                                                  in1=msg[:, j, :], op0=ALU.mult, op1=ALU.add)
                op.then_inc(sums_ready[h], 1)

            def keep_of(h, i):
                dve.tensor_copy(kp[:, h, :], keep[:, bass.ds(i * (2 * U) + U * h, U)])

            def node_sums(n, w):
                shape = [P, TILES, w]

                def open_nodes(g):
                    k = n * GROUPS + g
                    if g >= 2:
                        dve.wait_ge(product, at["mm"] - 1)
                    dve.tensor_scalar(OH[:, g % 2, :], C[0:CH, C_IOTA:C_IOTA + GRP * P], lastg[:, g:g + 1],
                                      open_c[:, 0:1], ALU.is_equal, ALU.mult).then_inc(open_ready, 1)
                dve.drain()
                open_nodes(0)
                dve.wait_ge(ends_landed, 16 * TILES * (n + 1))
                dve.tensor_tensor(AGG[:, :, 0:w], AGG[:, :, 0:w], has_in[:, :].unsqueeze(2).to_broadcast(shape),
                                  ALU.mult)
                dve.drain()
                for g in range(GROUPS):
                    if g + 1 < GROUPS:
                        open_nodes(g + 1)
                    dve.wait_ge(product, at["mm"] + 1)
                    n_t = min(GRP, TILES - GRP * g)
                    to = AGG[:, GRP * g:GRP * g + n_t, 0:w]
                    dve.tensor_tensor(to, to, p_mm[at["mm"] % 2][:, 0:n_t * w].rearrange("p (t f) -> p t f", t=n_t),
                                      ALU.add).then_inc(product_used, 1)
                    at["mm"] += 1
                dve.drain()

            def gcn(n, bias_name):
                dense([T])
                at["table"] += 1
                dve.tensor_tensor(T[:, :, :], T[:, :, :], per_node(dinv[:, :]), ALU.mult).then_inc(table_ready, 1)

                def body(i):
                    for h in (0, 1):
                        dve.wait_ge(rows_landed[n][h], (i + 1) * (16 * U))
                        keep_of(h, i)
                        running_sums(n, h, i, G[0:CH, h, :, 0:D], D)
                        dve.drain()
                        dve.sem_inc(rows_used[h], 1)
                turns(dve, body, n)
                node_sums(n, D)
                agg = AGG[:, :, 0:D]
                dve.tensor_tensor(agg, agg, T[:, :, :], ALU.add)
                dve.drain()
                dve.tensor_tensor(agg, agg, per_node(dinv[:, :]), ALU.mult)
                dve.drain()
                dve.tensor_tensor(agg, agg, per_feature(bias_name), ALU.add)
                dve.drain()

            def add_to_x(of):
                dve.tensor_tensor(X[:, :, :], X[:, :, :], of, ALU.add)
                dve.drain()

            agg = AGG[:, :, 0:D]
            dve.memset(R[:, :, :, :], 0.0)
            norm(H, X, T, lambda: relu_nodes(H))
            dense([T])
            dve.tensor_tensor(T[:, :, :], T[:, :, :], per_feature("L0_gnn_b_in"), ALU.add)
            dve.drain()
            dve.tensor_scalar(H[:, :, :], T[:, :, :], 0.0, None, ALU.max).then_inc(nodes_ready, 1)
            for n in range(3):
                gcn(n, str(n))
                dve.scalar_tensor_tensor(out=H[:, :, :], in0=agg, scalar=0.0, in1=H[:, :, :], op0=ALU.max,
                                         op1=ALU.add).then_inc(nodes_ready, 1)
            dense([T])
            dve.tensor_tensor(T[:, :, :], T[:, :, :], per_feature("L0_gnn_b_out"), ALU.add)
            dve.drain()
            add_to_x(T[:, :, :])
            norm(H, X, T, lambda: relu_nodes(H))
            gcn(3, "L1_gnn_b1")
            dve.tensor_scalar(T[:, :, :], agg, 0.0, sc[:, 0:1], ALU.min, ALU.mult)
            dve.drain()
            dve.scalar_tensor_tensor(out=H[:, :, :], in0=agg, scalar=0.0, in1=T[:, :, :], op0=ALU.max,
                                     op1=ALU.add).then_inc(nodes_ready, 1)
            gcn(4, "L1_gnn_b2")
            add_to_x(agg)
            norm(H, X, T, lambda: relu_nodes(H))
            dense([T, V])
            dve.tensor_tensor(T[:, :, :], T[:, :, :], per_feature("L2_gnn_mb1"), ALU.add)
            dve.tensor_tensor(V[:, :, :], V[:, :, :], per_feature("L2_gnn_gb1"), ALU.add).then_inc(table_ready, 6 - 5)
            dve.drain()

            def gated(i):
                n = PASS_L2
                for h in (0, 1):
                    keep_of(h, i)
                    dve.wait_ge(rows_landed[n][h], (i + 1) * (16 * U))
                    for g in range(U // EG):
                        dve.wait_ge(edge_product, i * (2 * U // EG) + (h * U // EG + g + 1))
                        for c in (0, 1):
                            rows = G[0:CH, h, EG * g + 2 * c:EG * g + 2 * c + 2, 0:2 * D]
                            add = dve.tensor_tensor(
                                rows, rows, p_e[2 * (g % 2) + c][0:CH, 0:4 * D].rearrange("p (a f) -> p a f", a=2),
                                ALU.add)
                        add.then_inc(edge_added, 1)
                    dve.wait_ge(gelu_done, i * 2 + (1 + h))
                    dve.tensor_tensor(M[:, :, 0:D], A[0:CH, h, :, D:2 * D],
                                      gw2[0:CH, :].unsqueeze(1).to_broadcast([CH, U, D]), ALU.mult)
                    dve.drain()
                    dve.tensor_reduce(small[:, 0, 0:U], M[:, :, 0:D], AX_X, ALU.add).then_inc(logit_ready, 1)
                    dve.wait_ge(gate_ready, i * 2 + (1 + h))
                    dve.tensor_tensor(M[:, :, 0:D], A[0:CH, h, :, 0:D],
                                      small[:, 1, 0:U].unsqueeze(2).to_broadcast([CH, U, D]), ALU.mult)
                    dve.tensor_copy(M[:, :, D:MW], small[:, 1, 0:U].unsqueeze(2))
                    running_sums(n, h, i, M[:, :, 0:MW], MW)
            turns(dve, gated, PASS_L2)
            node_sums(PASS_L2, MW)
            dense([V], ready=True)
            dve.tensor_tensor(T[:, :, :], per_node(AGG[:, :, D:MW].rearrange("p t f -> p (t f)")),
                              per_feature("L2_gnn_mb2"), ALU.mult)
            dve.drain()
            dve.tensor_tensor(V[:, :, :], V[:, :, :], T[:, :, :], ALU.add)
            dve.drain()
            dense([T], ready=True)
            dense([AGG], ready=True)
            dve.tensor_tensor(T[:, :, :], T[:, :, :], agg, ALU.add)
            dve.drain()
            dve.tensor_tensor(T[:, :, :], T[:, :, :], per_feature("L2_gnn_ub1"), ALU.add).then_inc(gelu_wanted, 1)
            dve.wait_ge(gelu_nodes, 1)
            dense([V], ready=True)
            dve.tensor_tensor(V[:, :, :], V[:, :, :], H[:, :, :], ALU.add)
            dve.drain()
            dve.tensor_tensor(V[:, :, :], V[:, :, :], per_feature("L2_gnn_ub2"), ALU.add)
            dve.drain()

            def scale_shift():
                dve.tensor_tensor(H[:, :, :], H[:, :, :], per_feature("L2_gnn_ln_g"), ALU.mult)
                dve.drain()
                dve.tensor_tensor(H[:, :, :], H[:, :, :], per_feature("L2_gnn_ln_b"), ALU.add)
                dve.drain()
            norm(H, V, T, scale_shift)
            add_to_x(H[:, :, :])
            norm(H, X, T, lambda: relu_nodes(H))
            dense([T, V, AGG])
            dve.sem_inc(table_ready, 1)
            dve.wait_ge(table_stored, 16 * 10)

            def attend(i):
                n = PASS_L3
                for h in (0, 1):
                    dve.wait_ge(idx_landed[h], i * 32 + (n * ITER * 16 + 32))
                    dve.wait_ge(srow_landed[h], i * 16 + 16)
                    wait(dve, comb_ready, i * 2 + (h - 1) if not isinstance(i, int) or i > 0 else 0)
                    for a in range(ACCS):
                        steps = len(range(a, U, ACCS))
                        wait(dve, scattered[a], i * (32 * steps) + 16 * steps * (h - 1)
                             if not isinstance(i, int) or i > 0 else 0)
                    dve.tensor_tensor(same[h], srow[:, h, :, :], si[h][:, :].unsqueeze(2).to_broadcast([CH, U, CH]),
                                      ALU.is_equal)
                    dve.drain()
                    dve.tensor_tensor(stmp, same[h],
                                      C[0:CH, C_BEFORE:C_BEFORE + CH].unsqueeze(1).to_broadcast([CH, U, CH]), ALU.mult)
                    dve.drain()
                    dve.tensor_reduce(small[:, 2, 0:U], stmp, AX_X, ALU.max)
                    dve.tensor_scalar(small[:, 3, 0:U], si[h][:, :], C[0:CH, C_TRASH:C_TRASH + 1], -1.0, ALU.subtract,
                                      ALU.mult)
                    dve.drain()
                    dve.tensor_tensor(small[:, 2, 0:U], small[:, 2, 0:U], small[:, 3, 0:U], ALU.mult)
                    dve.drain()
                    dve.tensor_tensor(ai[h][:, :], small[:, 2, 0:U], si[h][:, :], ALU.add).then_inc(targets_ready, 1)
                    dve.wait_ge(rows_landed[n][h], (i + 1) * (32 * U))
                    wait(dve, combined, i * 2 + h)
                    q, k, v = (G[0:CH, h, :, c * D:(c + 1) * D] for c in range(3))
                    dve.tensor_tensor(M[:, :, 0:D], q, k, ALU.mult)
                    dve.drain()
                    dve.tensor_reduce(small[:, 0, :].rearrange("p (u e) -> p u e", u=U),
                                      M[:, :, 0:D].rearrange("p u (e f) -> p u e f", e=HEADS), AX_X, ALU.add)
                    dve.drain()
                    dve.tensor_scalar(small[:, 1, :], small[:, 0, :], 10.0, -10.0, ALU.min,
                                      ALU.max).then_inc(score_ready, 1)
                    dve.wait_ge(exp_ready, i * 2 + (1 + h))
                    dve.tensor_tensor(M[:, :, 0:D].rearrange("p u (e f) -> p u e f", e=HEADS),
                                      v.rearrange("p u (e f) -> p u e f", e=HEADS),
                                      M[:, :, D:AW].unsqueeze(3).to_broadcast([CH, U, HEADS, DH]),
                                      ALU.mult).then_inc(msg_ready, 1)
                    dve.wait_ge(msg_ready, i * 2 + (1 + h))
                    dve.sem_inc(rows_used[h], 1)
            turns(dve, attend, PASS_L3)
            dve.wait_ge(acc_landed, 16 * ACCS)
            total = AGG[:, :, :].rearrange("p t f -> p (t f)")
            for part in (g_flat, a_flat):
                dve.tensor_tensor(total, total, part[:, 0:TILES * AW], ALU.add)
                dve.drain()
            weights_sum = AGG[:, :, D:AW]
            dve.tensor_scalar(weights_sum, weights_sum, 1e-8, None, ALU.add)
            dve.drain()
            dve.reciprocal(weights_sum, weights_sum)
            dve.drain()
            for e in range(HEADS):
                part = AGG[:, :, e * DH:(e + 1) * DH]
                dve.tensor_tensor(part, part, AGG[:, :, D + e:D + e + 1].to_broadcast([P, TILES, DH]), ALU.mult)
            dve.drain()
            add_to_x(H[:, :, :])
            dve.tensor_tensor(X[:, :, :], X[:, :, :], agg, ALU.add).then_inc(out_ready, 1)


def kernel(**inputs):
    import concourse.bacc as _bacc
    from concourse.bass_utils import run_bass_kernel_spmd as _run

    a = {k: np.asarray(v) for k, v in inputs.items()}
    w = {
        "W_in_T": a["L0_gnn_W_in"].T, "W_out_T": a["L0_gnn_W_out"].T,
        "mW1_x": a["L2_gnn_mW1"][:D], "gW1_x": a["L2_gnn_gW1"][:D],
        "uW1_x": a["L2_gnn_uW1"][:D], "uW1_a": a["L2_gnn_uW1"][D:],
        **{f"gcn_T{n}": a["L0_gnn_gcn_W"][n].T for n in range(3)},
    }
    arrays = {
        "x": a["x"], "src": a["src"], "dst": a["dst"],
        "src_rows": a["src"].reshape(CH, STEPS).T,
        "edge_t": a["edge_attr_32"].reshape(CH, STEPS // EG, EG, ED).transpose(2, 3, 1, 0).reshape(P, STEPS // EG, CH),
        "consts": shape_constants(),
        "weights": np.stack([w[k] if k in w else a[k] for k in WEIGHTS]),
        "bias": np.stack([a[k] for k in BIASES]),
        "gcn_b": a["L0_gnn_gcn_b"],
        "scalars": np.concatenate([a["L1_gnn_a1"], a["L2_gnn_gb2"]]),
        "gate_w": a["L2_gnn_gW2"].reshape(D),
        "mg_edge": np.stack([a["L2_gnn_mW1"][D:], a["L2_gnn_gW1"][D:]], axis=1),
    }
    nc = _bacc.Bacc("TRN2", target_bir_lowering=False, num_devices=1)
    feed, args = {}, []
    for name, v in arrays.items():
        v = np.ascontiguousarray(v)
        feed[f"in_{name}"] = v
        args.append(nc.dram_tensor(f"in_{name}", v.shape, mybir.dt.from_np(v.dtype), kind="ExternalInput").ap())
    args.append(nc.dram_tensor("out_x", (N, D), F32, kind="ExternalOutput").ap())
    build(nc, *args)
    r = _run(nc, [feed], core_ids=[0])
    return r.results[0]["out_x"]
```

```python
from contextlib import ExitStack

import numpy as np

import concourse.bass as bass
from concourse import mybir

F32 = mybir.dt.float32
BF16 = mybir.dt.bfloat16
I32 = mybir.dt.int32
ALU = mybir.AluOpType
ACT = mybir.ActivationFunctionType
AX_X = mybir.AxisListType.X

N = 6250
E = 200000
D = 96
ED = 32
HEADS = 4
DH = D // HEADS
P = 128
TILES = -(-N // P)
NPAD = TILES * P
FULL = N // P
REST = N - FULL * P
GRP = 4
GROUPS = -(-TILES // GRP)

CH = 125
STEPS = E // CH
U = 16
ITER = STEPS // (2 * U)
assert CH * STEPS == E and ITER * 2 * U == STEPS

EG = 4
BANKS = 8
assert U == 2 * BANKS
MW = D + 1
AW = D + HEADS
ACCS = 3
TRASH = P
AROWS = 50 * P
assert AROWS >= N + TRASH
LAGS = 64
LCOLS = 320
SHI, SLO, DHI = 7, 13, 20
NO_ENTRY = 28
PARTS = 3
HALF = (TILES + 1) // 2
GW = 3 * D

BIASES = ["L0_gnn_b_in", "L0_gnn_b_out", "L1_gnn_b1", "L1_gnn_b2", "L2_gnn_mb1", "L2_gnn_gb1", "L2_gnn_mb2",
          "L2_gnn_ub1", "L2_gnn_ub2", "L2_gnn_ln_g", "L2_gnn_ln_b"]
WEIGHTS = ["W_in_T", "gcn_T0", "gcn_T1", "gcn_T2", "W_out_T", "L1_gnn_W1", "L1_gnn_W2", "mW1_x", "gW1_x",
           "L2_gnn_mW2", "uW1_x", "uW1_a", "L2_gnn_uW2", "L3_gnn_qW", "L3_gnn_kW", "L3_gnn_vW"]

C_ID, C_TRI, C_IOTA = 0, P, 2 * P
C_BEFORE = C_IOTA + GRP * P
C_TRASH = C_BEFORE + P
C_GRP = C_TRASH + 1
C_W = C_GRP + GROUPS

CONVS = 5
GATE, ATTEND = CONVS, CONVS + 1
FILL_W = STEPS // ITER * 2 * D


def shape_constants():
    c = np.zeros((P, C_W), np.float32)
    c[:, C_ID:C_ID + P] = np.eye(P)
    c[:, C_TRI:C_TRI + P] = np.triu(np.ones((P, P)))
    c[:, C_IOTA:C_IOTA + GRP * P] = np.arange(GRP * P)
    c[:, C_BEFORE:C_BEFORE + P] = np.tril(np.ones((P, P)), -1)
    c[:, C_TRASH] = N + np.arange(P)
    c[:, C_GRP:C_GRP + GROUPS] = np.arange(GROUPS) * GRP * P
    return c


def build(nc, x, src, dst, src_rows, dst_rows, edge_t, consts, weights, bias, gcn_b, scalars, gate_w, mg_edge, out):
    def dram(name, shape, dt=F32):
        return nc.dram_tensor(name, shape, dt, kind="Internal").ap()

    table = dram("table", (NPAD, D))
    table_mg = dram("table_mg", (NPAD, 2 * D))
    table_q = dram("table_q", (NPAD, D))
    table_kv = dram("table_kv", (NPAD, 2 * D))
    run_m = dram("run_m", (E, MW))
    fill_kv = dram("fill_kv", (2 * E, D))
    adj = dram("adj", (TILES << DHI, 1), BF16)
    adj_v = adj.rearrange("(d p s n) o -> d p (s n o)", d=TILES, p=P, n=P)
    acc_d = [dram(f"acc{a}", (AROWS, AW)) for a in range(ACCS)]

    def by_chunk(ap):
        return ap.rearrange("(p s) f -> p s f", p=CH)

    def by_tile(ap):
        return ap.rearrange("(t p) f -> p t f", p=P)

    with ExitStack() as ctx:
        def sb(name, shape, dt=F32):
            return ctx.enter_context(nc.sbuf_tensor(name, shape, dt))

        def ps(name, shape, dt=F32):
            return ctx.enter_context(nc.psum_tensor(name, shape, dt))

        def sem(name):
            return ctx.enter_context(nc.semaphore(name))

        X = sb("X", [P, TILES, D])
        H = sb("H", [P, TILES, D])
        T = sb("T", [P, TILES, D])
        V = sb("V", [P, TILES, D])
        AGG = sb("AGG", [P, TILES, AW])
        G = sb("G", [P, 2, U, GW])
        A = sb("A", [P, 2, U, 2 * D])
        R = sb("R", [CH, 2, U, AW])
        M = sb("M", [CH, U, AW])
        EA = sb("EA", [P, 2, EG, CH])
        keep = sb("keep", [CH, STEPS])
        kp = sb("kp", [CH, 2, U])
        si = [sb(f"si{h}", [CH, U], I32) for h in (0, 1)]
        di = [sb(f"di{h}", [CH, U], I32) for h in (0, 1)]
        ai = [sb(f"ai{h}", [CH, U], I32) for h in (0, 1)]
        vi = [sb(f"vi{h}", [CH, U], BF16) for h in (0, 1)]
        cont = sb("cont", [CH, 1])
        heads = sb("heads", [CH, 1], I32)
        flags = sb("flags", [CH, 4])
        flag = sb("flag", [P, 1], I32)
        starts = sb("starts", [P, 2, TILES], I32)
        small = sb("small", [CH, 4, U * HEADS])
        C = sb("C", [P, C_W])
        W = sb("W", [D, len(WEIGHTS), D])
        B = sb("B", [P, len(BIASES) + 3, D])
        gw2 = sb("gw2", [P, D])
        sc = sb("sc", [P, 2])
        BD = sb("BD", [P, EG, 2, D])
        hT = sb("hT", [D, 2, GRP * P])
        deg = sb("deg", [P, TILES])
        dinv = sb("dinv", [P, TILES])
        has_in = sb("has_in", [P, TILES])
        ends = sb("ends", [P, TILES], I32)
        st = sb("st", [P, 5, TILES])
        lastg = sb("lastg", [CH, GROUPS])
        open_c = sb("open_c", [CH, 1])
        nxt = sb("nxt", [CH, 1], I32)

        scratch = AGG[:, :, :].rearrange("p t f -> p (t f)")
        dst_i = scratch[0:CH, 0:STEPS].bitcast(I32)
        dst_hi = scratch[0:CH, STEPS:2 * STEPS]
        dst_lo = scratch[0:CH, 2 * STEPS:3 * STEPS]
        OH = M[:, :, :].rearrange("p u f -> p (u f)")[:, 0:2 * GRP * P].rearrange("p (k n) -> p k n", k=2)
        g_flat = G[:, :, :, :].rearrange("p h u f -> p (h u f)")
        a_flat = A[:, :, :, :].rearrange("p h u f -> p (h u f)")
        lo_bits = [a_flat[0:CH, h * U * P // 2:(h + 1) * U * P // 2].bitcast(BF16).rearrange("p (u f) -> p u f", u=U)
                   for h in (0, 1)]
        hi_bits = [g_flat[0:CH, h * 1024:h * 1024 + U * 64 // 2].bitcast(BF16).rearrange("p (u f) -> p u f", u=U)
                   for h in (0, 1)]
        h_flat = H[:, :, :].rearrange("p t f -> p (t f)")
        v_flat = V[:, :, :].rearrange("p t f -> p (t f)")
        wide = STEPS + 2 * LAGS
        key_s = h_flat[0:CH, 0:wide].bitcast(I32)
        key_d = h_flat[0:CH, wide:2 * wide].bitcast(I32)
        x_b = v_flat[0:CH, 0:LCOLS].bitcast(I32)
        x_a = v_flat[0:CH, LCOLS:2 * LCOLS].bitcast(I32)
        cnt_b = v_flat[0:CH, 2 * LCOLS:3 * LCOLS]
        cnt_a = v_flat[0:CH, 3 * LCOLS:4 * LCOLS]
        r_flat = R[:, :, :, :].rearrange("p h u f -> p (h u f)")
        entry = r_flat[:, 0:STEPS].bitcast(I32)
        count_v = r_flat[:, STEPS:STEPS + STEPS // 2].bitcast(BF16)
        zeros_bf = a_flat[:, 0:TILES * P // 2].bitcast(BF16)
        parts = g_flat[:, 0:TILES * PARTS * D // 2].bitcast(BF16).rearrange("p (t k f) -> p t k f", t=TILES, k=PARTS)
        blk = [b[:, 0:TILES * P // 2].bitcast(BF16) for b in (a_flat, v_flat)]
        same = [a_flat[0:CH, h * U * P:h * U * P + U * CH].rearrange("p (u j) -> p u j", u=U) for h in (0, 1)]
        krow = V[:, :, :].rearrange("p t f -> p (t f)")[0:CH, 0:2 * U * CH].bitcast(I32).rearrange(
            "p (h u j) -> p h u j", h=2, u=U)
        stmp = scratch[0:CH, 0:U * CH].rearrange("p (u j) -> p u j", u=U)
        carry = a_flat[0:CH, 2 * U * P:2 * U * P + 2 * D]
        fill_zeros = g_flat[0:CH, 2304:2304 + FILL_W]
        gmg = [G[0:CH, h, :, 0:2 * D] for h in (0, 1)]

        p_tr = [ps(f"p_tr{k}", [P, 512]) for k in (0, 1)]
        p_mm = [ps(f"p_mm{k}", [P, 512]) for k in (0, 1)]
        p_c = [*p_tr, *p_mm]
        p_e = [ps(f"p_e{k}", [P, 512]) for k in range(4)]
        p_h = [*p_e, *p_tr, *p_mm]

        inputs_landed = sem("inputs_landed")
        keys_cleared = sem("keys_cleared")
        keys_landed = sem("keys_landed")
        flags_ready = sem("flags_ready")
        flags_summed = sem("flags_summed")
        flag_ready = sem("flag_ready")
        cleared = sem("cleared")
        adj_cleared = sem("adj_cleared")
        fill_cleared = sem("fill_cleared")
        zeros_wanted = sem("zeros_wanted")
        zeros_landed = sem("zeros_landed")
        bd_cleared = sem("bd_cleared")
        entries_ready = sem("entries_ready")
        entry_landed = [sem(f"entry_landed{h}") for h in (0, 1)]
        entry_stored = [sem(f"entry_stored{h}") for h in (0, 1)]
        block_landed = [[sem(f"block_landed{b}_{c}") for c in (0, 1)] for b in (0, 1)]
        block_used = sem("block_used")
        parts_ready = sem("parts_ready")
        adj_used = sem("adj_used")
        onehot_ready = sem("onehot_ready")
        onehot_used = sem("onehot_used")
        deg_ready = sem("deg_ready")
        cum_ready = sem("cum_ready")
        root_wanted = sem("root_wanted")
        root_ready = sem("root_ready")
        nodes_ready = sem("nodes_ready")
        turned = sem("turned")
        hT_ready = sem("hT_ready")
        product = sem("product")
        product_used = sem("product_used")
        table_ready = sem("table_ready")
        table_stored = sem("table_stored")
        idx_landed = [sem(f"idx_landed{h}") for h in (0, 1)]
        rows_landed = [sem(f"rows_landed{h}") for h in (0, 1)]
        hidden_ready = sem("hidden_ready")
        sums_ready = [sem(f"sums_ready{h}") for h in (0, 1)]
        sums_stored = [sem(f"sums_stored{h}") for h in (0, 1)]
        ends_landed = sem("ends_landed")
        open_ready = sem("open_ready")
        edge_landed = [sem(f"edge_landed{h}") for h in (0, 1)]
        edge_product = sem("edge_product")
        edge_added = sem("edge_added")
        gelu_done = sem("gelu_done")
        logit_ready = sem("logit_ready")
        gate_ready = sem("gate_ready")
        gelu_wanted = sem("gelu_wanted")
        gelu_nodes = sem("gelu_nodes")
        lists_landed = [sem(f"lists_landed{h}") for h in (0, 1)]
        gathered = [[sem(f"gathered{n}_{h}") for h in (0, 1)] for n in range(ATTEND + 1)]
        gathered_used = [sem(f"gathered_used{h}") for h in (0, 1)]
        krow_landed = [sem(f"krow_landed{h}") for h in (0, 1)]
        fill_landed = [sem(f"fill_landed{h}") for h in (0, 1)]
        heads_landed = sem("heads_landed")
        nodes_spread = sem("nodes_spread")
        targets_ready = sem("targets_ready")
        score_ready = sem("score_ready")
        exp_ready = sem("exp_ready")
        msg_ready = sem("msg_ready")
        combined = sem("combined")
        comb_ready = sem("comb_ready")
        scattered = [[sem(f"scattered{n}_{a}") for a in range(ACCS)] for n in range(ATTEND + 1)]
        acc_landed = sem("acc_landed")
        out_ready = sem("out_ready")
        out_stored = sem("out_stored")
        pool_passed = sem("pool_passed")
        sp_passed = sem("sp_passed")

        block = ctx.enter_context(nc.Block())

        def wait(eng, s, v):
            if not isinstance(v, int) or v > 0:
                eng.wait_ge(s, v)

        def first(i):
            return isinstance(i, int) and i == 0

        def turns(eng, body):
            body(0)
            with eng.Fori(1, ITER) as i:
                body(i)

        def tiles(eng, body, n):
            start = n * TILES % 2
            body(0, start)
            body(1, 1 - start)
            with eng.Fori(1, TILES // 2) as i:
                body(i * 2, start)
                body(i * 2 + 1, 1 - start)
            body(TILES - 1, start)

        def passed(eng, s):
            eng.sem_inc(s, 1)

        def both_ways(eng, way):
            eng.wait_ge(flag_ready, 1)
            with eng.If(eng.value_load(flag[0:1, 0:1]) == 0):
                way(True)
            with eng.Else():
                way(False)
            eng.drain()

        def acc_steps(a):
            return len(range(a, U, ACCS))

        def place(n, fast):
            return 0 if fast else n

        def width(n):
            return D if n < CONVS else MW if n == GATE else AW

        def wait_scattered(eng, n, i, h):
            if not first(i):
                for a in range(ACCS):
                    eng.wait_ge(scattered[n][a], i * (32 * acc_steps(a)) + 16 * acc_steps(a) * (h - 1))

        at_batch = lambda i, h: bass.ds(i * (2 * U) + U * h, U)
        src_c, dst_c = (v.rearrange("(p s) -> p s", p=CH) for v in (src, dst))
        n_inputs = 16

        @block.sync
        def _(sp):
            def load(to, of, slow=False):
                sp.dma_start(to, of, allow_slow_non_contiguous=slow).then_inc(inputs_landed, 16)

            sp.wait_ge(keys_cleared, 4)
            for rows, to in ((src_c, key_s), (dst_c, key_d)):
                sp.dma_start(to[:, LAGS:LAGS + STEPS], rows).then_inc(keys_landed, 16)
                sp.dma_start(to[1:CH, 0:LAGS], rows[0:CH - 1, STEPS - LAGS:STEPS]).then_inc(keys_landed, 16)
                sp.dma_start(to[0:CH - 1, LAGS + STEPS:wide], rows[1:CH, 0:LAGS]).then_inc(keys_landed, 16)
            load(C[:, :], consts)
            load(dst_i, dst_c)
            load(nxt[0:CH - 1, :], dst_c[1:CH, 0:1], slow=True)
            load(nxt[CH - 1:CH, :], dst_c[0:1, 0:1], slow=True)
            load(heads[:, :], dst_c[:, 0:1], slow=True)
            load(W[:, :, :], weights.rearrange("n i o -> i n o"))
            load(B[:, 0:len(BIASES), :], bias.unsqueeze(0).to_broadcast((P, len(BIASES), D)))
            load(B[:, len(BIASES):, :], gcn_b.unsqueeze(0).to_broadcast((P, 3, D)))
            load(gw2[:, :], gate_w.unsqueeze(0).to_broadcast((P, D)))
            load(sc[:, :], scalars.unsqueeze(0).to_broadcast((P, 2)))
            sp.wait_ge(bd_cleared, 2)
            for a in range(EG):
                load(BD[a * ED:(a + 1) * ED, a, :, :], mg_edge)
            load(X[:, 0:FULL, :], by_tile(x[0:FULL * P, :]))
            load(X[0:REST, FULL, :], x[FULL * P:N, :])

            def clear_sums():
                for a in range(ACCS):
                    sp.dma_start(acc_d[a].rearrange("(p t) f -> p (t f)", p=P),
                                 g_flat[:, 0:AROWS // P * AW]).then_inc(zeros_landed, 16)
            sp.wait_ge(cleared, 2)
            clear_sums()

            def put_table(k, to, of):
                sp.wait_ge(table_ready, k)
                sp.dma_start(by_tile(to), of).then_inc(table_stored, 16)

            def load_src(h, i, s):
                sp.dma_start(si[h][:, :], src_c[:, at_batch(i, h)]).then_inc(s[h], 16)

            def load_edges(h, i, fast):
                if not first(i):
                    if fast:
                        sp.wait_ge(edge_product, i * 2 + (h - 1))
                    else:
                        sp.wait_ge(edge_added, i * 8 + (4 * h - 4))
                passed(sp, sp_passed)
                sp.dma_start(EA[:, h, :, :], edge_t[:, bass.ds(i * (2 * U // EG) + (U // EG) * h, U // EG), :]
                             ).then_inc(edge_landed[h], 16)

            def sum_pass():
                def body(i, last=False):
                    for h in (0, 1):
                        sp.wait_ge(rows_landed[h], (i + 1) * (16 * U))
                        passed(sp, sp_passed)
                        if not last:
                            load_src(h, i + 1, idx_landed)
                            load_edges(h, i + 1, True)
                        sp.wait_ge(sums_ready[h], i + 1)
                        passed(sp, sp_passed)
                        sp.dma_start(by_chunk(run_m)[:, at_batch(i, h), :], R[:, h, :, 0:MW]
                                     ).then_inc(sums_stored[h], 16)
                for h in (0, 1):
                    load_src(h, 0, idx_landed)
                    load_edges(h, 0, True)
                with sp.Fori(0, ITER - 1) as i:
                    body(i)
                body(ITER - 1, last=True)

            def store_adjacency():
                fill_columns = by_chunk(fill_kv).rearrange("p s f -> p (s f)")

                def put_entries(i):
                    for h in (0, 1):
                        wait(sp, entry_stored[h], i * (16 * U))
                        passed(sp, sp_passed)
                        sp.dma_start(ai[h][:, :], entry[:, at_batch(i, h)]).then_inc(entry_landed[h], 16)
                        sp.dma_start(vi[h][:, :], count_v[:, at_batch(i, h)]).then_inc(entry_landed[h], 16)
                    sp.dma_start(fill_columns[:, bass.ds(i * FILL_W, FILL_W)], fill_zeros).then_inc(fill_cleared, 16)
                per = LCOLS // (2 * U)
                for b in range(STEPS // LCOLS):
                    sp.wait_ge(entries_ready, b + 1)
                    if b == 0:
                        put_entries(0)
                    with sp.Fori(max(b * per, 1), (b + 1) * per) as i:
                        put_entries(i)
                for h in (0, 1):
                    sp.wait_ge(entry_stored[h], 16 * U * ITER)

            def load_blocks(n):
                def block_of(d, b):
                    for c, (lo, hi) in enumerate(((0, HALF), (HALF, TILES))):
                        if not isinstance(d, int) or n or d > 1:
                            sp.wait_ge(block_used, d * 2 + (n * TILES * 2 + c - 3))
                        passed(sp, sp_passed)
                        sp.dma_start(blk[b][:, lo * P:hi * P], adj_v[bass.ds(d, 1), :, lo * P:hi * P].rearrange(
                            "o p f -> (o p) f")).then_inc(block_landed[b][c], 16)
                if n == 0:
                    sp.wait_ge(adj_cleared, 16 * TILES)
                    sp.wait_ge(parts_ready, 1)
                tiles(sp, block_of, n)

            def scatter_pass(n, fast, stored):
                q = place(n, fast)
                key_rows = src_rows if n == ATTEND else dst_rows

                def lists(h, i):
                    load_src(h, i, lists_landed)
                    if not fast:
                        sp.dma_start(di[h][:, :], dst_c[:, at_batch(i, h)]).then_inc(lists_landed[h], 16)
                    sp.dma_start(krow[:, h, :, :], key_rows[at_batch(i, h), :].unsqueeze(0).to_broadcast((CH, U, CH))
                                 ).then_inc(krow_landed[h], 16)
                    if n == GATE:
                        load_edges(h, i, False)

                def fill(h, i):
                    wait(sp, gathered_used[h], i)
                    passed(sp, sp_passed)
                    sp.dma_start(G[0:CH, h, :, D:3 * D], by_chunk(fill_kv.rearrange("(e c) f -> e (c f)", c=2))[:, at_batch(i, h), :]
                                 ).then_inc(fill_landed[h], 16)

                sp.wait_ge(table_stored, 16 * stored)
                if fast:
                    sp.wait_ge(nodes_spread, 16 * 2 * TILES)
                if q:
                    sp.wait_ge(zeros_wanted, q)
                    clear_sums()
                lists(0, 0)
                lists(1, 0)
                if fast:
                    fill(0, 0)
                    fill(1, 0)

                def body(i):
                    for h in (0, 1):
                        sp.wait_ge(gathered[n][h], (i + 1) * (16 * U * (2 if n == ATTEND and not fast else 1)))
                        passed(sp, sp_passed)
                        sp.wait_ge(targets_ready, i * 2 + (1 + h + q * 2 * ITER))
                        passed(sp, sp_passed)
                        for a in range(ACCS):
                            wait(sp, scattered[n][a], i * (32 * acc_steps(a)) + 16 * acc_steps(a) * h)
                            passed(sp, sp_passed)
                        lists(h, i + 1)
                        if fast:
                            fill(h, i + 1)
                body(0)
                with sp.Fori(1, ITER - 1) as i:
                    body(i)
                for a in range(ACCS):
                    sp.wait_ge(scattered[n][a], 16 * acc_steps(a) * 2 * ITER)
                sp.wait_ge(comb_ready, 2 * ITER * (q + 1))
                for a, to in enumerate((scratch, g_flat, a_flat)):
                    sp.dma_start(to[:, 0:TILES * AW].rearrange("p (t f) -> p t f", t=TILES),
                                 by_tile(acc_d[a][0:NPAD, :])).then_inc(acc_landed, 16)

            def way(fast):
                if fast:
                    store_adjacency()
                for n in range(CONVS):
                    if fast:
                        load_blocks(n)
                    else:
                        put_table(n + 1, table, T[:, :, :])
                        scatter_pass(n, fast, n + 1)
                k, stored = (1, 0) if fast else (CONVS + 1, CONVS)
                put_table(k, table_mg[:, 0:D], T[:, :, :])
                put_table(k, table_mg[:, D:2 * D], V[:, :, :])
                if fast:
                    sum_pass()
                else:
                    scatter_pass(GATE, fast, stored + 2)
                put_table(k + 1, table_q, T[:, :, :])
                put_table(k + 1, table_kv[:, 0:D], V[:, :, :])
                put_table(k + 1, table_kv[:, D:2 * D], AGG[:, :, 0:D])
                scatter_pass(ATTEND, fast, stored + 5)
                sp.wait_ge(out_ready, 1)
                sp.dma_start(by_tile(out[0:FULL * P, :]), X[:, 0:FULL, :]).then_inc(out_stored, 16)
                sp.dma_start(out[FULL * P:N, :], X[0:REST, FULL, :]).then_inc(out_stored, 16)
                sp.wait_ge(out_stored, 32)
            both_ways(sp, way)

        @block.gpsimd
        def _(pool):
            pool.memset(g_flat, 0.0).then_inc(cleared, 1)
            pool.memset(a_flat[:, 0:TILES * P // 2], 0.0).then_inc(cleared, 1)

            def gather(to, of, at, s):
                pool.indirect_dma_start(out=to, out_offset=None, in_=of,
                                        in_offset=bass.IndirectOffsetOnAxis(ap=at, axis=0)).then_inc(s, 16)

            def scatter_some(to, of, at, last, s):
                pool.indirect_dma_start(out=to, out_offset=bass.IndirectOffsetOnAxis(ap=at, axis=0), in_=of,
                                        in_offset=None, bounds_check=last, oob_is_err=False).then_inc(s, 16)

            def sum_pass():
                def body(i):
                    for h in (0, 1):
                        if not first(i):
                            pool.wait_ge(hidden_ready, i * (2 * BANKS) + (BANKS * (h - 1)))
                        pool.wait_ge(idx_landed[h], i * 16 + 16)
                        passed(pool, pool_passed)
                        for j in range(U):
                            gather(G[0:CH, h, j, 0:2 * D], table_mg, si[h][:, j:j + 1], rows_landed[h])
                pool.wait_ge(table_stored, 16 * 2)
                turns(pool, body)
                for h in (0, 1):
                    pool.wait_ge(sums_stored[h], 16 * ITER)
                for t in range(TILES):
                    gather(AGG[:, t, 0:MW], run_m, ends[:, t:t + 1], ends_landed)

            def store_adjacency():
                pool.wait_ge(adj_cleared, 16 * TILES)
                with pool.Fori(0, ITER) as i:
                    for h in (0, 1):
                        pool.wait_ge(entry_landed[h], i * 32 + 32)
                        passed(pool, pool_passed)
                        for j in range(U):
                            scatter_some(adj, vi[h][:, j:j + 1], ai[h][:, j:j + 1], (TILES << DHI) - 1,
                                         entry_stored[h])

            def scatter_pass(n, fast, stored):
                q = place(n, fast)

                def gathers(h, i):
                    if not first(i):
                        pool.wait_ge(gathered_used[h], i + q * ITER)
                    pool.wait_ge(lists_landed[h], (i + (q * ITER + 1)) * (16 if fast else 32))
                    passed(pool, pool_passed)
                    of = table if n < CONVS else table_mg if n == GATE else table_q
                    for j in range(U):
                        gather(G[0:CH, h, j, 0:of.shape[1]], of, si[h][:, j:j + 1], gathered[n][h])
                        if n == ATTEND and not fast:
                            gather(G[0:CH, h, j, D:3 * D], table_kv, di[h][:, j:j + 1], gathered[n][h])

                def scatters(h, i):
                    pool.wait_ge(comb_ready, i * 2 + (1 + h + q * 2 * ITER))
                    passed(pool, pool_passed)
                    for j in range(U):
                        a = j % ACCS
                        before = i * (32 * acc_steps(a)) + 16 * (h * acc_steps(a) + j // ACCS)
                        if not isinstance(before, int) or before > 0:
                            pool.wait_ge(scattered[n][a], before)
                            passed(pool, pool_passed)
                        pool.indirect_dma_start(out=acc_d[a],
                                                out_offset=bass.IndirectOffsetOnAxis(ap=ai[h][:, j:j + 1], axis=0),
                                                in_=R[:, h, j, :], in_offset=None,
                                                compute_op=ALU.add).then_inc(scattered[n][a], 16)

                pool.wait_ge(table_stored, 16 * stored)
                pool.wait_ge(zeros_landed, 16 * ACCS * (q + 1))
                if fast:
                    pool.wait_ge(fill_cleared, 16 * ITER)
                    for t in range(TILES):
                        for c, of in enumerate((V, AGG)):
                            scatter_some(fill_kv, of[:, t, 0:D], starts[:, c, t:t + 1], 2 * E - 1, nodes_spread)
                    gather(carry, table_kv, heads[:, 0:1], heads_landed)
                gathers(0, 0)
                gathers(1, 0)
                scatters(0, 0)
                with pool.Fori(1, ITER) as i:
                    gathers(0, i)
                    scatters(1, i + (-1))
                    gathers(1, i)
                    scatters(0, i)
                scatters(1, ITER - 1)

            def way(fast):
                if fast:
                    store_adjacency()
                    sum_pass()
                    scatter_pass(ATTEND, fast, 5)
                else:
                    for n in range(CONVS):
                        scatter_pass(n, fast, n + 1)
                    scatter_pass(GATE, fast, CONVS + 2)
                    scatter_pass(ATTEND, fast, CONVS + 5)
            both_ways(pool, way)

        @block.tensor
        def _(pe):
            pe.wait_ge(inputs_landed, 16 * n_inputs)
            ident = C[:, C_ID:C_ID + P]
            pe.wait_ge(flags_ready, 1)
            pe.matmul(p_mm[0][:, 0:1], C[0:CH, C_TRI + P - 1:C_TRI + P].to_broadcast((CH, P)), flags[:, 2:3],
                      start=True, stop=True).then_inc(flags_summed, 1)
            at = {}

            def degrees():
                counts = p_e[0][:, 0:TILES]

                def count(i, h, first=False, last=False):
                    pe.wait_ge(onehot_ready, i * 2 + (1 + h))
                    for j in range(U):
                        mm = pe.matmul(counts, lo_bits[h][:, j, :], hi_bits[h][:, j, 0:TILES],
                                       start=first and j == 0, stop=last and j == U - 1)
                    mm.then_inc(onehot_used, 1)
                count(0, 0, first=True)
                count(0, 1)
                with pe.Fori(1, ITER - 1) as i:
                    count(i, 0)
                    count(i, 1)
                count(ITER - 1, 0)
                count(ITER - 1, 1, last=True)
                pe.wait_ge(deg_ready, 1)
                pe.matmul(p_mm[0][:, 0:TILES], C[:, C_TRI:C_TRI + P], deg[:, :], start=True, stop=True)
                pe.matmul(p_mm[1][:, 0:TILES], C[:, C_TRI + P - 1:C_TRI + P].to_broadcast((P, P)), deg[:, :],
                          start=True, stop=True).then_inc(cum_ready, 1)

            def dense(h_in, ws):
                at["stage"] += 1
                pe.wait_ge(nodes_ready, at["stage"])

                def turn(g):
                    k = at["turn"] + g
                    wait(pe, hT_ready, k - 1)
                    for t in range(GRP * g, min(GRP * g + GRP, TILES)):
                        o = (t - GRP * g) * P
                        mm = pe.transpose(p_tr[k % 2][0:D, o:o + P], h_in[:, t, 0:D], ident)
                    mm.then_inc(turned, 1)
                turn(0)
                for g in range(GROUPS):
                    if g + 1 < GROUPS:
                        turn(g + 1)
                    k = at["turn"] + g
                    pe.wait_ge(hT_ready, k + 1)
                    for w in ws:
                        wait(pe, product_used, at["mm"] - 1)
                        for t in range(GRP * g, min(GRP * g + GRP, TILES)):
                            o = t - GRP * g
                            mm = pe.matmul(p_mm[at["mm"] % 2][:, o * D:(o + 1) * D],
                                           hT[:, k % 2, o * P:(o + 1) * P], W[:, WEIGHTS.index(w), :],
                                           start=True, stop=True)
                        mm.then_inc(product, 1)
                        at["mm"] += 1
                at["turn"] += GROUPS

            def close():
                for g in range(GROUPS):
                    pe.wait_ge(open_ready, g + 1)
                    wait(pe, product_used, at["mm"] - 1)
                    for t in range(GRP * g, min(GRP * g + GRP, TILES)):
                        o = t - GRP * g
                        mm = pe.matmul(p_mm[at["mm"] % 2][:, o * MW:(o + 1) * MW], OH[:, g % 2, o * P:(o + 1) * P],
                                       R[:, 1, U - 1, 0:MW], start=True, stop=True)
                    mm.then_inc(product, 1)
                    at["mm"] += 1

            def adjacency(n):
                pe.wait_ge(parts_ready, n + 1)

                def tile(d, b):
                    if not isinstance(d, int) or n or d > 1:
                        pe.wait_ge(adj_used, d + (n * TILES - 1))
                    before = (n * TILES + 1 - b) // 2
                    start = (b - n * TILES) % 2
                    landed = ((before + (d - start) // 2 + 1) * 16 if isinstance(d, int) else
                              (d - start) * 8 + (before + 1) * 16)
                    for c, (lo, hi) in enumerate(((0, HALF), (HALF, TILES))):
                        pe.wait_ge(block_landed[b][c], landed)
                        for s in range(lo, hi):
                            mm = pe.matmul(p_e[b][:, 0:PARTS * D], blk[b][:, s * P:(s + 1) * P],
                                           parts[:, s, :, :].rearrange("p k f -> p (k f)"),
                                           start=s == 0, stop=s == TILES - 1)
                        mm.then_inc(block_used, 1)
                tiles(pe, tile, n)

            def edge_products(i, h):
                pe.wait_ge(edge_landed[h], i * 16 + 16)
                for g in range(U // EG):
                    wait(pe, edge_added, i * (2 * U // EG) + (h * U // EG + g - 1))
                    for c in (0, 1):
                        mm = pe.matmul(p_e[2 * (g % 2) + c][0:CH, 0:4 * D], EA[:, h, g, :],
                                       BD[:, 2 * c:2 * c + 2, :, :].rearrange("p a b f -> p (a b f)"),
                                       start=True, stop=True)
                    mm.then_inc(edge_product, 1)

            def sum_pass():
                pe.wait_ge(hT_ready, at["turn"])
                pe.wait_ge(product_used, at["mm"])

                def body(i):
                    for h in (0, 1):
                        pe.wait_ge(edge_landed[h], i * 16 + 16)
                        for k in range(BANKS):
                            wait(pe, gelu_done, i * (2 * BANKS) + (BANKS * (h - 1) + k + 1))
                            mm = pe.matmul(p_h[k][0:CH, 0:4 * D], EA[:, h, k // 2, :],
                                           BD[:, 2 * (k % 2):2 * (k % 2) + 2, :, :].rearrange("p a b f -> p (a b f)"),
                                           start=True, stop=False)
                        mm.then_inc(edge_product, 1)
                        pe.wait_ge(rows_landed[h], (i + 1) * (16 * U))
                        for k in range(BANKS):
                            pe.matmul(p_h[k][0:CH, 0:4 * D].rearrange("p (a f) -> p a f", a=2), C[0:CH, C_ID:C_ID + CH],
                                      G[0:CH, h, 2 * k:2 * k + 2, 0:2 * D], start=False, stop=True
                                      ).then_inc(hidden_ready, 1)
                turns(pe, body)
                pe.wait_ge(gelu_done, 2 * BANKS * ITER)
                close()

            def scatter_pass(n, fast):
                base = place(n, fast) * 2 * ITER

                def body(i):
                    for h in (0, 1):
                        if n == GATE:
                            edge_products(i, h)
                        pe.wait_ge(msg_ready, i * 2 + (1 + h + base))
                        wait(pe, comb_ready, i * 2 + (h + base))
                        for j in range(U):
                            mm = pe.matmul(p_c[j // 4][0:CH, (j % 4) * P:(j % 4) * P + width(n)], same[h][:, j, :],
                                           M[:, j, 0:width(n)], start=True, stop=True)
                        mm.then_inc(combined, 1)
                turns(pe, body)

            def way(fast):
                at.update(turn=0, mm=0, stage=0)

                def convolution(n):
                    if fast:
                        adjacency(n)
                    else:
                        scatter_pass(n, fast)
                degrees()
                dense(H, ["W_in_T"])
                for n in range(3):
                    dense(H, [f"gcn_T{n}"])
                    convolution(n)
                dense(H, ["W_out_T"])
                dense(H, ["L1_gnn_W1"])
                convolution(3)
                dense(H, ["L1_gnn_W2"])
                convolution(4)
                dense(H, ["mW1_x", "gW1_x"])
                if fast:
                    sum_pass()
                else:
                    scatter_pass(GATE, fast)
                dense(AGG, ["L2_gnn_mW2"])
                dense(H, ["uW1_x"])
                dense(V, ["uW1_a"])
                dense(T, ["L2_gnn_uW2"])
                dense(H, ["L3_gnn_qW", "L3_gnn_kW", "L3_gnn_vW"])
                scatter_pass(ATTEND, fast)
            both_ways(pe, way)

        @block.scalar
        def _(act):
            act.wait_ge(cleared, 2)
            for d in range(TILES):
                act.dma_start(adj_v[d, :, 0:TILES * P], zeros_bf).then_inc(adj_cleared, 16)
            act.wait_ge(inputs_landed, 16 * n_inputs)
            at = {}

            def root():
                at["root"] += 1
                act.wait_ge(root_wanted, at["root"])
                act.activation(st[:, 1, :], st[:, 0, :], ACT.Sqrt).then_inc(root_ready, 1)

            def dense(n_w=1):
                for g in range(GROUPS):
                    k = at["turn"]
                    act.wait_ge(turned, k + 1)
                    if g >= 2:
                        act.wait_ge(product, at["mm"] + (g - 1) * n_w)
                    cols = min(GRP, TILES - GRP * g) * P
                    act.activation(hT[:, k % 2, 0:cols], p_tr[k % 2][0:D, 0:cols], ACT.Copy).then_inc(hT_ready, 1)
                    at["turn"] += 1
                at["mm"] += n_w * GROUPS

            def gate(i, h):
                act.wait_ge(logit_ready, i * 2 + (1 + h))
                act.activation(small[:, 1, 0:U], small[:, 0, 0:U], ACT.Sigmoid, bias=sc[0:CH, 1:2]
                               ).then_inc(gate_ready, 1)

            def sum_pass():
                def body(i):
                    for h in (0, 1):
                        wait(act, sums_ready[h], i)
                        for k in range(BANKS):
                            act.wait_ge(hidden_ready, i * (2 * BANKS) + (BANKS * h + k + 1))
                            act.activation(A[0:CH, h, 2 * k:2 * k + 2, :],
                                           p_h[k][0:CH, 0:4 * D].rearrange("p (a f) -> p a f", a=2), ACT.Gelu
                                           ).then_inc(gelu_done, 1)
                        gate(i, h)
                turns(act, body)

            def scatter_pass(n, fast):
                base = place(n, fast) * 2 * ITER

                def body(i):
                    for h in (0, 1):
                        if n == GATE:
                            act.wait_ge(edge_added, i * (2 * U // EG) + (h + 1) * (U // EG))
                            act.activation(gmg[h], gmg[h], ACT.Gelu).then_inc(gelu_done, 1)
                            gate(i, h)
                        if n == ATTEND:
                            act.wait_ge(score_ready, i * 2 + (1 + h))
                            act.activation(M[:, :, D:AW], small[:, 1, :].rearrange("p (u e) -> p u e", u=U),
                                           ACT.Exp).then_inc(exp_ready, 1)
                        act.wait_ge(combined, i * 2 + (1 + h + base))
                        wait_scattered(act, n, i, h)
                        for k in range(U // 4):
                            cp = act.activation(R[:, h, 4 * k:4 * k + 4, 0:width(n)],
                                                p_c[k][0:CH, :].rearrange("p (u f) -> p u f", u=4)[:, :, 0:width(n)],
                                                ACT.Copy)
                        cp.then_inc(comb_ready, 1)
                turns(act, body)

            def way(fast):
                at.update(turn=0, mm=0, root=0)
                def convolution(n):
                    if not fast:
                        scatter_pass(n, fast)
                root()
                root()
                dense()
                for n in range(3):
                    dense()
                    convolution(n)
                dense()
                root()
                dense()
                convolution(3)
                dense()
                convolution(4)
                root()
                dense(2)
                if fast:
                    sum_pass()
                    at["mm"] += GROUPS
                else:
                    scatter_pass(GATE, fast)
                dense()
                dense()
                dense()
                act.wait_ge(gelu_wanted, 1)
                act.activation(T[:, :, :], T[:, :, :], ACT.Gelu).then_inc(gelu_nodes, 1)
                dense()
                root()
                root()
                dense(3)
                scatter_pass(ATTEND, fast)
            both_ways(act, way)

        @block.vector
        def _(dve):
            at = {}
            nodes = [P, TILES, D]
            agg = AGG[:, :, 0:D]

            def per_node(ap):
                return ap.unsqueeze(2).to_broadcast(nodes)

            def per_feature(name):
                k = BIASES.index(name) if name in BIASES else len(BIASES) + int(name)
                return B[:, k, :].unsqueeze(1).to_broadcast(nodes)

            dve.memset(key_s, -1).then_inc(keys_cleared, 1)
            dve.memset(key_d[:, 0:LAGS], -1).then_inc(keys_cleared, 1)
            dve.memset(key_d[:, LAGS:LAGS + STEPS], 0).then_inc(keys_cleared, 1)
            dve.memset(key_d[:, LAGS + STEPS:wide], 1 << 30).then_inc(keys_cleared, 1)
            dve.memset(BD[:, :, :, :], 0.0).then_inc(bd_cleared, 1)
            dve.memset(X[:, FULL, :], 0.0).then_inc(bd_cleared, 1)

            dve.wait_ge(keys_landed, 16 * 6)
            dve.tensor_tensor(v_flat[0:CH, 0:wide - 1], key_d[:, 0:wide - 1], key_d[:, 1:wide], ALU.is_gt)
            dve.tensor_tensor(v_flat[0:CH, wide:2 * wide - LAGS - 1], key_d[:, 0:wide - LAGS - 1],
                              key_d[:, LAGS + 1:wide], ALU.is_equal)
            dve.tensor_tensor(cont[:, :], key_d[:, LAGS - 1:LAGS], key_d[:, LAGS:LAGS + 1], ALU.is_equal)
            dve.drain()
            dve.tensor_reduce(flags[:, 0:1], v_flat[0:CH, 0:wide - 1], AX_X, ALU.max)
            dve.tensor_reduce(flags[:, 1:2], v_flat[0:CH, wide:2 * wide - LAGS - 1], AX_X, ALU.max)
            dve.drain()
            dve.tensor_tensor(flags[:, 2:3], flags[:, 0:1], flags[:, 1:2], ALU.add).then_inc(flags_ready, 1)
            dve.wait_ge(flags_summed, 1)
            dve.tensor_copy(flag[:, :], p_mm[0][:, 0:1]).then_inc(flag_ready, 1)

            dve.wait_ge(inputs_landed, 16 * n_inputs)
            dve.memset(keep[:, 0:1], 0.0)
            dve.tensor_tensor(keep[:, 1:STEPS], dst_i[:, 1:STEPS], dst_i[:, 0:STEPS - 1], ALU.is_equal)
            dve.tensor_single_scalar(dst_hi.bitcast(I32), dst_i, 7, ALU.arith_shift_right)
            dve.tensor_single_scalar(dst_lo.bitcast(I32), dst_i, P - 1, ALU.bitwise_and)
            dve.tensor_tensor(open_c[:, :], nxt[:, :], dst_i[:, STEPS - 1:STEPS], ALU.is_equal)
            dve.tensor_copy(lastg[:, 0:1], dst_i[:, STEPS - 1:STEPS])
            dve.drain()
            dve.tensor_copy(dst_hi, dst_hi.bitcast(I32))
            dve.tensor_copy(dst_lo, dst_lo.bitcast(I32))
            dve.tensor_tensor(open_c[:, :], open_c[:, :], C[0:CH, C_ID + CH - 1:C_ID + CH], ALU.is_gt)
            dve.tensor_scalar(lastg[:, 1:GROUPS], C[0:CH, C_GRP + 1:C_GRP + GROUPS], lastg[:, 0:1], -1.0,
                              ALU.subtract, ALU.mult)
            dve.drain()

            def find_repeats():
                real_s, real_d = key_s[:, LAGS:LAGS + STEPS], key_d[:, LAGS:LAGS + STEPS]
                dve.tensor_scalar(entry, real_s, P - 1, SLO, ALU.bitwise_and, ALU.logical_shift_left)
                for v, mask, shift in ((real_s, None, SHI), (real_d, None, DHI), (real_d, P - 1, 0)):
                    for q in range(STEPS // LCOLS):
                        part = slice(q * LCOLS, (q + 1) * LCOLS)
                        if mask is None:
                            dve.tensor_scalar(x_a, v[:, part], 7, shift, ALU.logical_shift_right,
                                              ALU.logical_shift_left)
                        else:
                            dve.tensor_single_scalar(x_a, v[:, part], mask, ALU.bitwise_and)
                        dve.drain()
                        dve.tensor_tensor(entry[:, part], entry[:, part], x_a, ALU.bitwise_or)
                        dve.drain()
                dve.tensor_single_scalar(key_d, key_d, SLO, ALU.logical_shift_left)
                dve.drain()
                dve.tensor_tensor(key_s, key_s, key_d, ALU.bitwise_or)
                dve.drain()
                for q in range(STEPS // LCOLS):
                    o = LAGS + q * LCOLS
                    own = key_s[:, o:o + LCOLS]
                    dve.memset(cnt_b, 1.0)
                    dve.memset(cnt_a, 0.0)
                    dve.drain()
                    for lag in range(1, LAGS + 1):
                        dve.tensor_tensor(x_b, own, key_s[:, o - lag:o - lag + LCOLS], ALU.bitwise_xor)
                        dve.tensor_tensor(x_a, own, key_s[:, o + lag:o + lag + LCOLS], ALU.bitwise_xor)
                        dve.drain()
                        dve.scalar_tensor_tensor(out=cnt_b, in0=x_b, scalar=0.0, in1=cnt_b, op0=ALU.is_equal,
                                                 op1=ALU.add)
                        dve.scalar_tensor_tensor(out=cnt_a, in0=x_a, scalar=0.0, in1=cnt_a, op0=ALU.is_equal,
                                                 op1=ALU.add)
                        dve.drain()
                    part = slice(q * LCOLS, (q + 1) * LCOLS)
                    dve.tensor_copy(count_v[:, part], cnt_b)
                    dve.tensor_scalar(x_a, cnt_a, 0.0, None, ALU.is_gt)
                    dve.drain()
                    dve.tensor_single_scalar(x_a, x_a, NO_ENTRY, ALU.logical_shift_left)
                    dve.drain()
                    dve.tensor_tensor(entry[:, part], entry[:, part], x_a, ALU.bitwise_or).then_inc(entries_ready, 1)
                dve.drain()

            def rsqrt(plus):
                at["root"] += 1
                dve.tensor_scalar(st[:, 0, :], st[:, 0, :], plus, None, ALU.add).then_inc(root_wanted, 1)
                dve.wait_ge(root_ready, at["root"])
                dve.reciprocal(st[:, 2, :], st[:, 1, :])
                dve.drain()
                dve.tensor_tensor(st[:, 1, :], st[:, 2, :], st[:, 2, :], ALU.mult)
                dve.drain()
                dve.tensor_tensor(st[:, 1, :], st[:, 1, :], st[:, 0, :], ALU.mult)
                dve.drain()
                dve.tensor_scalar(st[:, 1, :], st[:, 1, :], -0.5, 1.5, ALU.mult, ALU.add)
                dve.drain()
                dve.tensor_tensor(st[:, 2, :], st[:, 2, :], st[:, 1, :], ALU.mult)
                dve.drain()

            def degrees():
                dve.wait_ge(zeros_landed, 16 * ACCS)
                dve.wait_ge(adj_cleared, 16 * TILES)

                def onehots(i):
                    for h in (0, 1):
                        if not first(i):
                            dve.wait_ge(onehot_used, i * 2 + (h - 1))
                        dve.tensor_tensor(lo_bits[h][:, :, :],
                                          dst_lo[:, at_batch(i, h)].unsqueeze(2).to_broadcast([CH, U, P]),
                                          C[0:CH, C_IOTA:C_IOTA + P].unsqueeze(1).to_broadcast([CH, U, P]),
                                          ALU.is_equal)
                        dve.tensor_tensor(hi_bits[h][:, :, 0:TILES],
                                          dst_hi[:, at_batch(i, h)].unsqueeze(2).to_broadcast([CH, U, TILES]),
                                          C[0:CH, C_IOTA:C_IOTA + TILES].unsqueeze(1).to_broadcast([CH, U, TILES]),
                                          ALU.is_equal).then_inc(onehot_ready, 1)
                turns(dve, onehots)
                dve.wait_ge(onehot_used, 2 * ITER)
                dve.tensor_copy(deg[:, :], p_e[0][:, 0:TILES]).then_inc(deg_ready, 1)
                dve.drain()
                dve.tensor_copy(st[:, 0, :], deg[:, :])
                dve.tensor_scalar(has_in[:, :], deg[:, :], 0.0, None, ALU.is_gt)
                dve.drain()
                rsqrt(1.0)
                dve.tensor_copy(dinv[:, :], st[:, 2, :])
                dve.wait_ge(cum_ready, 1)
                dve.tensor_copy(st[:, 4, :], p_mm[1][:, 0:TILES])
                dve.memset(st[:, 0, :], 1.0)
                dve.drain()
                dve.tensor_tensor_scan(st[:, 3, :], st[:, 0, :], st[:, 4, :], 0.0, ALU.mult, ALU.add)
                dve.drain()
                dve.tensor_tensor(st[:, 3, :], st[:, 3, :], st[:, 4, :], ALU.subtract)
                dve.drain()
                dve.tensor_tensor(st[:, 3, :], st[:, 3, :], p_mm[0][:, 0:TILES], ALU.add)
                dve.drain()
                dve.tensor_scalar(ends[:, :], st[:, 3, :], -1.0, 0.0, ALU.add, ALU.max)
                dve.tensor_scalar(st[:, 4, :], has_in[:, :], 1.0, -float(1 << 22), ALU.subtract, ALU.mult)
                dve.tensor_tensor(st[:, 3, :], st[:, 3, :], deg[:, :], ALU.subtract)
                dve.drain()
                dve.tensor_tensor(st[:, 3, :], st[:, 3, :], st[:, 4, :], ALU.add)
                dve.drain()
                for c in (0, 1):
                    dve.tensor_scalar(starts[:, c, :], st[:, 3, :], 2.0, float(c), ALU.mult, ALU.add)
                dve.drain()

            def norm(to, of, tmp, finish):
                dve.tensor_reduce(st[:, 3, :], of[:, :, :], AX_X, ALU.add)
                dve.drain()
                dve.tensor_scalar(st[:, 3, :], st[:, 3, :], 1.0 / D, None, ALU.mult)
                dve.drain()
                dve.tensor_tensor(to[:, :, :], of[:, :, :], per_node(st[:, 3, :]), ALU.subtract)
                dve.drain()
                dve.tensor_tensor(tmp[:, :, :], to[:, :, :], to[:, :, :], ALU.mult)
                dve.drain()
                dve.tensor_reduce(st[:, 0, :], tmp[:, :, :], AX_X, ALU.add)
                dve.drain()
                dve.tensor_scalar(st[:, 0, :], st[:, 0, :], 1.0 / D, None, ALU.mult)
                dve.drain()
                rsqrt(1e-5)
                dve.tensor_tensor(to[:, :, :], to[:, :, :], per_node(st[:, 2, :]), ALU.mult)
                dve.drain()
                finish()

            def relu_nodes(ap):
                dve.tensor_scalar(ap[:, :, :], ap[:, :, :], 0.0, None, ALU.max).then_inc(nodes_ready, 1)
                dve.drain()

            def dense(tos, ready=False):
                if ready:
                    dve.sem_inc(nodes_ready, 1)
                for g in range(GROUPS):
                    for to in tos:
                        dve.wait_ge(product, at["mm"] + 1)
                        n_t = min(GRP, TILES - GRP * g)
                        dve.tensor_copy(to[:, GRP * g:GRP * g + n_t, 0:D],
                                        p_mm[at["mm"] % 2][:, 0:n_t * D].rearrange("p (t f) -> p t f", t=n_t)
                                        ).then_inc(product_used, 1)
                        at["mm"] += 1
                dve.drain()

            def add_feature(ap, name):
                return dve.tensor_tensor(ap, ap, per_feature(name), ALU.add)

            def adjacency(n):
                if n == 0:
                    dve.wait_ge(fill_cleared, 16 * ITER)
                rest = T[:, :, :]
                for k in range(PARTS):
                    dve.tensor_copy(parts[:, :, k, :], rest)
                    dve.drain()
                    if k < PARTS - 1:
                        dve.tensor_tensor(agg, rest, parts[:, :, k, :], ALU.subtract)
                        dve.drain()
                        rest = agg
                dve.sem_inc(parts_ready, 1)

                def tile(d, b):
                    dve.wait_ge(block_used, d * 2 + (n * TILES * 2 + 2))
                    dve.tensor_reduce(AGG[:, bass.ds(d, 1), 0:D].rearrange("p o f -> p (o f)"),
                                      p_e[b][:, 0:PARTS * D].rearrange("p (k f) -> p f k", k=PARTS), AX_X,
                                      ALU.add).then_inc(adj_used, 1)
                tiles(dve, tile, n)
                dve.drain()

            def add_edges(i, h):
                for g in range(U // EG):
                    dve.wait_ge(edge_product, i * (2 * U // EG) + (h * U // EG + g + 1))
                    for c in (0, 1):
                        rows = G[0:CH, h, EG * g + 2 * c:EG * g + 2 * c + 2, 0:2 * D]
                        add = dve.tensor_tensor(
                            rows, rows, p_e[2 * (g % 2) + c][0:CH, 0:4 * D].rearrange("p (a f) -> p a f", a=2),
                            ALU.add)
                    add.then_inc(edge_added, 1)

            def gated(i, h, hid):
                dve.tensor_tensor(M[:, :, 0:D], hid[:, :, D:2 * D],
                                  gw2[0:CH, :].unsqueeze(1).to_broadcast([CH, U, D]), ALU.mult)
                dve.drain()
                dve.tensor_reduce(small[:, 0, 0:U], M[:, :, 0:D], AX_X, ALU.add).then_inc(logit_ready, 1)
                dve.wait_ge(gate_ready, i * 2 + (1 + h))
                dve.tensor_tensor(M[:, :, 0:D], hid[:, :, 0:D],
                                  small[:, 1, 0:U].unsqueeze(2).to_broadcast([CH, U, D]), ALU.mult)
                return dve.tensor_copy(M[:, :, D:MW], small[:, 1, 0:U].unsqueeze(2))

            def sum_pass():
                def body(i):
                    for h in (0, 1):
                        dve.tensor_copy(kp[:, h, :], keep[:, at_batch(i, h)])
                        dve.drain()
                        dve.wait_ge(gelu_done, i * (2 * BANKS) + (BANKS * (h + 1)))
                        gated(i, h, A[0:CH, h, :, :])
                        for j in range(U):
                            before = R[:, h, j - 1, 0:MW] if j else R[:, 1 - h, U - 1, 0:MW]
                            dve.drain()
                            if j == 0:
                                wait(dve, sums_stored[h], i * 16)
                            op = dve.scalar_tensor_tensor(out=R[:, h, j, 0:MW], in0=before, scalar=kp[:, h, j:j + 1],
                                                          in1=M[:, j, 0:MW], op0=ALU.mult, op1=ALU.add)
                        op.then_inc(sums_ready[h], 1)
                turns(dve, body)

                def open_nodes(g):
                    if g >= 2:
                        dve.wait_ge(product, at["mm"] - 1)
                    dve.tensor_scalar(OH[:, g % 2, :], C[0:CH, C_IOTA:C_IOTA + GRP * P], lastg[:, g:g + 1],
                                      open_c[:, 0:1], ALU.is_equal, ALU.mult).then_inc(open_ready, 1)
                dve.drain()
                open_nodes(0)
                dve.wait_ge(ends_landed, 16 * TILES)
                dve.tensor_tensor(AGG[:, :, 0:MW], AGG[:, :, 0:MW],
                                  has_in[:, :].unsqueeze(2).to_broadcast([P, TILES, MW]), ALU.mult)
                dve.drain()
                for g in range(GROUPS):
                    if g + 1 < GROUPS:
                        open_nodes(g + 1)
                    dve.wait_ge(product, at["mm"] + 1)
                    n_t = min(GRP, TILES - GRP * g)
                    to = AGG[:, GRP * g:GRP * g + n_t, 0:MW]
                    dve.tensor_tensor(to, to, p_mm[at["mm"] % 2][:, 0:n_t * MW].rearrange("p (t f) -> p t f", t=n_t),
                                      ALU.add).then_inc(product_used, 1)
                    at["mm"] += 1
                dve.drain()

            def leaders(n, fast, i, h):
                q = place(n, fast)
                key = si[h] if n == ATTEND else di[h]
                dve.wait_ge(lists_landed[h], (i + (q * ITER + 1)) * (16 if fast else 32))
                dve.wait_ge(krow_landed[h], i * 16 + (q * ITER * 16 + 16))
                if not first(i):
                    dve.wait_ge(comb_ready, i * 2 + (h - 1 + q * 2 * ITER))
                wait_scattered(dve, n, i, h)
                dve.tensor_tensor(same[h], krow[:, h, :, :], key[:, :].unsqueeze(2).to_broadcast([CH, U, CH]),
                                  ALU.is_equal)
                dve.drain()
                dve.tensor_tensor(stmp, same[h],
                                  C[0:CH, C_BEFORE:C_BEFORE + CH].unsqueeze(1).to_broadcast([CH, U, CH]), ALU.mult)
                dve.drain()
                dve.tensor_reduce(small[:, 2, 0:U], stmp, AX_X, ALU.max)
                dve.tensor_scalar(small[:, 3, 0:U], key[:, :], C[0:CH, C_TRASH:C_TRASH + 1], -1.0, ALU.subtract,
                                  ALU.mult)
                dve.drain()
                dve.tensor_tensor(small[:, 2, 0:U], small[:, 2, 0:U], small[:, 3, 0:U], ALU.mult)
                dve.drain()
                dve.tensor_tensor(ai[h][:, :], small[:, 2, 0:U], key[:, :], ALU.add).then_inc(targets_ready, 1)

            def attend(i, h, fast):
                if fast:
                    dve.wait_ge(fill_landed[h], i * 16 + 16)
                    dve.tensor_copy(kp[:, h, :], keep[:, at_batch(i, h)])
                    for j in range(U):
                        row = G[0:CH, h, j, D:3 * D]
                        dve.drain()
                        dve.scalar_tensor_tensor(out=row, in0=G[0:CH, h, j - 1, D:3 * D] if j else carry,
                                                 scalar=kp[:, h, j:j + 1], in1=row, op0=ALU.mult, op1=ALU.add)
                    dve.drain()
                    dve.tensor_copy(carry, G[0:CH, h, U - 1, D:3 * D])
                q, k, v = (G[0:CH, h, :, c * D:(c + 1) * D] for c in range(3))
                dve.tensor_tensor(M[:, :, 0:D], q, k, ALU.mult)
                dve.drain()
                dve.tensor_reduce(small[:, 0, :].rearrange("p (u e) -> p u e", u=U),
                                  M[:, :, 0:D].rearrange("p u (e f) -> p u e f", e=HEADS), AX_X, ALU.add)
                dve.drain()
                dve.tensor_scalar(small[:, 1, :], small[:, 0, :], 10.0, -10.0, ALU.min,
                                  ALU.max).then_inc(score_ready, 1)
                dve.wait_ge(exp_ready, i * 2 + (1 + h))
                return dve.tensor_tensor(M[:, :, 0:D].rearrange("p u (e f) -> p u e f", e=HEADS),
                                         v.rearrange("p u (e f) -> p u e f", e=HEADS),
                                         M[:, :, D:AW].unsqueeze(3).to_broadcast([CH, U, HEADS, DH]), ALU.mult)

            def scatter_pass(n, fast):
                q = place(n, fast)
                if fast:
                    dve.wait_ge(nodes_spread, 16 * 2 * TILES)
                    dve.wait_ge(heads_landed, 16)
                    dve.tensor_copy(keep[:, 0:1], cont[:, :])
                else:
                    dve.wait_ge(table_stored, 16 * (n + 1 if n < CONVS else CONVS + 2 if n == GATE else CONVS + 5))

                def body(i):
                    for h in (0, 1):
                        leaders(n, fast, i, h)
                        dve.wait_ge(gathered[n][h], (i + 1) * (16 * U * (2 if n == ATTEND and not fast else 1)))
                        wait(dve, combined, i * 2 + (h + q * 2 * ITER))
                        if n < CONVS:
                            op = dve.tensor_copy(M[:, :, 0:D], G[0:CH, h, :, 0:D])
                        elif n == GATE:
                            add_edges(i, h)
                            dve.wait_ge(gelu_done, i * 2 + (1 + h))
                            op = gated(i, h, gmg[h])
                        else:
                            op = attend(i, h, fast)
                        dve.drain()
                        dve.sem_inc(msg_ready, 1)
                        dve.sem_inc(gathered_used[h], 1)
                turns(dve, body)
                dve.wait_ge(acc_landed, 16 * ACCS * (q + 1))
                for part in (g_flat, a_flat):
                    dve.tensor_tensor(scratch, scratch, part[:, 0:TILES * AW], ALU.add)
                    dve.drain()
                if n < ATTEND:
                    dve.memset(g_flat, 0.0).then_inc(zeros_wanted, 1)

            def way(fast):
                at.update(mm=0, root=0, table=0)

                def convolution(n, bias_name):
                    dense([T])
                    scaled = dve.tensor_tensor(T[:, :, :], T[:, :, :], per_node(dinv[:, :]), ALU.mult)
                    if fast:
                        dve.drain()
                        adjacency(n)
                    else:
                        scaled.then_inc(table_ready, 1)
                        scatter_pass(n, fast)
                    dve.tensor_tensor(agg, agg, T[:, :, :], ALU.add)
                    dve.drain()
                    dve.tensor_tensor(agg, agg, per_node(dinv[:, :]), ALU.mult)
                    dve.drain()
                    add_feature(agg, bias_name)
                    dve.drain()

                def add_to_x(of):
                    dve.tensor_tensor(X[:, :, :], X[:, :, :], of, ALU.add)
                    dve.drain()

                if fast:
                    find_repeats()
                degrees()
                norm(H, X, V, lambda: relu_nodes(H))
                dense([T])
                add_feature(T[:, :, :], "L0_gnn_b_in")
                dve.drain()
                dve.tensor_scalar(H[:, :, :], T[:, :, :], 0.0, None, ALU.max).then_inc(nodes_ready, 1)
                if not fast:
                    dve.memset(R[:, :, :, :], 0.0)
                for n in range(3):
                    convolution(n, str(n))
                    dve.scalar_tensor_tensor(out=H[:, :, :], in0=agg, scalar=0.0, in1=H[:, :, :], op0=ALU.max,
                                             op1=ALU.add).then_inc(nodes_ready, 1)
                dense([T])
                add_feature(T[:, :, :], "L0_gnn_b_out")
                dve.drain()
                add_to_x(T[:, :, :])
                norm(H, X, T, lambda: relu_nodes(H))
                convolution(3, "L1_gnn_b1")
                dve.tensor_scalar(T[:, :, :], agg, 0.0, sc[:, 0:1], ALU.min, ALU.mult)
                dve.drain()
                dve.scalar_tensor_tensor(out=H[:, :, :], in0=agg, scalar=0.0, in1=T[:, :, :], op0=ALU.max,
                                         op1=ALU.add).then_inc(nodes_ready, 1)
                convolution(4, "L1_gnn_b2")
                add_to_x(agg)
                norm(H, X, T, lambda: relu_nodes(H))
                if fast:
                    dve.memset(R[:, :, :, :], 0.0)
                dense([T, V])
                add_feature(T[:, :, :], "L2_gnn_mb1")
                dve.drain()
                add_feature(V[:, :, :], "L2_gnn_gb1").then_inc(table_ready, 1)
                if fast:
                    sum_pass()
                else:
                    scatter_pass(GATE, fast)
                dense([V], ready=True)
                dve.tensor_tensor(T[:, :, :], per_node(AGG[:, :, D:MW].rearrange("p t f -> p (t f)")),
                                  per_feature("L2_gnn_mb2"), ALU.mult)
                dve.drain()
                dve.tensor_tensor(V[:, :, :], V[:, :, :], T[:, :, :], ALU.add)
                dve.drain()
                dense([T], ready=True)
                dense([AGG], ready=True)
                dve.tensor_tensor(T[:, :, :], T[:, :, :], agg, ALU.add)
                dve.drain()
                add_feature(T[:, :, :], "L2_gnn_ub1").then_inc(gelu_wanted, 1)
                dve.wait_ge(gelu_nodes, 1)
                dense([V], ready=True)
                dve.tensor_tensor(V[:, :, :], V[:, :, :], H[:, :, :], ALU.add)
                dve.drain()
                add_feature(V[:, :, :], "L2_gnn_ub2")
                dve.drain()

                def scale_shift():
                    dve.tensor_tensor(H[:, :, :], H[:, :, :], per_feature("L2_gnn_ln_g"), ALU.mult)
                    dve.drain()
                    add_feature(H[:, :, :], "L2_gnn_ln_b")
                    dve.drain()
                norm(H, V, T, scale_shift)
                add_to_x(H[:, :, :])
                norm(H, X, T, lambda: relu_nodes(H))
                dense([T, V, AGG])
                dve.sem_inc(table_ready, 1)
                scatter_pass(ATTEND, fast)
                weights_sum = AGG[:, :, D:AW]
                dve.tensor_scalar(weights_sum, weights_sum, 1e-8, None, ALU.add)
                dve.drain()
                dve.reciprocal(weights_sum, weights_sum)
                dve.drain()
                for e in range(HEADS):
                    part = AGG[:, :, e * DH:(e + 1) * DH]
                    dve.tensor_tensor(part, part, AGG[:, :, D + e:D + e + 1].to_broadcast([P, TILES, DH]), ALU.mult)
                dve.drain()
                add_to_x(H[:, :, :])
                dve.tensor_tensor(X[:, :, :], X[:, :, :], agg, ALU.add).then_inc(out_ready, 1)
            both_ways(dve, way)


def kernel(**inputs):
    import concourse.bacc as _bacc
    from concourse.bass_utils import run_bass_kernel_spmd as _run

    a = {k: np.asarray(v) for k, v in inputs.items()}
    w = {
        "W_in_T": a["L0_gnn_W_in"].T, "W_out_T": a["L0_gnn_W_out"].T,
        "mW1_x": a["L2_gnn_mW1"][:D], "gW1_x": a["L2_gnn_gW1"][:D],
        "uW1_x": a["L2_gnn_uW1"][:D], "uW1_a": a["L2_gnn_uW1"][D:],
        **{f"gcn_T{n}": a["L0_gnn_gcn_W"][n].T for n in range(3)},
    }
    arrays = {
        "x": a["x"], "src": a["src"], "dst": a["dst"],
        "src_rows": a["src"].reshape(CH, STEPS).T, "dst_rows": a["dst"].reshape(CH, STEPS).T,
        "edge_t": a["edge_attr_32"].reshape(CH, STEPS // EG, EG, ED).transpose(2, 3, 1, 0).reshape(P, STEPS // EG, CH),
        "consts": shape_constants(),
        "weights": np.stack([w[k] if k in w else a[k] for k in WEIGHTS]),
        "bias": np.stack([a[k] for k in BIASES]),
        "gcn_b": a["L0_gnn_gcn_b"],
        "scalars": np.concatenate([a["L1_gnn_a1"], a["L2_gnn_gb2"]]),
        "gate_w": a["L2_gnn_gW2"].reshape(D),
        "mg_edge": np.stack([a["L2_gnn_mW1"][D:], a["L2_gnn_gW1"][D:]], axis=1),
    }
    nc = _bacc.Bacc("TRN2", target_bir_lowering=False, num_devices=1)
    feed, args = {}, []
    for name, v in arrays.items():
        v = np.ascontiguousarray(v)
        feed[f"in_{name}"] = v
        args.append(nc.dram_tensor(f"in_{name}", v.shape, mybir.dt.from_np(v.dtype), kind="ExternalInput").ap())
    args.append(nc.dram_tensor("out_x", (N, D), F32, kind="ExternalOutput").ap())
    build(nc, *args)
    r = _run(nc, [feed], core_ids=[0])
    return r.results[0]["out_x"]
```

```python
from contextlib import ExitStack

import numpy as np

import concourse.bass as bass
from concourse import mybir

F32 = mybir.dt.float32
BF16 = mybir.dt.bfloat16
I32 = mybir.dt.int32
ALU = mybir.AluOpType
ACT = mybir.ActivationFunctionType
AX_X = mybir.AxisListType.X

N = 6250
EDGES = 200000
D = 96
ED = 32
HEADS = 4
DH = D // HEADS
P = 128
TILES = -(-N // P)
NPAD = TILES * P
FULL = N // P
REST = N - FULL * P
GRP = 4
GROUPS = -(-TILES // GRP)

CH = P
U = 16
ITER = -(-EDGES // (CH * 2 * U))
STEPS = ITER * 2 * U
E = CH * STEPS
PADS = E - EDGES
assert PADS % (NPAD - N) == 0

EG = 4
PIECES = 4
BANKS = 8
assert U == 2 * BANKS
MW = D + 1
AW = D + HEADS
ACCS = 3
TRASH = P
AROWS = 50 * P
assert AROWS >= NPAD + TRASH
LAGS = 64
LCOLS = 224
SHI, SLO, DHI = 7, 13, 20
NO_ENTRY = 28
PARTS = 3
HALF = (TILES + 1) // 2
GW = 3 * D

BIASES = ["L0_gnn_b_in", "L0_gnn_b_out", "L1_gnn_b1", "L1_gnn_b2", "L2_gnn_mb1", "L2_gnn_gb1", "L2_gnn_mb2",
          "L2_gnn_ub1", "L2_gnn_ub2", "L2_gnn_ln_g", "L2_gnn_ln_b"]
WEIGHTS = ["W_in_T", "gcn_T0", "gcn_T1", "gcn_T2", "W_out_T", "L1_gnn_W1", "L1_gnn_W2", "mW1_x", "gW1_x",
           "L2_gnn_mW2", "uW1_x", "uW1_a", "L2_gnn_uW2", "L3_gnn_qW", "L3_gnn_kW", "L3_gnn_vW"]

C_ID, C_TRI, C_IOTA = 0, P, 2 * P
C_BEFORE = C_IOTA + GRP * P
C_TRASH = C_BEFORE + P
C_GRP = C_TRASH + 1
C_W = C_GRP + GROUPS

CONVS = 5
GATE, ATTEND = CONVS, CONVS + 1
FILL_DMAS = 3
FILL_W = STEPS // ITER * 2 * D // FILL_DMAS
assert FILL_W * FILL_DMAS * ITER == STEPS * 2 * D


def shape_constants():
    c = np.zeros((P, C_W), np.float32)
    c[:, C_ID:C_ID + P] = np.eye(P)
    c[:, C_TRI:C_TRI + P] = np.triu(np.ones((P, P)))
    c[:, C_IOTA:C_IOTA + GRP * P] = np.arange(GRP * P)
    c[:, C_BEFORE:C_BEFORE + P] = np.tril(np.ones((P, P)), -1)
    c[:, C_TRASH] = NPAD + np.arange(P)
    c[:, C_GRP:C_GRP + GROUPS] = np.arange(GROUPS) * GRP * P
    return c


def build(nc, x, src, dst, src_rows, dst_rows, edge_t, consts, weights, bias, gcn_b, scalars, gate_w, mg_edge, out):
    def dram(name, shape, dt=F32):
        return nc.dram_tensor(name, shape, dt, kind="Internal").ap()

    table = dram("table", (NPAD, D))
    table_mg = dram("table_mg", (NPAD, 2 * D))
    table_q = dram("table_q", (NPAD, D))
    table_kv = dram("table_kv", (NPAD, 2 * D))
    run_m = dram("run_m", (E, MW))
    fill_kv = dram("fill_kv", (E, 2 * D))
    adj = dram("adj", (TILES << DHI, 1), BF16)
    adj_v = adj.rearrange("(d p s n) o -> d p (s n o)", d=TILES, p=P, n=P)
    acc_d = [dram(f"acc{a}", (AROWS, AW)) for a in range(ACCS)]

    def by_chunk(ap):
        return ap.rearrange("(p s) f -> p s f", p=CH)

    def by_tile(ap):
        return ap.rearrange("(t p) f -> p t f", p=P)

    with ExitStack() as ctx:
        def sb(name, shape, dt=F32):
            return ctx.enter_context(nc.sbuf_tensor(name, shape, dt))

        def ps(name, shape, dt=F32):
            return ctx.enter_context(nc.psum_tensor(name, shape, dt))

        def sem(name):
            return ctx.enter_context(nc.semaphore(name))

        X = sb("X", [P, TILES, D])
        H = sb("H", [P, TILES, D])
        T = sb("T", [P, TILES, D])
        VA = sb("VA", [P, TILES * (D + AW)])
        V = VA[:, 0:TILES * D].rearrange("p (t f) -> p t f", t=TILES)
        AGG = VA[:, TILES * D:].rearrange("p (t f) -> p t f", t=TILES)
        KV = VA[:, 0:TILES * 2 * D].rearrange("p (t f) -> p t f", t=TILES)
        G = sb("G", [P, 2, U, GW])
        A = sb("A", [P, 2, U, 2 * D])
        R = sb("R", [CH, 2, U, AW])
        M = sb("M", [CH, U, AW])
        EA = sb("EA", [P, 2, EG, CH])
        keep = sb("keep", [CH, STEPS])
        kp = sb("kp", [CH, 2, U])
        si = [sb(f"si{h}", [CH, U], I32) for h in (0, 1)]
        di = [sb(f"di{h}", [CH, U], I32) for h in (0, 1)]
        ai = [sb(f"ai{h}", [CH, U], I32) for h in (0, 1)]
        vi = [sb(f"vi{h}", [CH, U], BF16) for h in (0, 1)]
        cont = sb("cont", [CH, 1])
        heads = sb("heads", [CH, 1], I32)
        flags = sb("flags", [CH, 4])
        flag = sb("flag", [P, 1], I32)
        starts = sb("starts", [P, TILES], I32)
        small = sb("small", [CH, 4, U * HEADS])
        C = sb("C", [P, C_W])
        W = sb("W", [D, len(WEIGHTS), D])
        B = sb("B", [P, len(BIASES) + 3, D])
        gw2 = sb("gw2", [P, D])
        sc = sb("sc", [P, 2])
        BD = sb("BD", [P, EG, 2, D])
        hT = sb("hT", [D, 2, GRP * P])
        deg = sb("deg", [P, TILES])
        dinv = sb("dinv", [P, TILES])
        has_in = sb("has_in", [P, TILES])
        ends = sb("ends", [P, TILES], I32)
        st = sb("st", [P, 5, TILES])
        lastg = sb("lastg", [CH, GROUPS])
        open_c = sb("open_c", [CH, 1])
        nxt = sb("nxt", [CH, 1], I32)

        scratch = AGG[:, :, :].rearrange("p t f -> p (t f)")
        dst_i = scratch[0:CH, 0:STEPS].bitcast(I32)
        dst_hi = scratch[0:CH, STEPS:2 * STEPS]
        dst_lo = scratch[0:CH, 2 * STEPS:3 * STEPS]
        OH = M[:, :, :].rearrange("p u f -> p (u f)")[:, 0:2 * GRP * P].rearrange("p (k n) -> p k n", k=2)
        g_flat = G[:, :, :, :].rearrange("p h u f -> p (h u f)")
        a_flat = A[:, :, :, :].rearrange("p h u f -> p (h u f)")
        lo_bits = [a_flat[0:CH, h * U * P // 2:(h + 1) * U * P // 2].bitcast(BF16).rearrange("p (u f) -> p u f", u=U)
                   for h in (0, 1)]
        hi_bits = [g_flat[0:CH, h * 1024:h * 1024 + U * 64 // 2].bitcast(BF16).rearrange("p (u f) -> p u f", u=U)
                   for h in (0, 1)]
        h_flat = H[:, :, :].rearrange("p t f -> p (t f)")
        v_flat = V[:, :, :].rearrange("p t f -> p (t f)")
        wide = STEPS + 2 * LAGS
        key_s = h_flat[0:CH, 0:wide].bitcast(I32)
        key_d = h_flat[0:CH, wide:2 * wide].bitcast(I32)
        x_b = v_flat[0:CH, 0:LCOLS].bitcast(I32)
        x_a = v_flat[0:CH, LCOLS:2 * LCOLS].bitcast(I32)
        cnt_b = v_flat[0:CH, 2 * LCOLS:3 * LCOLS]
        cnt_a = v_flat[0:CH, 3 * LCOLS:4 * LCOLS]
        r_flat = R[:, :, :, :].rearrange("p h u f -> p (h u f)")
        entry = r_flat[:, 0:STEPS].bitcast(I32)
        count_v = r_flat[:, STEPS:STEPS + STEPS // 2].bitcast(BF16)
        zeros_bf = a_flat[:, 0:TILES * P // 2].bitcast(BF16)
        parts = g_flat[:, 0:TILES * PARTS * D // 2].bitcast(BF16).rearrange("p (t k f) -> p t k f", t=TILES, k=PARTS)
        blk = [b[:, 0:TILES * P // 2].bitcast(BF16) for b in (a_flat, v_flat)]
        same = [a_flat[0:CH, h * U * P:h * U * P + U * CH].rearrange("p (u j) -> p u j", u=U) for h in (0, 1)]
        krow = V[:, :, :].rearrange("p t f -> p (t f)")[0:CH, 0:2 * U * CH].bitcast(I32).rearrange(
            "p (h u j) -> p h u j", h=2, u=U)
        stmp = scratch[0:CH, 0:U * CH].rearrange("p (u j) -> p u j", u=U)
        carry = a_flat[0:CH, 2 * U * P:2 * U * P + 2 * D]
        fill_zeros = g_flat[0:CH, TILES * PARTS * D // 2:TILES * PARTS * D // 2 + FILL_W]
        gmg = [G[0:CH, h, :, 0:2 * D] for h in (0, 1)]

        p_tr = [ps(f"p_tr{k}", [P, 512]) for k in (0, 1)]
        p_mm = [ps(f"p_mm{k}", [P, 512]) for k in (0, 1)]
        p_c = [*p_tr, *p_mm]
        p_e = [ps(f"p_e{k}", [P, 512]) for k in range(4)]
        p_h = [*p_e, *p_tr, *p_mm]

        inputs_landed = sem("inputs_landed")
        keys_cleared = sem("keys_cleared")
        keys_landed = sem("keys_landed")
        flags_ready = sem("flags_ready")
        flags_summed = sem("flags_summed")
        flag_ready = sem("flag_ready")
        cleared = sem("cleared")
        adj_cleared = sem("adj_cleared")
        fill_cleared = sem("fill_cleared")
        zeros_wanted = sem("zeros_wanted")
        zeros_landed = sem("zeros_landed")
        bd_cleared = sem("bd_cleared")
        entries_ready = sem("entries_ready")
        entry_landed = [sem(f"entry_landed{h}") for h in (0, 1)]
        entry_stored = [sem(f"entry_stored{h}") for h in (0, 1)]
        block_landed = [[sem(f"block_landed{b}_{c}") for c in (0, 1)] for b in (0, 1)]
        block_used = sem("block_used")
        cast_ready = sem("cast_ready")
        parts_ready = sem("parts_ready")
        adj_used = sem("adj_used")
        onehot_ready = sem("onehot_ready")
        onehot_used = sem("onehot_used")
        deg_ready = sem("deg_ready")
        cum_ready = sem("cum_ready")
        root_wanted = sem("root_wanted")
        root_ready = sem("root_ready")
        nodes_ready = sem("nodes_ready")
        turned = sem("turned")
        hT_ready = sem("hT_ready")
        product = sem("product")
        product_used = sem("product_used")
        table_ready = sem("table_ready")
        table_stored = sem("table_stored")
        idx_landed = [sem(f"idx_landed{h}") for h in (0, 1)]
        rows_landed = [sem(f"rows_landed{h}") for h in (0, 1)]
        hidden_ready = sem("hidden_ready")
        sums_ready = [sem(f"sums_ready{h}") for h in (0, 1)]
        sums_stored = [sem(f"sums_stored{h}") for h in (0, 1)]
        ends_landed = [sem(f"ends_landed{g}") for g in range(GROUPS)]
        open_ready = sem("open_ready")
        edge_landed = [sem(f"edge_landed{h}") for h in (0, 1)]
        edge_product = sem("edge_product")
        edge_added = sem("edge_added")
        gelu_done = sem("gelu_done")
        logit_ready = sem("logit_ready")
        gate_ready = sem("gate_ready")
        gelu_wanted = sem("gelu_wanted")
        gelu_nodes = sem("gelu_nodes")
        lists_landed = [sem(f"lists_landed{h}") for h in (0, 1)]
        gathered = [[sem(f"gathered{n}_{h}") for h in (0, 1)] for n in range(ATTEND + 1)]
        gathered_used = [sem(f"gathered_used{h}") for h in (0, 1)]
        krow_landed = [sem(f"krow_landed{h}") for h in (0, 1)]
        fill_landed = [sem(f"fill_landed{h}") for h in (0, 1)]
        heads_landed = sem("heads_landed")
        nodes_spread = sem("nodes_spread")
        targets_ready = sem("targets_ready")
        score_ready = sem("score_ready")
        exp_ready = sem("exp_ready")
        msg_ready = sem("msg_ready")
        combined = sem("combined")
        comb_ready = sem("comb_ready")
        scattered = [[sem(f"scattered{n}_{a}") for a in range(ACCS)] for n in range(ATTEND + 1)]
        acc_landed = [sem(f"acc_landed{k}") for k in range(PIECES)]
        out_ready = sem("out_ready")
        out_stored = sem("out_stored")
        pool_passed = sem("pool_passed")
        sp_passed = sem("sp_passed")

        block = ctx.enter_context(nc.Block())

        def wait(eng, s, v):
            if not isinstance(v, int) or v > 0:
                eng.wait_ge(s, v)

        def first(i):
            return isinstance(i, int) and i == 0

        def turns(eng, body):
            body(0)
            with eng.Fori(1, ITER) as i:
                body(i)

        def tiles(eng, body, n):
            start = n * TILES % 2
            body(0, start)
            body(1, 1 - start)
            with eng.Fori(1, TILES // 2) as i:
                body(i * 2, start)
                body(i * 2 + 1, 1 - start)
            body(TILES - 1, start)

        def passed(eng, s):
            eng.sem_inc(s, 1)

        def both_ways(eng, way):
            eng.wait_ge(flag_ready, 1)
            with eng.If(eng.value_load(flag[0:1, 0:1]) == 0):
                way(True)
            with eng.Else():
                way(False)
            eng.drain()

        def bank_tiles(g, n_w):
            per = 4 // n_w if n_w < 3 else 1
            stop = min(GRP * g + GRP, TILES)
            return [range(t, min(t + per, stop)) for t in range(GRP * g, stop, per)]

        def products(groups, n_w):
            return sum(len(bank_tiles(g, n_w)) for g in range(groups))

        def acc_steps(a):
            return len(range(a, U, ACCS))

        def place(n, fast):
            return 0 if fast else n

        def width(n):
            return D if n < CONVS else MW if n == GATE else AW

        def wait_scattered(eng, n, i, h):
            if not first(i):
                for a in range(ACCS):
                    eng.wait_ge(scattered[n][a], i * (32 * acc_steps(a)) + 16 * acc_steps(a) * (h - 1))

        pieces = [slice(TILES * k // PIECES, TILES * (k + 1) // PIECES) for k in range(PIECES)]
        at_batch = lambda i, h: bass.ds(i * (2 * U) + U * h, U)
        src_c, dst_c = (v.rearrange("(p s) -> p s", p=CH) for v in (src, dst))
        n_inputs = 16

        @block.sync
        def _(sp):
            def load(to, of, slow=False):
                sp.dma_start(to, of, allow_slow_non_contiguous=slow).then_inc(inputs_landed, 16)

            sp.wait_ge(keys_cleared, 4)
            for rows, to in ((src_c, key_s), (dst_c, key_d)):
                sp.dma_start(to[:, LAGS:LAGS + STEPS], rows).then_inc(keys_landed, 16)
                sp.dma_start(to[1:CH, 0:LAGS], rows[0:CH - 1, STEPS - LAGS:STEPS]).then_inc(keys_landed, 16)
                sp.dma_start(to[0:CH - 1, LAGS + STEPS:wide], rows[1:CH, 0:LAGS]).then_inc(keys_landed, 16)
            load(C[:, :], consts)
            load(dst_i, dst_c)
            load(nxt[0:CH - 1, :], dst_c[1:CH, 0:1], slow=True)
            load(nxt[CH - 1:CH, :], dst_c[0:1, 0:1], slow=True)
            load(heads[:, :], dst_c[:, 0:1], slow=True)
            load(W[:, :, :], weights.rearrange("n i o -> i n o"))
            load(B[:, 0:len(BIASES), :], bias.unsqueeze(0).to_broadcast((P, len(BIASES), D)))
            load(B[:, len(BIASES):, :], gcn_b.unsqueeze(0).to_broadcast((P, 3, D)))
            load(gw2[:, :], gate_w.unsqueeze(0).to_broadcast((P, D)))
            load(sc[:, :], scalars.unsqueeze(0).to_broadcast((P, 2)))
            sp.wait_ge(bd_cleared, 2)
            for a in range(EG):
                load(BD[a * ED:(a + 1) * ED, a, :, :], mg_edge)
            load(X[:, 0:FULL, :], by_tile(x[0:FULL * P, :]))
            load(X[0:REST, FULL, :], x[FULL * P:N, :])

            def clear_sums():
                for a in range(ACCS):
                    sp.dma_start(acc_d[a].rearrange("(p t) f -> p (t f)", p=P),
                                 g_flat[:, 0:AROWS // P * AW]).then_inc(zeros_landed, 16)
            sp.wait_ge(cleared, 2)

            def put_tables(k, *tables):
                for g in range(GROUPS):
                    sp.wait_ge(table_ready, (k - 1) * GROUPS + g + 1)
                    group = slice(GRP * g, min(GRP * g + GRP, TILES))
                    for to, of in tables:
                        sp.dma_start(by_tile(to)[:, group, :], of[:, group, :]).then_inc(table_stored, 16)

            def load_src(h, i, s):
                sp.dma_start(si[h][:, :], src_c[:, at_batch(i, h)]).then_inc(s[h], 16)

            def load_edges(h, i, fast):
                if not first(i):
                    if fast:
                        sp.wait_ge(edge_product, i * 2 + (h - 1))
                    else:
                        sp.wait_ge(edge_added, i * 8 + (4 * h - 4))
                passed(sp, sp_passed)
                sp.dma_start(EA[:, h, :, :], edge_t[:, bass.ds(i * (2 * U // EG) + (U // EG) * h, U // EG), :]
                             ).then_inc(edge_landed[h], 16)

            def sum_pass():
                def body(i, last=False):
                    for h in (0, 1):
                        sp.wait_ge(rows_landed[h], (i + 1) * (16 * U))
                        passed(sp, sp_passed)
                        if not last:
                            load_src(h, i + 1, idx_landed)
                            load_edges(h, i + 1, True)
                        sp.wait_ge(sums_ready[h], i + 1)
                        passed(sp, sp_passed)
                        sp.dma_start(by_chunk(run_m)[:, at_batch(i, h), :], R[:, h, :, 0:MW]
                                     ).then_inc(sums_stored[h], 16)
                for h in (0, 1):
                    load_src(h, 0, idx_landed)
                    load_edges(h, 0, True)
                with sp.Fori(0, ITER - 1) as i:
                    body(i)
                body(ITER - 1, last=True)

            def store_adjacency():
                fill_columns = by_chunk(fill_kv).rearrange("p s f -> p (s f)")

                def put_entries(i):
                    for h in (0, 1):
                        wait(sp, entry_stored[h], i * (16 * U))
                        passed(sp, sp_passed)
                        sp.dma_start(ai[h][:, :], entry[:, at_batch(i, h)]).then_inc(entry_landed[h], 16)
                        sp.dma_start(vi[h][:, :], count_v[:, at_batch(i, h)]).then_inc(entry_landed[h], 16)
                    for k in range(FILL_DMAS):
                        sp.dma_start(fill_columns[:, bass.ds(i * (FILL_DMAS * FILL_W) + k * FILL_W, FILL_W)], fill_zeros
                                     ).then_inc(fill_cleared, 16)
                per = LCOLS // (2 * U)
                for b in range(STEPS // LCOLS):
                    sp.wait_ge(entries_ready, b + 1)
                    if b == 0:
                        put_entries(0)
                    if b == 1:
                        clear_sums()
                    with sp.Fori(max(b * per, 1), (b + 1) * per) as i:
                        put_entries(i)
                for h in (0, 1):
                    sp.wait_ge(entry_stored[h], 16 * U * ITER)

            def load_blocks(n):
                def block_of(d, b):
                    for c, (lo, hi) in enumerate(((0, HALF), (HALF, TILES))):
                        if not isinstance(d, int) or n or d > 1:
                            sp.wait_ge(block_used, d * 2 + (n * TILES * 2 + c - 3))
                        passed(sp, sp_passed)
                        sp.dma_start(blk[b][:, lo * P:hi * P], adj_v[bass.ds(d, 1), :, lo * P:hi * P].rearrange(
                            "o p f -> (o p) f")).then_inc(block_landed[b][c], 16)
                if n == 0:
                    sp.wait_ge(adj_cleared, 16 * TILES)
                    sp.wait_ge(parts_ready, 1)
                tiles(sp, block_of, n)

            def scatter_pass(n, fast, stored):
                q = place(n, fast)
                key_rows = src_rows if n == ATTEND else dst_rows

                def lists(h, i):
                    load_src(h, i, lists_landed)
                    if not fast:
                        sp.dma_start(di[h][:, :], dst_c[:, at_batch(i, h)]).then_inc(lists_landed[h], 16)
                    sp.dma_start(krow[:, h, :, :], key_rows[at_batch(i, h), :].unsqueeze(0).to_broadcast((CH, U, CH))
                                 ).then_inc(krow_landed[h], 16)
                    if n == GATE:
                        load_edges(h, i, False)

                def fill(h, i):
                    wait(sp, gathered_used[h], i)
                    passed(sp, sp_passed)
                    sp.dma_start(G[0:CH, h, :, D:3 * D], by_chunk(fill_kv)[:, at_batch(i, h), :]
                                 ).then_inc(fill_landed[h], 16)

                sp.wait_ge(table_stored, 16 * GROUPS * stored)
                if fast:
                    sp.wait_ge(nodes_spread, 16 * TILES)
                if q:
                    sp.wait_ge(zeros_wanted, q)
                    clear_sums()
                lists(0, 0)
                lists(1, 0)
                if fast:
                    fill(0, 0)
                    fill(1, 0)

                def body(i):
                    for h in (0, 1):
                        sp.wait_ge(gathered[n][h], (i + 1) * (16 * U * (2 if n == ATTEND and not fast else 1)))
                        passed(sp, sp_passed)
                        sp.wait_ge(targets_ready, i * 2 + (1 + h + q * 2 * ITER))
                        passed(sp, sp_passed)
                        for a in range(ACCS):
                            wait(sp, scattered[n][a], i * (32 * acc_steps(a)) + 16 * acc_steps(a) * h)
                            passed(sp, sp_passed)
                        lists(h, i + 1)
                        if fast:
                            fill(h, i + 1)
                body(0)
                with sp.Fori(1, ITER - 1) as i:
                    body(i)
                for a in range(ACCS):
                    sp.wait_ge(scattered[n][a], 16 * acc_steps(a) * 2 * ITER)
                sp.wait_ge(comb_ready, 2 * ITER * (q + 1))
                for k, piece in enumerate(pieces):
                    for a, to in enumerate((scratch, g_flat, a_flat)):
                        sp.dma_start(to[:, 0:TILES * AW].rearrange("p (t f) -> p t f", t=TILES)[:, piece, :],
                                     by_tile(acc_d[a][0:NPAD, :])[:, piece, :]).then_inc(acc_landed[k], 16)

            def way(fast):
                if fast:
                    store_adjacency()
                else:
                    clear_sums()
                for n in range(CONVS):
                    if fast:
                        load_blocks(n)
                    else:
                        put_tables(n + 1, (table, T))
                        scatter_pass(n, fast, n + 1)
                k, stored = (1, 0) if fast else (CONVS + 1, CONVS)
                put_tables(k, (table_mg[:, 0:D], T), (table_mg[:, D:2 * D], V))
                if fast:
                    sum_pass()
                else:
                    scatter_pass(GATE, fast, stored + 2)
                put_tables(k + 1, (table_q, T), (table_kv, KV))
                scatter_pass(ATTEND, fast, stored + 4)
                for k, piece in enumerate(pieces):
                    sp.wait_ge(out_ready, k + 1)
                    full = slice(piece.start, min(piece.stop, FULL))
                    sp.dma_start(by_tile(out[0:FULL * P, :])[:, full, :], X[:, full, :]).then_inc(out_stored, 16)
                sp.dma_start(out[FULL * P:N, :], X[0:REST, FULL, :]).then_inc(out_stored, 16)
                sp.wait_ge(out_stored, 16 * (PIECES + 1))
            both_ways(sp, way)

        @block.gpsimd
        def _(pool):
            pool.memset(g_flat, 0.0).then_inc(cleared, 1)
            pool.memset(a_flat[:, 0:TILES * P // 2], 0.0).then_inc(cleared, 1)

            def gather(to, of, at, s):
                pool.indirect_dma_start(out=to, out_offset=None, in_=of,
                                        in_offset=bass.IndirectOffsetOnAxis(ap=at, axis=0)).then_inc(s, 16)

            def scatter_some(to, of, at, last, s):
                pool.indirect_dma_start(out=to, out_offset=bass.IndirectOffsetOnAxis(ap=at, axis=0), in_=of,
                                        in_offset=None, bounds_check=last, oob_is_err=False).then_inc(s, 16)

            def sum_pass():
                def body(i):
                    for h in (0, 1):
                        if not first(i):
                            pool.wait_ge(hidden_ready, i * (2 * BANKS) + (BANKS * (h - 1)))
                        pool.wait_ge(idx_landed[h], i * 16 + 16)
                        passed(pool, pool_passed)
                        for j in range(U):
                            gather(G[0:CH, h, j, 0:2 * D], table_mg, si[h][:, j:j + 1], rows_landed[h])
                pool.wait_ge(table_stored, 16 * GROUPS * 2)
                turns(pool, body)
                for h in (0, 1):
                    pool.wait_ge(sums_stored[h], 16 * ITER)
                for t in range(TILES):
                    gather(AGG[:, t, 0:MW], run_m, ends[:, t:t + 1], ends_landed[t // GRP])

            def store_adjacency():
                pool.wait_ge(adj_cleared, 16 * TILES)
                with pool.Fori(0, ITER) as i:
                    for h in (0, 1):
                        pool.wait_ge(entry_landed[h], i * 32 + 32)
                        passed(pool, pool_passed)
                        for j in range(U):
                            scatter_some(adj, vi[h][:, j:j + 1], ai[h][:, j:j + 1], (TILES << DHI) - 1,
                                         entry_stored[h])

            def scatter_pass(n, fast, stored):
                q = place(n, fast)

                def gathers(h, i):
                    if not first(i):
                        pool.wait_ge(gathered_used[h], i + q * ITER)
                    pool.wait_ge(lists_landed[h], (i + (q * ITER + 1)) * (16 if fast else 32))
                    passed(pool, pool_passed)
                    of = table if n < CONVS else table_mg if n == GATE else table_q
                    for j in range(U):
                        gather(G[0:CH, h, j, 0:of.shape[1]], of, si[h][:, j:j + 1], gathered[n][h])
                        if n == ATTEND and not fast:
                            gather(G[0:CH, h, j, D:3 * D], table_kv, di[h][:, j:j + 1], gathered[n][h])

                def scatters(h, i):
                    pool.wait_ge(comb_ready, i * 2 + (1 + h + q * 2 * ITER))
                    passed(pool, pool_passed)
                    for j in range(U):
                        a = j % ACCS
                        before = i * (32 * acc_steps(a)) + 16 * (h * acc_steps(a) + j // ACCS)
                        if not isinstance(before, int) or before > 0:
                            pool.wait_ge(scattered[n][a], before)
                            passed(pool, pool_passed)
                        pool.indirect_dma_start(out=acc_d[a],
                                                out_offset=bass.IndirectOffsetOnAxis(ap=ai[h][:, j:j + 1], axis=0),
                                                in_=R[:, h, j, :], in_offset=None,
                                                compute_op=ALU.add).then_inc(scattered[n][a], 16)

                if fast:
                    pool.wait_ge(fill_cleared, 16 * FILL_DMAS * ITER)
                    for g in range(GROUPS):
                        pool.wait_ge(table_ready, GROUPS + g + 1)
                        for t in range(GRP * g, min(GRP * g + GRP, TILES)):
                            scatter_some(fill_kv, KV[:, t, :], starts[:, t:t + 1], E - 1, nodes_spread)
                pool.wait_ge(table_stored, 16 * GROUPS * stored)
                pool.wait_ge(zeros_landed, 16 * ACCS * (q + 1))
                if fast:
                    gather(carry, table_kv, heads[:, 0:1], heads_landed)
                gathers(0, 0)
                gathers(1, 0)
                scatters(0, 0)
                with pool.Fori(1, ITER) as i:
                    gathers(0, i)
                    scatters(1, i + (-1))
                    gathers(1, i)
                    scatters(0, i)
                scatters(1, ITER - 1)

            def way(fast):
                if fast:
                    store_adjacency()
                    sum_pass()
                    scatter_pass(ATTEND, fast, 4)
                else:
                    for n in range(CONVS):
                        scatter_pass(n, fast, n + 1)
                    scatter_pass(GATE, fast, CONVS + 2)
                    scatter_pass(ATTEND, fast, CONVS + 4)
            both_ways(pool, way)

        @block.tensor
        def _(pe):
            pe.wait_ge(inputs_landed, 16 * n_inputs)
            ident = C[:, C_ID:C_ID + P]
            pe.wait_ge(flags_ready, 1)
            pe.matmul(p_mm[0][:, 0:1], C[0:CH, C_TRI + P - 1:C_TRI + P].to_broadcast((CH, P)), flags[:, 2:3],
                      start=True, stop=True).then_inc(flags_summed, 1)
            at = {}

            def degrees():
                counts = p_e[0][:, 0:TILES]

                def count(i, h, first=False, last=False):
                    pe.wait_ge(onehot_ready, i * 2 + (1 + h))
                    for j in range(U):
                        mm = pe.matmul(counts, lo_bits[h][:, j, :], hi_bits[h][:, j, 0:TILES],
                                       start=first and j == 0, stop=last and j == U - 1)
                    mm.then_inc(onehot_used, 1)
                count(0, 0, first=True)
                count(0, 1)
                with pe.Fori(1, ITER - 1) as i:
                    count(i, 0)
                    count(i, 1)
                count(ITER - 1, 0)
                count(ITER - 1, 1, last=True)
                pe.wait_ge(deg_ready, 1)
                pe.matmul(p_mm[0][:, 0:TILES], C[:, C_TRI:C_TRI + P], deg[:, :], start=True, stop=True)
                pe.matmul(p_mm[1][:, 0:TILES], C[:, C_TRI + P - 1:C_TRI + P].to_broadcast((P, P)), deg[:, :],
                          start=True, stop=True).then_inc(cum_ready, 1)

            def dense(h_in, ws):
                w_0, cols = WEIGHTS.index(ws[0]), len(ws) * D
                w_all = W[:, w_0:w_0 + len(ws), :].rearrange("p n f -> p (n f)")
                at["stage"] += 1
                pe.wait_ge(nodes_ready, at["stage"])

                def turn(g):
                    k = at["turn"] + g
                    wait(pe, hT_ready, k - 1)
                    for t in range(GRP * g, min(GRP * g + GRP, TILES)):
                        o = (t - GRP * g) * P
                        mm = pe.transpose(p_tr[k % 2][0:D, o:o + P], h_in[:, t, 0:D], ident)
                    mm.then_inc(turned, 1)
                turn(0)
                for g in range(GROUPS):
                    if g + 1 < GROUPS:
                        turn(g + 1)
                    k = at["turn"] + g
                    pe.wait_ge(hT_ready, k + 1)
                    for tiles_in in bank_tiles(g, len(ws)):
                        wait(pe, product_used, at["mm"] - 1)
                        for j, t in enumerate(tiles_in):
                            o = t - GRP * g
                            mm = pe.matmul(p_mm[at["mm"] % 2][:, j * cols:(j + 1) * cols],
                                           hT[:, k % 2, o * P:(o + 1) * P], w_all, start=True, stop=True)
                        mm.then_inc(product, 1)
                        at["mm"] += 1
                at["turn"] += GROUPS

            def close():
                for g in range(GROUPS):
                    pe.wait_ge(open_ready, g + 1)
                    wait(pe, product_used, at["mm"] - 1)
                    for t in range(GRP * g, min(GRP * g + GRP, TILES)):
                        o = t - GRP * g
                        mm = pe.matmul(p_mm[at["mm"] % 2][:, o * MW:(o + 1) * MW], OH[:, g % 2, o * P:(o + 1) * P],
                                       R[:, 1, U - 1, 0:MW], start=True, stop=True)
                    mm.then_inc(product, 1)
                    at["mm"] += 1

            def adjacency(n):
                pe.wait_ge(parts_ready, n + 1)

                def tile(d, b):
                    if not isinstance(d, int) or n or d > 1:
                        pe.wait_ge(adj_used, d + (n * TILES - 1))
                    before = (n * TILES + 1 - b) // 2
                    start = (b - n * TILES) % 2
                    landed = ((before + (d - start) // 2 + 1) * 16 if isinstance(d, int) else
                              (d - start) * 8 + (before + 1) * 16)
                    for c, (lo, hi) in enumerate(((0, HALF), (HALF, TILES))):
                        pe.wait_ge(block_landed[b][c], landed)
                        for s in range(lo, hi):
                            mm = pe.matmul(p_e[b][:, 0:PARTS * D], blk[b][:, s * P:(s + 1) * P],
                                           parts[:, s, :, :].rearrange("p k f -> p (k f)"),
                                           start=s == 0, stop=s == TILES - 1)
                        mm.then_inc(block_used, 1)
                tiles(pe, tile, n)

            def edge_products(i, h):
                pe.wait_ge(edge_landed[h], i * 16 + 16)
                for g in range(U // EG):
                    wait(pe, edge_added, i * (2 * U // EG) + (h * U // EG + g - 1))
                    for c in (0, 1):
                        mm = pe.matmul(p_e[2 * (g % 2) + c][0:CH, 0:4 * D], EA[:, h, g, :],
                                       BD[:, 2 * c:2 * c + 2, :, :].rearrange("p a b f -> p (a b f)"),
                                       start=True, stop=True)
                    mm.then_inc(edge_product, 1)

            def sum_pass():
                pe.wait_ge(hT_ready, at["turn"])
                pe.wait_ge(product_used, at["mm"])

                def body(i):
                    for h in (0, 1):
                        pe.wait_ge(edge_landed[h], i * 16 + 16)
                        for k in range(BANKS):
                            wait(pe, gelu_done, i * (2 * BANKS) + (BANKS * (h - 1) + k + 1))
                            mm = pe.matmul(p_h[k][0:CH, 0:4 * D], EA[:, h, k // 2, :],
                                           BD[:, 2 * (k % 2):2 * (k % 2) + 2, :, :].rearrange("p a b f -> p (a b f)"),
                                           start=True, stop=False)
                        mm.then_inc(edge_product, 1)
                        pe.wait_ge(rows_landed[h], (i + 1) * (16 * U))
                        for k in range(BANKS):
                            pe.matmul(p_h[k][0:CH, 0:4 * D].rearrange("p (a f) -> p a f", a=2), C[0:CH, C_ID:C_ID + CH],
                                      G[0:CH, h, 2 * k:2 * k + 2, 0:2 * D], start=False, stop=True
                                      ).then_inc(hidden_ready, 1)
                turns(pe, body)
                pe.wait_ge(gelu_done, 2 * BANKS * ITER)
                close()

            def scatter_pass(n, fast):
                base = place(n, fast) * 2 * ITER

                def body(i):
                    for h in (0, 1):
                        if n == GATE:
                            edge_products(i, h)
                        pe.wait_ge(msg_ready, i * 2 + (1 + h + base))
                        wait(pe, comb_ready, i * 2 + (h + base))
                        for j in range(U):
                            mm = pe.matmul(p_c[j // 4][0:CH, (j % 4) * P:(j % 4) * P + width(n)], same[h][:, j, :],
                                           M[:, j, 0:width(n)], start=True, stop=True)
                        mm.then_inc(combined, 1)
                turns(pe, body)

            def way(fast):
                at.update(turn=0, mm=0, stage=0)

                def convolution(n):
                    if fast:
                        adjacency(n)
                    else:
                        scatter_pass(n, fast)
                degrees()
                dense(H, ["W_in_T"])
                for n in range(3):
                    dense(H, [f"gcn_T{n}"])
                    convolution(n)
                dense(H, ["W_out_T"])
                dense(H, ["L1_gnn_W1"])
                convolution(3)
                dense(H, ["L1_gnn_W2"])
                convolution(4)
                dense(H, ["mW1_x", "gW1_x"])
                dense(H, ["uW1_x"])
                if fast:
                    sum_pass()
                else:
                    scatter_pass(GATE, fast)
                dense(AGG, ["L2_gnn_mW2"])
                dense(V, ["uW1_a"])
                dense(T, ["L2_gnn_uW2"])
                dense(H, ["L3_gnn_qW", "L3_gnn_kW", "L3_gnn_vW"])
                scatter_pass(ATTEND, fast)
            both_ways(pe, way)

        @block.scalar
        def _(act):
            act.wait_ge(cleared, 2)
            for d in range(TILES):
                act.dma_start(adj_v[d, :, 0:TILES * P], zeros_bf).then_inc(adj_cleared, 16)
            act.wait_ge(inputs_landed, 16 * n_inputs)
            at = {}

            def root():
                at["root"] += 1
                act.wait_ge(root_wanted, at["root"])
                act.activation(st[:, 1, :], st[:, 0, :], ACT.Sqrt).then_inc(root_ready, 1)

            def dense(n_w=1, cast=False):
                def first_part(g):
                    act.wait_ge(product_used, at["mm"] + g + 1)
                    group = slice(GRP * g, min(GRP * g + GRP, TILES))
                    act.activation(parts[:, group, 0, :], T[:, group, :], ACT.Copy).then_inc(cast_ready, 1)
                for g in range(GROUPS):
                    k = at["turn"]
                    act.wait_ge(turned, k + 1)
                    if g >= 2:
                        act.wait_ge(product, at["mm"] + products(g - 1, n_w))
                    cols = min(GRP, TILES - GRP * g) * P
                    act.activation(hT[:, k % 2, 0:cols], p_tr[k % 2][0:D, 0:cols], ACT.Copy).then_inc(hT_ready, 1)
                    at["turn"] += 1
                    if cast and g >= 2:
                        first_part(g - 2)
                if cast:
                    first_part(GROUPS - 2)
                    first_part(GROUPS - 1)
                at["mm"] += products(GROUPS, n_w)

            def gate(i, h):
                act.wait_ge(logit_ready, i * 2 + (1 + h))
                act.activation(small[:, 1, 0:U], small[:, 0, 0:U], ACT.Sigmoid, bias=sc[0:CH, 1:2]
                               ).then_inc(gate_ready, 1)

            def sum_pass():
                def body(i):
                    for h in (0, 1):
                        wait(act, sums_ready[h], i)
                        for k in range(BANKS):
                            act.wait_ge(hidden_ready, i * (2 * BANKS) + (BANKS * h + k + 1))
                            act.activation(A[0:CH, h, 2 * k:2 * k + 2, :],
                                           p_h[k][0:CH, 0:4 * D].rearrange("p (a f) -> p a f", a=2), ACT.Gelu
                                           ).then_inc(gelu_done, 1)
                        gate(i, h)
                turns(act, body)

            def scatter_pass(n, fast):
                base = place(n, fast) * 2 * ITER

                def body(i):
                    for h in (0, 1):
                        if n == GATE:
                            act.wait_ge(edge_added, i * (2 * U // EG) + (h + 1) * (U // EG))
                            act.activation(gmg[h], gmg[h], ACT.Gelu).then_inc(gelu_done, 1)
                            gate(i, h)
                        if n == ATTEND:
                            act.wait_ge(score_ready, i * 2 + (1 + h))
                            act.activation(M[:, :, D:AW], small[:, 1, :].rearrange("p (u e) -> p u e", u=U),
                                           ACT.Exp).then_inc(exp_ready, 1)
                        act.wait_ge(combined, i * 2 + (1 + h + base))
                        wait_scattered(act, n, i, h)
                        for k in range(U // 4):
                            cp = act.activation(R[:, h, 4 * k:4 * k + 4, 0:width(n)],
                                                p_c[k][0:CH, :].rearrange("p (u f) -> p u f", u=4)[:, :, 0:width(n)],
                                                ACT.Copy)
                        cp.then_inc(comb_ready, 1)
                turns(act, body)

            def way(fast):
                at.update(turn=0, mm=0, root=0)
                def convolution(n):
                    if not fast:
                        scatter_pass(n, fast)
                root()
                root()
                dense()
                for n in range(3):
                    dense(cast=fast)
                    convolution(n)
                dense()
                root()
                dense(cast=fast)
                convolution(3)
                dense(cast=fast)
                convolution(4)
                root()
                dense(2)
                dense()
                if fast:
                    sum_pass()
                    at["mm"] += GROUPS
                else:
                    scatter_pass(GATE, fast)
                dense()
                dense()
                act.wait_ge(gelu_wanted, 1)
                act.activation(T[:, :, :], T[:, :, :], ACT.Gelu).then_inc(gelu_nodes, 1)
                dense()
                root()
                root()
                dense(3)
                scatter_pass(ATTEND, fast)
            both_ways(act, way)

        @block.vector
        def _(dve):
            at = {}
            nodes = [P, TILES, D]
            agg = AGG[:, :, 0:D]

            def per_node(ap):
                return ap.unsqueeze(2).to_broadcast(nodes)

            def bias_index(name):
                return BIASES.index(name) if name in BIASES else len(BIASES) + int(name)

            def per_feature(name):
                return B[:, bias_index(name), :].unsqueeze(1).to_broadcast(nodes)

            dve.memset(key_s, -1).then_inc(keys_cleared, 1)
            dve.memset(key_d[:, 0:LAGS], -1).then_inc(keys_cleared, 1)
            dve.memset(key_d[:, LAGS:LAGS + STEPS], 0).then_inc(keys_cleared, 1)
            dve.memset(key_d[:, LAGS + STEPS:wide], 1 << 30).then_inc(keys_cleared, 1)
            dve.memset(BD[:, :, :, :], 0.0).then_inc(bd_cleared, 1)
            dve.memset(X[:, FULL, :], 0.0).then_inc(bd_cleared, 1)

            dve.wait_ge(keys_landed, 16 * 6)
            dve.tensor_tensor(v_flat[0:CH, 0:wide - 1], key_d[:, 0:wide - 1], key_d[:, 1:wide], ALU.is_gt)
            dve.tensor_tensor(v_flat[0:CH, wide:2 * wide - LAGS - 1], key_d[:, 0:wide - LAGS - 1],
                              key_d[:, LAGS + 1:wide], ALU.is_equal)
            dve.tensor_tensor(cont[:, :], key_d[:, LAGS - 1:LAGS], key_d[:, LAGS:LAGS + 1], ALU.is_equal)
            dve.drain()
            dve.tensor_reduce(flags[:, 0:1], v_flat[0:CH, 0:wide - 1], AX_X, ALU.max)
            dve.tensor_reduce(flags[:, 1:2], v_flat[0:CH, wide:2 * wide - LAGS - 1], AX_X, ALU.max)
            dve.drain()
            dve.tensor_tensor(flags[:, 2:3], flags[:, 0:1], flags[:, 1:2], ALU.add).then_inc(flags_ready, 1)
            dve.wait_ge(flags_summed, 1)
            dve.tensor_copy(flag[:, :], p_mm[0][:, 0:1]).then_inc(flag_ready, 1)

            dve.wait_ge(inputs_landed, 16 * n_inputs)
            dve.memset(keep[:, 0:1], 0.0)
            dve.tensor_tensor(keep[:, 1:STEPS], dst_i[:, 1:STEPS], dst_i[:, 0:STEPS - 1], ALU.is_equal)
            dve.tensor_single_scalar(dst_hi.bitcast(I32), dst_i, 7, ALU.arith_shift_right)
            dve.tensor_single_scalar(dst_lo.bitcast(I32), dst_i, P - 1, ALU.bitwise_and)
            dve.tensor_tensor(open_c[:, :], nxt[:, :], dst_i[:, STEPS - 1:STEPS], ALU.is_equal)
            dve.tensor_copy(lastg[:, 0:1], dst_i[:, STEPS - 1:STEPS])
            dve.drain()
            dve.tensor_copy(dst_hi, dst_hi.bitcast(I32))
            dve.tensor_copy(dst_lo, dst_lo.bitcast(I32))
            dve.tensor_tensor(open_c[:, :], open_c[:, :], C[0:CH, C_ID + CH - 1:C_ID + CH], ALU.is_gt)
            dve.tensor_scalar(lastg[:, 1:GROUPS], C[0:CH, C_GRP + 1:C_GRP + GROUPS], lastg[:, 0:1], -1.0,
                              ALU.subtract, ALU.mult)
            dve.drain()

            def find_repeats():
                real_s, real_d = key_s[:, LAGS:LAGS + STEPS], key_d[:, LAGS:LAGS + STEPS]
                dve.tensor_scalar(entry, real_s, P - 1, SLO, ALU.bitwise_and, ALU.logical_shift_left)
                for v, mask, shift in ((real_s, None, SHI), (real_d, None, DHI), (real_d, P - 1, 0)):
                    for q in range(STEPS // LCOLS):
                        part = slice(q * LCOLS, (q + 1) * LCOLS)
                        if mask is None:
                            dve.tensor_scalar(x_a, v[:, part], 7, shift, ALU.logical_shift_right,
                                              ALU.logical_shift_left)
                        else:
                            dve.tensor_single_scalar(x_a, v[:, part], mask, ALU.bitwise_and)
                        dve.drain()
                        dve.tensor_tensor(entry[:, part], entry[:, part], x_a, ALU.bitwise_or)
                        dve.drain()
                dve.tensor_single_scalar(key_d, key_d, SLO, ALU.logical_shift_left)
                dve.drain()
                dve.tensor_tensor(key_s, key_s, key_d, ALU.bitwise_or)
                dve.drain()
                for q in range(STEPS // LCOLS):
                    o = LAGS + q * LCOLS
                    own = key_s[:, o:o + LCOLS]
                    dve.memset(cnt_b, 1.0)
                    dve.memset(cnt_a, 0.0)
                    dve.drain()
                    for lag in range(1, LAGS + 1):
                        dve.tensor_tensor(x_b, own, key_s[:, o - lag:o - lag + LCOLS], ALU.bitwise_xor)
                        dve.tensor_tensor(x_a, own, key_s[:, o + lag:o + lag + LCOLS], ALU.bitwise_xor)
                        dve.drain()
                        dve.scalar_tensor_tensor(out=cnt_b, in0=x_b, scalar=0.0, in1=cnt_b, op0=ALU.is_equal,
                                                 op1=ALU.add)
                        dve.scalar_tensor_tensor(out=cnt_a, in0=x_a, scalar=0.0, in1=cnt_a, op0=ALU.is_equal,
                                                 op1=ALU.add)
                        dve.drain()
                    part = slice(q * LCOLS, (q + 1) * LCOLS)
                    dve.tensor_copy(count_v[:, part], cnt_b)
                    dve.tensor_scalar(x_a, cnt_a, 0.0, None, ALU.is_gt)
                    dve.drain()
                    dve.tensor_single_scalar(x_a, x_a, NO_ENTRY, ALU.logical_shift_left)
                    dve.drain()
                    dve.tensor_tensor(entry[:, part], entry[:, part], x_a, ALU.bitwise_or).then_inc(entries_ready, 1)
                dve.drain()

            def rsqrt(plus):
                at["root"] += 1
                dve.tensor_scalar(st[:, 0, :], st[:, 0, :], plus, None, ALU.add).then_inc(root_wanted, 1)
                dve.wait_ge(root_ready, at["root"])
                dve.reciprocal(st[:, 2, :], st[:, 1, :])
                dve.drain()
                dve.tensor_tensor(st[:, 1, :], st[:, 2, :], st[:, 2, :], ALU.mult)
                dve.drain()
                dve.tensor_tensor(st[:, 1, :], st[:, 1, :], st[:, 0, :], ALU.mult)
                dve.drain()
                dve.tensor_scalar(st[:, 1, :], st[:, 1, :], -0.5, 1.5, ALU.mult, ALU.add)
                dve.drain()
                dve.tensor_tensor(st[:, 2, :], st[:, 2, :], st[:, 1, :], ALU.mult)
                dve.drain()

            def degrees():
                dve.wait_ge(zeros_landed, 16 * ACCS)
                dve.wait_ge(adj_cleared, 16 * TILES)

                def onehots(i):
                    for h in (0, 1):
                        if not first(i):
                            dve.wait_ge(onehot_used, i * 2 + (h - 1))
                        dve.tensor_tensor(lo_bits[h][:, :, :],
                                          dst_lo[:, at_batch(i, h)].unsqueeze(2).to_broadcast([CH, U, P]),
                                          C[0:CH, C_IOTA:C_IOTA + P].unsqueeze(1).to_broadcast([CH, U, P]),
                                          ALU.is_equal)
                        dve.tensor_tensor(hi_bits[h][:, :, 0:TILES],
                                          dst_hi[:, at_batch(i, h)].unsqueeze(2).to_broadcast([CH, U, TILES]),
                                          C[0:CH, C_IOTA:C_IOTA + TILES].unsqueeze(1).to_broadcast([CH, U, TILES]),
                                          ALU.is_equal).then_inc(onehot_ready, 1)
                turns(dve, onehots)
                dve.wait_ge(onehot_used, 2 * ITER)
                dve.tensor_copy(deg[:, :], p_e[0][:, 0:TILES]).then_inc(deg_ready, 1)
                dve.drain()
                dve.tensor_copy(st[:, 0, :], deg[:, :])
                dve.tensor_scalar(has_in[:, :], deg[:, :], 0.0, None, ALU.is_gt)
                dve.drain()
                rsqrt(1.0)
                dve.tensor_copy(dinv[:, :], st[:, 2, :])
                dve.wait_ge(cum_ready, 1)
                dve.tensor_copy(st[:, 4, :], p_mm[1][:, 0:TILES])
                dve.memset(st[:, 0, :], 1.0)
                dve.drain()
                dve.tensor_tensor_scan(st[:, 3, :], st[:, 0, :], st[:, 4, :], 0.0, ALU.mult, ALU.add)
                dve.drain()
                dve.tensor_tensor(st[:, 3, :], st[:, 3, :], st[:, 4, :], ALU.subtract)
                dve.drain()
                dve.tensor_tensor(st[:, 3, :], st[:, 3, :], p_mm[0][:, 0:TILES], ALU.add)
                dve.drain()
                dve.tensor_scalar(ends[:, :], st[:, 3, :], -1.0, 0.0, ALU.add, ALU.max)
                dve.tensor_scalar(st[:, 4, :], has_in[:, :], 1.0, -float(1 << 22), ALU.subtract, ALU.mult)
                dve.tensor_tensor(st[:, 3, :], st[:, 3, :], deg[:, :], ALU.subtract)
                dve.drain()
                dve.tensor_tensor(starts[:, :], st[:, 3, :], st[:, 4, :], ALU.add)
                dve.drain()

            def moments(to, of, tmp, one):
                def pair(ap):
                    return ap.unsqueeze(2).to_broadcast([P, ap.shape[1], D])
                dve.tensor_reduce(st[:, 3, one], of[:, one, :], AX_X, ALU.add)
                dve.drain()
                dve.tensor_scalar(st[:, 3, one], st[:, 3, one], 1.0 / D, None, ALU.mult)
                dve.drain()
                dve.tensor_tensor(to[:, one, :], of[:, one, :], pair(st[:, 3, one]), ALU.subtract)
                dve.drain()
                dve.tensor_tensor(tmp[:, one, :], to[:, one, :], to[:, one, :], ALU.mult)
                dve.drain()
                dve.tensor_reduce(st[:, 0, one], tmp[:, one, :], AX_X, ALU.add)
                dve.drain()
                dve.tensor_scalar(st[:, 0, one], st[:, 0, one], 1.0 / D, None, ALU.mult)
                dve.drain()

            def norm(to, of, tmp, relu=False, centred=False):
                if not centred:
                    moments(to, of, tmp, slice(0, TILES))
                rsqrt(1e-5)
                if relu:
                    dve.scalar_tensor_tensor(out=to[:, :, :], in0=to[:, :, :], scalar=0.0, in1=per_node(st[:, 2, :]),
                                             op0=ALU.max, op1=ALU.mult).then_inc(nodes_ready, 1)
                else:
                    dve.tensor_tensor(to[:, :, :], to[:, :, :], per_node(st[:, 2, :]), ALU.mult)
                dve.drain()

            def split_group(g, n):
                group = slice(GRP * g, min(GRP * g + GRP, TILES))
                rest = AGG[:, group, 0:D]
                dve.wait_ge(cast_ready, n * GROUPS + g + 1)
                dve.tensor_tensor(rest, T[:, group, :], parts[:, group, 0, :], ALU.subtract)
                dve.drain()
                dve.tensor_copy(parts[:, group, 1, :], rest)
                dve.drain()
                dve.tensor_tensor(parts[:, group, 2, :], rest, parts[:, group, 1, :], ALU.subtract)

            def dense(tos, ready=False, biases=None, factor=None, base=None, table=False,
                      split=None):
                if ready:
                    dve.sem_inc(nodes_ready, 1)
                for g in range(GROUPS):
                    for tiles_in in bank_tiles(g, len(tos)):
                        dve.wait_ge(product, at["mm"] + 1)
                        n_t = len(tiles_in)
                        group = slice(tiles_in.start, tiles_in.stop)
                        held = p_mm[at["mm"] % 2][:, 0:n_t * len(tos) * D].rearrange(
                            "p (t k f) -> p t k f", t=n_t, k=len(tos))
                        for k, to in enumerate(tos):
                            rows = held[:, :, k, :]
                            to = to[:, group, 0:D]
                            if biases:
                                bias_row = B[:, bias_index(biases[k]), :].unsqueeze(1).to_broadcast([P, n_t, D])
                                op = dve.tensor_tensor(to, rows, bias_row, ALU.add)
                            elif factor is not None:
                                op = dve.tensor_tensor(to, rows, factor[:, group].unsqueeze(2).to_broadcast(
                                    [P, n_t, D]), ALU.mult)
                            elif base is not None:
                                op = dve.tensor_tensor(to, rows, base[:, group, :], ALU.add)
                            else:
                                op = dve.tensor_copy(to, rows)
                        op.then_inc(product_used, 1)
                        at["mm"] += 1
                    if table:
                        dve.drain()
                        dve.sem_inc(table_ready, 1)
                    if split is not None and g:
                        split_group(g - 1, split)
                if split is not None:
                    split_group(GROUPS - 1, split)
                dve.drain()

            def add_feature(ap, name):
                return dve.tensor_tensor(ap, ap, per_feature(name), ALU.add)

            def adjacency(n, bias_name, finish):
                dve.sem_inc(parts_ready, 1)

                def tile(d, b):
                    dve.wait_ge(block_used, d * 2 + (n * TILES * 2 + 2))
                    one = bass.ds(d, 1)
                    sums = AGG[:, one, 0:D]
                    dve.tensor_reduce(sums.rearrange("p o f -> p (o f)"),
                                      p_e[b][:, 0:PARTS * D].rearrange("p (k f) -> p f k", k=PARTS), AX_X,
                                      ALU.add).then_inc(adj_used, 1)
                    dve.drain()
                    dve.tensor_tensor(sums, sums, T[:, one, :], ALU.add)
                    dve.drain()
                    dve.tensor_tensor(sums, sums, dinv[:, one].unsqueeze(2).to_broadcast([P, 1, D]), ALU.mult)
                    dve.drain()
                    dve.tensor_tensor(sums, sums, B[:, bias_index(bias_name), :].unsqueeze(1), ALU.add)
                    dve.drain()
                    finish(one, T)
                    dve.drain()
                tiles(dve, tile, n)

            def add_edges(i, h):
                for g in range(U // EG):
                    dve.wait_ge(edge_product, i * (2 * U // EG) + (h * U // EG + g + 1))
                    for c in (0, 1):
                        rows = G[0:CH, h, EG * g + 2 * c:EG * g + 2 * c + 2, 0:2 * D]
                        add = dve.tensor_tensor(
                            rows, rows, p_e[2 * (g % 2) + c][0:CH, 0:4 * D].rearrange("p (a f) -> p a f", a=2),
                            ALU.add)
                    add.then_inc(edge_added, 1)

            def gated(i, h, hid):
                dve.tensor_tensor(M[:, :, 0:D], hid[:, :, D:2 * D],
                                  gw2[0:CH, :].unsqueeze(1).to_broadcast([CH, U, D]), ALU.mult)
                dve.drain()
                dve.tensor_reduce(small[:, 0, 0:U], M[:, :, 0:D], AX_X, ALU.add).then_inc(logit_ready, 1)
                dve.wait_ge(gate_ready, i * 2 + (1 + h))
                dve.tensor_tensor(M[:, :, 0:D], hid[:, :, 0:D],
                                  small[:, 1, 0:U].unsqueeze(2).to_broadcast([CH, U, D]), ALU.mult)
                return dve.tensor_copy(M[:, :, D:MW], small[:, 1, 0:U].unsqueeze(2))

            def sum_pass():
                def body(i):
                    for h in (0, 1):
                        dve.tensor_copy(kp[:, h, :], keep[:, at_batch(i, h)])
                        dve.drain()
                        dve.wait_ge(gelu_done, i * (2 * BANKS) + (BANKS * (h + 1)))
                        gated(i, h, A[0:CH, h, :, :])
                        for j in range(U):
                            before = R[:, h, j - 1, 0:MW] if j else R[:, 1 - h, U - 1, 0:MW]
                            dve.drain()
                            if j == 0:
                                wait(dve, sums_stored[h], i * 16)
                            op = dve.scalar_tensor_tensor(out=R[:, h, j, 0:MW], in0=before, scalar=kp[:, h, j:j + 1],
                                                          in1=M[:, j, 0:MW], op0=ALU.mult, op1=ALU.add)
                        op.then_inc(sums_ready[h], 1)
                turns(dve, body)

                def open_nodes(g):
                    if g >= 2:
                        dve.wait_ge(product, at["mm"] - 1)
                    dve.tensor_scalar(OH[:, g % 2, :], C[0:CH, C_IOTA:C_IOTA + GRP * P], lastg[:, g:g + 1],
                                      open_c[:, 0:1], ALU.is_equal, ALU.mult).then_inc(open_ready, 1)
                dve.drain()
                open_nodes(0)
                for g in range(GROUPS):
                    if g + 1 < GROUPS:
                        open_nodes(g + 1)
                    n_t = min(GRP, TILES - GRP * g)
                    to = AGG[:, GRP * g:GRP * g + n_t, 0:MW]
                    dve.wait_ge(ends_landed[g], 16 * n_t)
                    dve.tensor_tensor(to, to, has_in[:, GRP * g:GRP * g + n_t].unsqueeze(2).to_broadcast(
                        [P, n_t, MW]), ALU.mult)
                    dve.drain()
                    dve.wait_ge(product, at["mm"] + 1)
                    dve.tensor_tensor(to, to, p_mm[at["mm"] % 2][:, 0:n_t * MW].rearrange("p (t f) -> p t f", t=n_t),
                                      ALU.add).then_inc(product_used, 1)
                    at["mm"] += 1
                dve.drain()

            def leaders(n, fast, i, h):
                q = place(n, fast)
                key = si[h] if n == ATTEND else di[h]
                dve.wait_ge(lists_landed[h], (i + (q * ITER + 1)) * (16 if fast else 32))
                dve.wait_ge(krow_landed[h], i * 16 + (q * ITER * 16 + 16))
                if not first(i):
                    dve.wait_ge(comb_ready, i * 2 + (h - 1 + q * 2 * ITER))
                wait_scattered(dve, n, i, h)
                dve.tensor_tensor(same[h], krow[:, h, :, :], key[:, :].unsqueeze(2).to_broadcast([CH, U, CH]),
                                  ALU.is_equal)
                dve.drain()
                dve.tensor_tensor(stmp, same[h],
                                  C[0:CH, C_BEFORE:C_BEFORE + CH].unsqueeze(1).to_broadcast([CH, U, CH]), ALU.mult)
                dve.drain()
                dve.tensor_reduce(small[:, 2, 0:U], stmp, AX_X, ALU.max)
                dve.tensor_scalar(small[:, 3, 0:U], key[:, :], C[0:CH, C_TRASH:C_TRASH + 1], -1.0, ALU.subtract,
                                  ALU.mult)
                dve.drain()
                dve.tensor_tensor(small[:, 2, 0:U], small[:, 2, 0:U], small[:, 3, 0:U], ALU.mult)
                dve.drain()
                dve.tensor_tensor(ai[h][:, :], small[:, 2, 0:U], key[:, :], ALU.add).then_inc(targets_ready, 1)

            def attend(i, h, fast):
                if fast:
                    dve.wait_ge(fill_landed[h], i * 16 + 16)
                    dve.tensor_copy(kp[:, h, :], keep[:, at_batch(i, h)])
                    for j in range(U):
                        row = G[0:CH, h, j, D:3 * D]
                        dve.drain()
                        dve.scalar_tensor_tensor(out=row, in0=G[0:CH, h, j - 1, D:3 * D] if j else carry,
                                                 scalar=kp[:, h, j:j + 1], in1=row, op0=ALU.mult, op1=ALU.add)
                    dve.drain()
                    dve.tensor_copy(carry, G[0:CH, h, U - 1, D:3 * D])
                q, k, v = (G[0:CH, h, :, c * D:(c + 1) * D] for c in range(3))
                dve.tensor_tensor(M[:, :, 0:D], q, k, ALU.mult)
                dve.drain()
                dve.tensor_reduce(small[:, 0, :].rearrange("p (u e) -> p u e", u=U),
                                  M[:, :, 0:D].rearrange("p u (e f) -> p u e f", e=HEADS), AX_X, ALU.add)
                dve.drain()
                dve.tensor_scalar(small[:, 1, :], small[:, 0, :], 10.0, -10.0, ALU.min,
                                  ALU.max).then_inc(score_ready, 1)
                dve.wait_ge(exp_ready, i * 2 + (1 + h))
                return dve.tensor_tensor(M[:, :, 0:D].rearrange("p u (e f) -> p u e f", e=HEADS),
                                         v.rearrange("p u (e f) -> p u e f", e=HEADS),
                                         M[:, :, D:AW].unsqueeze(3).to_broadcast([CH, U, HEADS, DH]), ALU.mult)

            def finish_attention(piece):
                weights_sum = AGG[:, piece, D:AW]
                dve.tensor_scalar(weights_sum, weights_sum, 1e-8, None, ALU.add)
                dve.drain()
                dve.reciprocal(weights_sum, weights_sum)
                dve.drain()
                for e in range(HEADS):
                    part = AGG[:, piece, e * DH:(e + 1) * DH]
                    dve.tensor_tensor(part, part, AGG[:, piece, D + e:D + e + 1].to_broadcast(
                        [P, piece.stop - piece.start, DH]), ALU.mult)
                dve.drain()
                dve.tensor_tensor(X[:, piece, :], X[:, piece, :], AGG[:, piece, 0:D], ALU.add).then_inc(out_ready, 1)

            def scatter_pass(n, fast):
                q = place(n, fast)
                if fast:
                    dve.wait_ge(nodes_spread, 16 * TILES)
                    dve.wait_ge(heads_landed, 16)
                    dve.tensor_copy(keep[:, 0:1], cont[:, :])
                else:
                    dve.wait_ge(table_stored, 16 * GROUPS * (n + 1 if n < CONVS else CONVS + 2 if n == GATE else CONVS + 4))

                def body(i):
                    for h in (0, 1):
                        leaders(n, fast, i, h)
                        dve.wait_ge(gathered[n][h], (i + 1) * (16 * U * (2 if n == ATTEND and not fast else 1)))
                        wait(dve, combined, i * 2 + (h + q * 2 * ITER))
                        if n < CONVS:
                            op = dve.tensor_copy(M[:, :, 0:D], G[0:CH, h, :, 0:D])
                        elif n == GATE:
                            add_edges(i, h)
                            dve.wait_ge(gelu_done, i * 2 + (1 + h))
                            op = gated(i, h, gmg[h])
                        else:
                            op = attend(i, h, fast)
                        dve.drain()
                        dve.sem_inc(msg_ready, 1)
                        dve.sem_inc(gathered_used[h], 1)
                turns(dve, body)
                for k, piece in enumerate(pieces):
                    dve.wait_ge(acc_landed[k], 16 * ACCS * (q + 1))
                    cols = slice(piece.start * AW, piece.stop * AW)
                    for part in (g_flat, a_flat):
                        dve.tensor_tensor(scratch[:, cols], scratch[:, cols], part[:, cols], ALU.add)
                        dve.drain()
                    if n == ATTEND:
                        finish_attention(piece)
                if n < ATTEND:
                    dve.memset(g_flat, 0.0).then_inc(zeros_wanted, 1)

            def way(fast):
                at.update(mm=0, root=0, table=0)

                def convolution(n, bias_name, finish):
                    dense([T], factor=dinv, table=not fast, split=n if fast else None)
                    if fast:
                        adjacency(n, bias_name, finish)
                        return
                    scatter_pass(n, fast)
                    dve.tensor_tensor(agg, agg, T[:, :, :], ALU.add)
                    dve.drain()
                    dve.tensor_tensor(agg, agg, per_node(dinv[:, :]), ALU.mult)
                    dve.drain()
                    add_feature(agg, bias_name)
                    dve.drain()
                    finish(slice(0, TILES), T)

                def add_to_x(of):
                    dve.tensor_tensor(X[:, :, :], X[:, :, :], of, ALU.add)
                    dve.drain()

                if fast:
                    find_repeats()
                degrees()
                norm(H, X, V, relu=True)
                dense([T], biases=["L0_gnn_b_in"])
                dve.tensor_scalar(H[:, :, :], T[:, :, :], 0.0, None, ALU.max).then_inc(nodes_ready, 1)
                add_feature(X[:, :, :], "L0_gnn_b_out")
                if not fast:
                    dve.memset(R[:, :, :, :], 0.0)

                def relu_step(of, tmp):
                    dve.scalar_tensor_tensor(out=H[:, of, :], in0=AGG[:, of, 0:D], scalar=0.0, in1=H[:, of, :],
                                             op0=ALU.max, op1=ALU.add)
                for n in range(3):
                    convolution(n, str(n), relu_step)
                    dve.drain()
                    dve.sem_inc(nodes_ready, 1)
                dense([X], base=X)
                norm(H, X, T, relu=True)

                def prelu(of, tmp):
                    dve.tensor_scalar(tmp[:, of, :], AGG[:, of, 0:D], 0.0, sc[:, 0:1], ALU.min, ALU.mult)
                    dve.drain()
                    dve.scalar_tensor_tensor(out=H[:, of, :], in0=AGG[:, of, 0:D], scalar=0.0, in1=tmp[:, of, :],
                                             op0=ALU.max, op1=ALU.add)
                convolution(3, "L1_gnn_b1", prelu)
                dve.drain()
                dve.sem_inc(nodes_ready, 1)

                def to_x(of, tmp):
                    dve.tensor_tensor(X[:, of, :], X[:, of, :], AGG[:, of, 0:D], ALU.add)
                    dve.drain()
                    moments(H, X, tmp, of)
                convolution(4, "L1_gnn_b2", to_x)
                norm(H, X, T, relu=True, centred=True)
                if fast:
                    dve.memset(R[:, :, :, :], 0.0)
                dense([T, V], biases=["L2_gnn_mb1", "L2_gnn_gb1"], table=True)
                dve.wait_ge(table_stored, 16 * GROUPS * (2 if fast else CONVS + 2))
                dense([T], ready=True, biases=["L2_gnn_ub1"])
                add_feature(H[:, :, :], "L2_gnn_ub2")
                add_feature(X[:, :, :], "L2_gnn_ln_b")
                dve.drain()
                if fast:
                    sum_pass()
                else:
                    scatter_pass(GATE, fast)
                dve.sem_inc(nodes_ready, 1)
                gates_bias = a_flat[:, 0:TILES * D].rearrange("p (t f) -> p t f", t=TILES)
                dve.tensor_tensor(gates_bias, per_node(AGG[:, :, D:MW].rearrange("p t f -> p (t f)")),
                                  per_feature("L2_gnn_mb2"), ALU.mult)
                dve.drain()
                dense([V], base=gates_bias)
                dense([T], ready=True, base=T)
                dve.sem_inc(gelu_wanted, 1)
                dve.wait_ge(gelu_nodes, 1)
                dense([V], ready=True, base=H)
                norm(H, V, T)
                dve.tensor_tensor(H[:, :, :], H[:, :, :], per_feature("L2_gnn_ln_g"), ALU.mult)
                dve.drain()
                add_to_x(H[:, :, :])
                norm(H, X, T, relu=True)
                dense([T, KV[:, :, 0:D], KV[:, :, D:2 * D]], table=True)
                add_to_x(H[:, :, :])
                scatter_pass(ATTEND, fast)
            both_ways(dve, way)


def kernel(**inputs):
    import concourse.bacc as _bacc
    from concourse.bass_utils import run_bass_kernel_spmd as _run

    a = {k: np.asarray(v) for k, v in inputs.items()}
    w = {
        "W_in_T": a["L0_gnn_W_in"].T, "W_out_T": a["L0_gnn_W_out"].T,
        "mW1_x": a["L2_gnn_mW1"][:D], "gW1_x": a["L2_gnn_gW1"][:D],
        "uW1_x": a["L2_gnn_uW1"][:D], "uW1_a": a["L2_gnn_uW1"][D:],
        **{f"gcn_T{n}": a["L0_gnn_gcn_W"][n].T for n in range(3)},
    }
    pads = np.repeat(np.arange(N, NPAD, dtype=a["src"].dtype), PADS // (NPAD - N))
    src, dst = (np.concatenate([a[k], pads]) for k in ("src", "dst"))
    edge_attr = np.concatenate([a["edge_attr_32"], np.zeros((PADS, ED), a["edge_attr_32"].dtype)])
    arrays = {
        "x": a["x"], "src": src, "dst": dst,
        "src_rows": src.reshape(CH, STEPS).T, "dst_rows": dst.reshape(CH, STEPS).T,
        "edge_t": edge_attr.reshape(CH, STEPS // EG, EG, ED).transpose(2, 3, 1, 0).reshape(P, STEPS // EG, CH),
        "consts": shape_constants(),
        "weights": np.stack([w[k] if k in w else a[k] for k in WEIGHTS]),
        "bias": np.stack([a[k] for k in BIASES]),
        "gcn_b": a["L0_gnn_gcn_b"],
        "scalars": np.concatenate([a["L1_gnn_a1"], a["L2_gnn_gb2"]]),
        "gate_w": a["L2_gnn_gW2"].reshape(D),
        "mg_edge": np.stack([a["L2_gnn_mW1"][D:], a["L2_gnn_gW1"][D:]], axis=1),
    }
    nc = _bacc.Bacc("TRN2", target_bir_lowering=False, num_devices=1)
    feed, args = {}, []
    for name, v in arrays.items():
        v = np.ascontiguousarray(v)
        feed[f"in_{name}"] = v
        args.append(nc.dram_tensor(f"in_{name}", v.shape, mybir.dt.from_np(v.dtype), kind="ExternalInput").ap())
    args.append(nc.dram_tensor("out_x", (N, D), F32, kind="ExternalOutput").ap())
    build(nc, *args)
    r = _run(nc, [feed], core_ids=[0])
    return r.results[0]["out_x"]
```
